# Optimizing a Trainium2 kernel written in Bass

```python
import numpy as np
import jax
import jax.numpy as jnp

def _softmax(x, axis=-1):
    return jax.nn.softmax(x, axis=axis)

def _gelu(x):
    return jax.nn.gelu(x, approximate=True)

def _silu(x):
    return jax.nn.silu(x)

def _sigmoid(x):
    return jax.nn.sigmoid(x)

def _layernorm(x, axis=-1, eps=1e-05):
    m = jnp.mean(x, axis=axis, keepdims=True)
    v = jnp.var(x, axis=axis, keepdims=True)
    return (x - m) / jnp.sqrt(v + eps)

def _scatter_add(tgt, idx, src, axis=0):
    return tgt.at[idx].add(src)

def _segment_sum(src, seg, n):
    return jax.ops.segment_sum(src, seg, n)
kernel_name = 'mk_gnn_resnorm_d2_gnn_r16_1a518b'

def setup_inputs(seed: int=0):
    np.random.seed(seed)
    _w = jnp.asarray

    def _rec_inputs():
        import jax
        import jax.numpy as jnp
        _gk = jax.random.key(seed)
        x = -0.0003713 + 1 * jax.random.normal(jax.random.fold_in(_gk, 1), (6250, 128), jnp.float32)
        _s = jax.random.randint(jax.random.fold_in(_gk, 2), (50000,), 0, 6250, jnp.int32)
        _d = jax.random.randint(jax.random.fold_in(_gk, 3), (50000,), 0, 6250, jnp.int32)
        _loop = jnp.arange(6250, dtype=jnp.int32)
        src = jnp.concatenate([_s, _d, _loop])
        dst = jnp.concatenate([_d, _s, _loop])
        _o = jnp.argsort(dst, stable=True)
        src = src[_o]
        dst = dst[_o]
        edge_attr_32 = 0.000283511 + 1.00007 * jax.random.normal(jax.random.fold_in(_gk, 11), (106250, 32), jnp.float32)
        edge_type_2 = jax.random.randint(jax.random.fold_in(_gk, 13), (106250,), 0, 2, jnp.int32)
        edge_type_8 = jax.random.randint(jax.random.fold_in(_gk, 14), (106250,), 0, 8, jnp.int32)
        edge_weight = jax.random.uniform(jax.random.fold_in(_gk, 15), (106250,), jnp.float32, 0.0, 0.999998)
        return (x, src, dst, edge_attr_32, edge_type_2, edge_type_8, edge_weight)
    x, src, dst, edge_attr_32, edge_type_2, edge_type_8, edge_weight = _rec_inputs()

    def _L0_gnn_setup():
        import jax, jax.numpy as jnp
        import numpy as np
        N = 6250
        E = 37500
        D = 128
        H = 8
        DH = D // H
        T = 32
        NET = 2

        def _ln(x, g, b, eps=1e-05):
            mu = jnp.mean(x, axis=-1, keepdims=True)
            var = jnp.mean((x - mu) ** 2, axis=-1, keepdims=True)
            return (x - mu) * jax.lax.rsqrt(var + eps) * g + b

        def _expmap(e, c):
            abs_c = jnp.maximum(jnp.abs(c), 1e-15)
            sq = jnp.sqrt(abs_c)
            n = jnp.maximum(jnp.linalg.norm(e, axis=-1, keepdims=True), 1e-15)
            tanh_p = jnp.tanh(sq * n) * e / (sq * n)
            tan_p = jnp.tan(sq * n) * e / (sq * n)
            return jnp.where(c < 0, tanh_p, tan_p)

        def _proj(x, c, eps=1e-05):
            abs_c = jnp.maximum(jnp.abs(c), 1e-15)
            maxnorm = (1.0 - eps) / jnp.sqrt(abs_c)
            norm = jnp.linalg.norm(x, axis=-1, keepdims=True)
            scale = jnp.where(norm > maxnorm, maxnorm / norm, jnp.ones_like(norm))
            return x * scale

        def _forward(x, time_emb, edge_time, Wq, Wk, Wv, rel_q, rel_k, rel_v, Wt, bt, Wd1, bd1, Wd2, bd2, decay_scale, c_mag, hyp_beta, logit_alpha, Wo, bo, g1, be1, g2, be2, Wf1, bf1, Wf2, bf2, src, dst, edge_type):
            n = x.shape[0]
            Q = (x @ Wq).reshape(n, H, DH)
            K = (x @ Wk).reshape(n, H, DH)
            V = (x @ Wv).reshape(n, H, DH)
            q_dst = Q[dst] + rel_q[edge_type].reshape(-1, H, DH)
            k_src = K[src] + rel_k[edge_type].reshape(-1, H, DH)
            v_src = V[src] + rel_v[edge_type].reshape(-1, H, DH)
            k_src = k_src + (time_emb @ Wt + bt).reshape(-1, H, DH)
            euclid = jnp.sum(q_dst * k_src, axis=-1) / np.float32(np.sqrt(DH))
            denom_t = jnp.maximum(1.0, edge_type.max().astype(jnp.float32) + 1.0)
            et = edge_type.astype(jnp.float32)[:, None] / denom_t
            dec_in = jnp.concatenate([edge_time[:, None], et], axis=-1)
            decay_raw = jnp.tanh(jax.nn.relu(dec_in @ Wd1 + bd1) @ Wd2 + bd2)
            decay = jnp.exp(decay_scale[None, :] * decay_raw)
            euclid = euclid * decay
            c = -jnp.abs(c_mag)
            m = _proj(_expmap(x, c), c)
            man_dist = jnp.linalg.norm(m[src] - m[dst], axis=-1)[:, None]
            hyp = -hyp_beta[None, :] * man_dist * decay
            alpha = jax.nn.sigmoid(logit_alpha)[None, :]
            logits = alpha * euclid + (1.0 - alpha) * hyp
            seg_max = jax.ops.segment_max(logits, dst, num_segments=n)
            ex = jnp.exp(logits - seg_max[dst])
            denom = jax.ops.segment_sum(ex, dst, num_segments=n)
            attn = ex / denom[dst]
            agg = jax.ops.segment_sum(v_src * attn[..., None], dst, num_segments=n).reshape(n, D)
            out = agg @ Wo + bo
            x = _ln(x + out, g1, be1)
            ffn = jax.nn.gelu(x @ Wf1 + bf1, approximate=False) @ Wf2 + bf2
            x = _ln(x + ffn, g2, be2)
            return x
        key = jax.random.key(seed)
        ks = jax.random.split(key, 20)

        def lin(k, fi, fo):
            return jax.random.normal(k, (fi, fo), jnp.float32) / np.float32(np.sqrt(fi))
        return {'x': jax.random.normal(ks[0], (N, D), jnp.float32), 'edge_index': jax.random.randint(ks[1], (2, E), 0, N), 'time_emb': jax.random.normal(ks[2], (E, T), jnp.float32), 'edge_type': jax.random.randint(ks[3], (E,), 0, NET), 'edge_time': jax.random.uniform(ks[4], (E,), jnp.float32), 'Wq': lin(ks[5], D, D), 'Wk': lin(ks[6], D, D), 'Wv': lin(ks[7], D, D), 'rel_q': jax.random.normal(ks[8], (NET, D), jnp.float32) * 0.1, 'rel_k': jax.random.normal(ks[9], (NET, D), jnp.float32) * 0.1, 'rel_v': jax.random.normal(ks[10], (NET, D), jnp.float32) * 0.1, 'Wt': lin(ks[11], T, D), 'bt': jnp.zeros((D,), jnp.float32), 'Wd1': lin(ks[12], 2, 64), 'bd1': jnp.zeros((64,), jnp.float32), 'Wd2': lin(ks[13], 64, H), 'bd2': jnp.zeros((H,), jnp.float32), 'decay_scale': jnp.full((H,), 0.5, jnp.float32), 'c_mag': jnp.asarray(1.0, jnp.float32), 'hyp_beta': jnp.ones((H,), jnp.float32), 'logit_alpha': jnp.zeros((H,), jnp.float32), 'Wo': lin(ks[14], D, D), 'bo': jnp.zeros((D,), jnp.float32), 'g1': jnp.ones((D,), jnp.float32), 'be1': jnp.zeros((D,), jnp.float32), 'g2': jnp.ones((D,), jnp.float32), 'be2': jnp.zeros((D,), jnp.float32), 'Wf1': lin(ks[15], D, 4 * D), 'bf1': jnp.zeros((4 * D,), jnp.float32), 'Wf2': lin(ks[16], 4 * D, D), 'bf2': jnp.zeros((D,), jnp.float32)}
    _L0_gnn_all = _L0_gnn_setup()
    _L0_gnn_in = {k: v for k, v in _L0_gnn_all.items() if k in ('Wq', 'Wk', 'Wv', 'rel_q', 'rel_k', 'rel_v', 'Wt', 'bt', 'Wd1', 'bd1', 'Wd2', 'bd2', 'decay_scale', 'c_mag', 'hyp_beta', 'logit_alpha', 'Wo', 'bo', 'g1', 'be1', 'g2', 'be2', 'Wf1', 'bf1', 'Wf2', 'bf2')}
    del _L0_gnn_all

    def _L1_gnn_setup():
        import jax, jax.numpy as jnp
        import numpy as np
        N = 3125
        E = 31250
        HID = 128
        H = 4
        D = HID // H
        NUM_EDGE_TYPES = 8
        EPS_LN = 1e-05
        key = jax.random.key(seed)
        ks = jax.random.split(key, 16)
        s = 1.0 / np.sqrt(HID)
        return {'node_embeddings': jax.random.normal(ks[0], (N, HID), jnp.float32), 'edge_index': jax.random.randint(ks[1], (2, E), 0, N, jnp.int32), 'edge_type': jax.random.randint(ks[2], (E,), 0, NUM_EDGE_TYPES, jnp.int32), 'task_embedding': jax.random.normal(ks[3], (HID,), jnp.float32), 'W_src': jax.random.normal(ks[4], (HID, HID), jnp.float32) * s, 'b_src': jnp.zeros((HID,), jnp.float32), 'W_dst': jax.random.normal(ks[5], (HID, HID), jnp.float32) * s, 'b_dst': jnp.zeros((HID,), jnp.float32), 'edge_emb': jax.random.normal(ks[6], (NUM_EDGE_TYPES, HID), jnp.float32), 'att': jax.random.normal(ks[7], (H, D), jnp.float32) * s, 'W_out': jax.random.normal(ks[8], (HID, HID), jnp.float32) * s, 'b_out': jnp.zeros((HID,), jnp.float32), 'norm_w': jnp.ones((HID,), jnp.float32), 'norm_b': jnp.zeros((HID,), jnp.float32), 'W_film': jax.random.normal(ks[9], (HID, 2 * HID), jnp.float32) * s, 'b_film': jnp.zeros((2 * HID,), jnp.float32)}
    _L1_gnn_all = _L1_gnn_setup()
    _L1_gnn_in = {k: v for k, v in _L1_gnn_all.items() if k in ('task_embedding', 'W_src', 'b_src', 'W_dst', 'b_dst', 'edge_emb', 'att', 'W_out', 'b_out', 'norm_w', 'norm_b', 'W_film', 'b_film')}
    del _L1_gnn_all
    return {'x': x, 'src': src, 'dst': dst, 'edge_attr_32': edge_attr_32, 'edge_type_2': edge_type_2, 'edge_type_8': edge_type_8, 'edge_weight': edge_weight, 'L0_gnn_Wq': _L0_gnn_in['Wq'], 'L0_gnn_Wk': _L0_gnn_in['Wk'], 'L0_gnn_Wv': _L0_gnn_in['Wv'], 'L0_gnn_rel_q': _L0_gnn_in['rel_q'], 'L0_gnn_rel_k': _L0_gnn_in['rel_k'], 'L0_gnn_rel_v': _L0_gnn_in['rel_v'], 'L0_gnn_Wt': _L0_gnn_in['Wt'], 'L0_gnn_bt': _L0_gnn_in['bt'], 'L0_gnn_Wd1': _L0_gnn_in['Wd1'], 'L0_gnn_bd1': _L0_gnn_in['bd1'], 'L0_gnn_Wd2': _L0_gnn_in['Wd2'], 'L0_gnn_bd2': _L0_gnn_in['bd2'], 'L0_gnn_decay_scale': _L0_gnn_in['decay_scale'], 'L0_gnn_c_mag': _L0_gnn_in['c_mag'], 'L0_gnn_hyp_beta': _L0_gnn_in['hyp_beta'], 'L0_gnn_logit_alpha': _L0_gnn_in['logit_alpha'], 'L0_gnn_Wo': _L0_gnn_in['Wo'], 'L0_gnn_bo': _L0_gnn_in['bo'], 'L0_gnn_g1': _L0_gnn_in['g1'], 'L0_gnn_be1': _L0_gnn_in['be1'], 'L0_gnn_g2': _L0_gnn_in['g2'], 'L0_gnn_be2': _L0_gnn_in['be2'], 'L0_gnn_Wf1': _L0_gnn_in['Wf1'], 'L0_gnn_bf1': _L0_gnn_in['bf1'], 'L0_gnn_Wf2': _L0_gnn_in['Wf2'], 'L0_gnn_bf2': _L0_gnn_in['bf2'], 'L1_gnn_task_embedding': _L1_gnn_in['task_embedding'], 'L1_gnn_W_src': _L1_gnn_in['W_src'], 'L1_gnn_b_src': _L1_gnn_in['b_src'], 'L1_gnn_W_dst': _L1_gnn_in['W_dst'], 'L1_gnn_b_dst': _L1_gnn_in['b_dst'], 'L1_gnn_edge_emb': _L1_gnn_in['edge_emb'], 'L1_gnn_att': _L1_gnn_in['att'], 'L1_gnn_W_out': _L1_gnn_in['W_out'], 'L1_gnn_b_out': _L1_gnn_in['b_out'], 'L1_gnn_norm_w': _L1_gnn_in['norm_w'], 'L1_gnn_norm_b': _L1_gnn_in['norm_b'], 'L1_gnn_W_film': _L1_gnn_in['W_film'], 'L1_gnn_b_film': _L1_gnn_in['b_film']}

def reference(x, src, dst, edge_attr_32, edge_type_2, edge_type_8, edge_weight, L0_gnn_Wq, L0_gnn_Wk, L0_gnn_Wv, L0_gnn_rel_q, L0_gnn_rel_k, L0_gnn_rel_v, L0_gnn_Wt, L0_gnn_bt, L0_gnn_Wd1, L0_gnn_bd1, L0_gnn_Wd2, L0_gnn_bd2, L0_gnn_decay_scale, L0_gnn_c_mag, L0_gnn_hyp_beta, L0_gnn_logit_alpha, L0_gnn_Wo, L0_gnn_bo, L0_gnn_g1, L0_gnn_be1, L0_gnn_g2, L0_gnn_be2, L0_gnn_Wf1, L0_gnn_bf1, L0_gnn_Wf2, L0_gnn_bf2, L1_gnn_task_embedding, L1_gnn_W_src, L1_gnn_b_src, L1_gnn_W_dst, L1_gnn_b_dst, L1_gnn_edge_emb, L1_gnn_att, L1_gnn_W_out, L1_gnn_b_out, L1_gnn_norm_w, L1_gnn_norm_b, L1_gnn_W_film, L1_gnn_b_film):
    import jax
    import jax.numpy as jnp

    def _L0_gnn_ref(x, edge_index, time_emb, edge_type, edge_time, Wq, Wk, Wv, rel_q, rel_k, rel_v, Wt, bt, Wd1, bd1, Wd2, bd2, decay_scale, c_mag, hyp_beta, logit_alpha, Wo, bo, g1, be1, g2, be2, Wf1, bf1, Wf2, bf2):
        import jax, jax.numpy as jnp
        import numpy as np
        N = 6250
        E = 37500
        D = 128
        H = 8
        DH = D // H
        T = 32
        NET = 2

        def _ln(x, g, b, eps=1e-05):
            mu = jnp.mean(x, axis=-1, keepdims=True)
            var = jnp.mean((x - mu) ** 2, axis=-1, keepdims=True)
            return (x - mu) * jax.lax.rsqrt(var + eps) * g + b

        def _expmap(e, c):
            abs_c = jnp.maximum(jnp.abs(c), 1e-15)
            sq = jnp.sqrt(abs_c)
            n = jnp.maximum(jnp.linalg.norm(e, axis=-1, keepdims=True), 1e-15)
            tanh_p = jnp.tanh(sq * n) * e / (sq * n)
            tan_p = jnp.tan(sq * n) * e / (sq * n)
            return jnp.where(c < 0, tanh_p, tan_p)

        def _proj(x, c, eps=1e-05):
            abs_c = jnp.maximum(jnp.abs(c), 1e-15)
            maxnorm = (1.0 - eps) / jnp.sqrt(abs_c)
            norm = jnp.linalg.norm(x, axis=-1, keepdims=True)
            scale = jnp.where(norm > maxnorm, maxnorm / norm, jnp.ones_like(norm))
            return x * scale

        def _forward(x, time_emb, edge_time, Wq, Wk, Wv, rel_q, rel_k, rel_v, Wt, bt, Wd1, bd1, Wd2, bd2, decay_scale, c_mag, hyp_beta, logit_alpha, Wo, bo, g1, be1, g2, be2, Wf1, bf1, Wf2, bf2, src, dst, edge_type):
            n = x.shape[0]
            Q = (x @ Wq).reshape(n, H, DH)
            K = (x @ Wk).reshape(n, H, DH)
            V = (x @ Wv).reshape(n, H, DH)
            q_dst = Q[dst] + rel_q[edge_type].reshape(-1, H, DH)
            k_src = K[src] + rel_k[edge_type].reshape(-1, H, DH)
            v_src = V[src] + rel_v[edge_type].reshape(-1, H, DH)
            k_src = k_src + (time_emb @ Wt + bt).reshape(-1, H, DH)
            euclid = jnp.sum(q_dst * k_src, axis=-1) / np.float32(np.sqrt(DH))
            denom_t = jnp.maximum(1.0, edge_type.max().astype(jnp.float32) + 1.0)
            et = edge_type.astype(jnp.float32)[:, None] / denom_t
            dec_in = jnp.concatenate([edge_time[:, None], et], axis=-1)
            decay_raw = jnp.tanh(jax.nn.relu(dec_in @ Wd1 + bd1) @ Wd2 + bd2)
            decay = jnp.exp(decay_scale[None, :] * decay_raw)
            euclid = euclid * decay
            c = -jnp.abs(c_mag)
            m = _proj(_expmap(x, c), c)
            man_dist = jnp.linalg.norm(m[src] - m[dst], axis=-1)[:, None]
            hyp = -hyp_beta[None, :] * man_dist * decay
            alpha = jax.nn.sigmoid(logit_alpha)[None, :]
            logits = alpha * euclid + (1.0 - alpha) * hyp
            seg_max = jax.ops.segment_max(logits, dst, num_segments=n)
            ex = jnp.exp(logits - seg_max[dst])
            denom = jax.ops.segment_sum(ex, dst, num_segments=n)
            attn = ex / denom[dst]
            agg = jax.ops.segment_sum(v_src * attn[..., None], dst, num_segments=n).reshape(n, D)
            out = agg @ Wo + bo
            x = _ln(x + out, g1, be1)
            ffn = jax.nn.gelu(x @ Wf1 + bf1, approximate=False) @ Wf2 + bf2
            x = _ln(x + ffn, g2, be2)
            return x
        src, dst = (edge_index[0], edge_index[1])
        return _forward(x, time_emb, edge_time, Wq, Wk, Wv, rel_q, rel_k, rel_v, Wt, bt, Wd1, bd1, Wd2, bd2, decay_scale, c_mag, hyp_beta, logit_alpha, Wo, bo, g1, be1, g2, be2, Wf1, bf1, Wf2, bf2, src, dst, edge_type)

    def _L1_gnn_ref(node_embeddings, edge_index, edge_type, task_embedding, W_src, b_src, W_dst, b_dst, edge_emb, att, W_out, b_out, norm_w, norm_b, W_film, b_film):
        import jax, jax.numpy as jnp
        import numpy as np
        N = 3125
        E = 31250
        HID = 128
        H = 4
        D = HID // H
        NUM_EDGE_TYPES = 8
        EPS_LN = 1e-05
        num_nodes = node_embeddings.shape[0]
        src, dst = (edge_index[0], edge_index[1])
        x_src = (node_embeddings @ W_src + b_src).reshape(num_nodes, H, D)
        x_dst = (node_embeddings @ W_dst + b_dst).reshape(num_nodes, H, D)
        e = edge_emb[edge_type].reshape(-1, H, D)
        combined = jax.nn.leaky_relu(x_src[src] + x_dst[dst] + e, negative_slope=0.2)
        logits = jnp.einsum('ehd,hd->eh', combined, att)
        mx = jax.ops.segment_max(logits, dst, num_segments=num_nodes)
        mx = jnp.where(jnp.isinf(mx), jnp.zeros_like(mx), mx)
        ex = jnp.exp(logits - mx[dst])
        sums = jax.ops.segment_sum(ex, dst, num_segments=num_nodes)
        attn = ex / jnp.maximum(sums[dst], 1e-12)
        msg = x_src[src] * attn[..., None]
        agg = jax.ops.segment_sum(msg, dst, num_segments=num_nodes)
        agg = agg.reshape(num_nodes, HID) @ W_out + b_out
        film = task_embedding @ W_film + b_film
        gamma, beta = (film[:HID], film[HID:])
        agg = agg * (1.0 + 0.5 * jnp.tanh(gamma))[None, :] + beta[None, :]
        y = node_embeddings + agg
        mu = jnp.mean(y, axis=-1, keepdims=True)
        var = jnp.mean((y - mu) ** 2, axis=-1, keepdims=True)
        return (y - mu) / jnp.sqrt(var + EPS_LN) * norm_w + norm_b
    edge_index = jnp.stack([src, dst])
    x = _layernorm(x + _L0_gnn_ref(x, edge_index, edge_attr_32, edge_type_2, edge_weight, L0_gnn_Wq, L0_gnn_Wk, L0_gnn_Wv, L0_gnn_rel_q, L0_gnn_rel_k, L0_gnn_rel_v, L0_gnn_Wt, L0_gnn_bt, L0_gnn_Wd1, L0_gnn_bd1, L0_gnn_Wd2, L0_gnn_bd2, L0_gnn_decay_scale, L0_gnn_c_mag, L0_gnn_hyp_beta, L0_gnn_logit_alpha, L0_gnn_Wo, L0_gnn_bo, L0_gnn_g1, L0_gnn_be1, L0_gnn_g2, L0_gnn_be2, L0_gnn_Wf1, L0_gnn_bf1, L0_gnn_Wf2, L0_gnn_bf2), axis=-1)
    x = _layernorm(x + _L1_gnn_ref(x, edge_index, edge_type_8, L1_gnn_task_embedding, L1_gnn_W_src, L1_gnn_b_src, L1_gnn_W_dst, L1_gnn_b_dst, L1_gnn_edge_emb, L1_gnn_att, L1_gnn_W_out, L1_gnn_b_out, L1_gnn_norm_w, L1_gnn_norm_b, L1_gnn_W_film, L1_gnn_b_film), axis=-1)
    return x

_drawn_inputs = setup_inputs


def setup_inputs(seed=0):
    import zlib

    import numpy as np

    out = dict(_drawn_inputs(seed))
    spreads = {'L0_gnn_bt': (0.0, 2.0),
     'L0_gnn_bd1': (0.0, 0.8),
     'L0_gnn_bd2': (0.0, 2.0),
     'L0_gnn_decay_scale': (0.5, 0.6),
     'L0_gnn_hyp_beta': (1.0, 0.6),
     'L0_gnn_logit_alpha': (0.0, 0.8),
     'L0_gnn_bo': (0.0, 0.1),
     'L0_gnn_g1': (1.0, 0.2),
     'L0_gnn_be1': (0.0, 0.1),
     'L0_gnn_g2': (1.0, 0.2),
     'L0_gnn_be2': (0.0, 0.1),
     'L0_gnn_bf1': (0.0, 0.269),
     'L0_gnn_bf2': (0.0, 0.1),
     'L1_gnn_b_src': (0.0, 0.1),
     'L1_gnn_b_dst': (0.0, 2.0),
     'L1_gnn_b_out': (0.0, 0.1),
     'L1_gnn_norm_w': (1.0, 0.2),
     'L1_gnn_norm_b': (0.0, 0.1),
     'L1_gnn_b_film': (0.0, 0.1)}
    factors = {'edge_weight': 8.0,
     'L0_gnn_rel_q': 5.933,
     'L0_gnn_rel_k': 8.0,
     'L0_gnn_Wd1': 4.643,
     'L0_gnn_Wd2': 4.568,
     'L1_gnn_W_dst': 3.419}
    for name, (base, spread) in spreads.items():
        noise = np.random.default_rng([zlib.crc32(name.encode()), seed]).standard_normal(out[name].shape)
        drawn = base * np.exp(spread * noise) if base else spread * noise
        out[name] = jnp.asarray(drawn.astype(out[name].dtype))
    for name, factor in factors.items():
        out[name] = (out[name] * factor).astype(out[name].dtype)
    return out
```

```python
import math
from contextlib import ExitStack

import numpy as np

import concourse.bass as bass
from concourse import mybir

F32 = mybir.dt.float32
BF16 = mybir.dt.bfloat16
I32 = mybir.dt.int32
ALU = mybir.AluOpType
ACT = mybir.ActivationFunctionType
AX = mybir.AxisListType
ET = mybir.EngineType

P = 128
D = 128
BN = 120
NT = P - BN
G = 16
QS = 4
NQ = G // QS
BIG = 1e30
H0, H1 = 8, 4
TE_ROWS = 32
HID = 64
R_TYPE, R_TIME, R_ONE = 32, 33, 34
FF = 512


class Mark:

    def __init__(self, sem, per, credit=0):
        self.sem, self.per, self.credit = sem, per, credit

    def at(self, g, k):
        return g * self.per + (self.credit + k)


class Chain:

    def __init__(self, eng, sem, base=0):
        self.eng, self.sem, self.base, self.n = eng, sem, base, 0

    def did(self, ins):
        self.n += 1
        ins.then_inc(self.sem, 1)

    def settle(self):
        self.eng.wait_ge(self.sem, self.base + self.n)

    def __call__(self, ins):
        self.did(ins)
        self.settle()


def apart(eng, passed):
    eng.sem_inc(passed, 1)


def bc(ap, axis, n):
    a = ap.unsqueeze(axis)
    shape = list(a.shape)
    shape[axis] = n
    return a.broadcast_to(shape)


class Sizes:
    def __init__(self, n_nodes, n_tiles):
        self.n = n_nodes
        self.tiles = n_tiles
        self.nb = math.ceil(n_nodes / BN)
        self.nbp = math.ceil(self.nb / 6) * 6
        self.steps = math.ceil((n_tiles + self.nb - 1) / (2 * G)) * 2 * G
        self.ng = self.steps // G


def program(nc, io, sz):
    with ExitStack() as ctx:
        k = Kept(nc, ctx, io, sz)
        prepare(nc, k)
        tables0(nc, k)
        edges0(nc, k)
        scores0(nc, k)
        segment_max(nc, k, H0, "a")
        weighted_sums(nc, k, H0, D + 2 * H0, "a")
        nodes0(nc, k)
        clear_semaphores(nc, k)
        edges1(nc, k)
        segment_max(nc, k, H1, "b")
        weighted_sums(nc, k, H1, D + H1, "b")
        nodes1(nc, k)


class Kept:

    def __init__(self, nc, ctx, io, sz):
        self.io, self.sz = io, sz
        S, nbp = sz.steps, sz.nbp

        def sb(name, shape, dt=F32):
            return ctx.enter_context(nc.sbuf_tensor(name, shape, dt))

        self.dst = sb("dst_f", [P, S])
        self.dstl = sb("dst_local", [P, S], BF16)
        self.typ2 = sb("type2", [P, S], BF16)
        self.typ8 = sb("type8", [P, S], BF16)
        self.src = sb("src_i", [P, S], I32)
        self.blkf = sb("block_first", [P, S])
        self.tile_block = sb("tile_block", [2, S], I32)
        self.iden = sb("iden", [P, P])
        self.idenb = sb("idenb", [P, P], BF16)
        self.iota = sb("iota_f", [P, P])
        self.iotab = sb("iota_b", [P, P], BF16)
        self.wedge = sb("wedge", [R_ONE + 1, D])
        self.wdec1 = sb("wdec1", [R_ONE + 1, HID])
        self.wdec2 = sb("wdec2", [HID + 1, H0])
        self.heads = sb("heads", [P, 3, H0])
        self.big = sb("big", [P, max(nbp * 256, S * 22)])
        self.pair = sb("scores_exps", [P, max(2 * S * H0, nbp * D)])
        self.sco = self.pair[:, 0:S * H0]
        self.exs = self.pair[:, S * H0:2 * S * H0]
        self.retired = []
        self.passed = ctx.enter_context(nc.semaphore("passed"))
        def dr(name, shape, dt=F32):
            return nc.dram_tensor(name, shape, dt, kind="Internal").ap()

        self.d_sched = dr("d_sched", (2, S), I32)
        self.d_blkf = dr("d_blkf", (S,))
        self.d_typerows = dr("d_typerows", (NT, 256))
        self.d_table0 = dr("d_table0", (nbp * BN, 3 * D))
        self.d_table1 = dr("d_table1", (nbp * BN, D))
        self.d_value = dr("d_value", (S // QS, P, QS, D))
        self.d_x1 = dr("d_x1", (nbp * BN, D))


def clear_semaphores(nc, k):
    numbers = sorted(k.retired)
    assert numbers == list(range(numbers[0], numbers[-1] + 1))
    with nc.Block() as block:
        @block.sync
        def _(sp):
            sp.sem_clear(range(numbers[0], numbers[-1] + 1))


def stage(nc, ctx, prefix, retired=None):
    def sb(name, shape, dt=F32):
        return ctx.enter_context(nc.sbuf_tensor(f"{prefix}_{name}", shape, dt))

    def pb(name, shape, dt=F32):
        return ctx.enter_context(nc.psum_tensor(f"{prefix}_{name}", shape, dt))

    def sem(name):
        s = ctx.enter_context(nc.semaphore(f"{prefix}_{name}"))
        if retired is not None:
            retired.append(s.num)
        return s

    return sb, pb, sem


class Carve:

    def __init__(self, ap, start=0):
        self.ap, self.at = ap, start

    def __call__(self, shape, dt=F32):
        n = math.prod(shape[1:])
        v = self.ap[0:shape[0], self.at:self.at + n]
        self.at += n
        assert self.at <= self.ap.shape[1]
        if dt is not F32:
            v = v.bitcast(dt)
        if len(shape) == 3:
            v = v.rearrange("p (a b) -> p a b", b=shape[2])
        return v


def row(ap):
    return ap.rearrange("(a n) -> a n", a=1)


def prepare(nc, k):
    io, sz = k.io, k.sz
    T, S, NB = sz.tiles, sz.steps, sz.nb
    C = S // P if S % P == 0 else S // P + 1
    with ExitStack() as ctx:
        sb, pb, sem = stage(nc, ctx, "pre", k.retired)
        cut = Carve(k.big)
        ends_i = cut([P, 2, T], I32)
        ends = cut([P, 2, T])
        q_i = cut([P, 2, T], I32)
        q = cut([P, 2, T])
        rem = cut([P, 2, T])
        flag = cut([P, 2, T])
        count = cut([P, T])
        begin = cut([P, T])
        gap = cut([P, T])
        dgap = cut([P, T])
        zero = cut([P, T])
        junk = cut([P, T])
        stepno_i = sb("stepno_i", [P, C], I32)
        stepno = sb("stepno", [P, C])
        tno = sb("tno", [P, C])
        bno = sb("bno", [P, C])
        gsum = sb("gsum", [P, C])
        both_i = sb("both_i", [P, 2, C], I32)
        io_i = sb("io_i", [P, P], I32)
        types = cut([P, T], I32)
        typesf = cut([P, T])
        tmax = sb("tmax", [P, 1])
        tall = sb("tall", [P, 1])
        rden = sb("rden", [P, 1])
        la = sb("la", [P, H0])
        beta = sb("beta", [P, H0])
        sig = sb("sig", [P, 3, H0])
        rk = sb("rk", [1, 3, D])
        rk_out = sb("rk_out", [1, 2, D])
        wd = sb("wd", [1, HID])
        wd_out = sb("wd_out", [1, HID])
        zrow = sb("zrow", [1, D])
        rq = sb("rq", [2, D])
        trow = sb("trow", [NT, 2 * D])
        loaded, ident, vec, vdone, pool, sched, late, act_s = (sem(n) for n in (
            "loaded", "ident", "vec", "vdone", "pool", "sched", "late", "act"))
        n_loads = 15
        with nc.Block() as block:
            @block.sync
            def _(sp):
                def load(dst, src):
                    sp.dma_start(dst, src).then_inc(loaded, 16)

                load(ends_i[:, 0, :], io["first"].partition_broadcast(P))
                load(ends_i[:, 1, :], io["last"].partition_broadcast(P))
                load(types[:, :], io["type2"].rearrange("(p c) -> p c", p=P))
                load(la[:, :], io["L0_gnn_logit_alpha"].partition_broadcast(P))
                load(beta[:, :], io["L0_gnn_hyp_beta"].partition_broadcast(P))
                load(k.heads[:, 0, :], io["L0_gnn_decay_scale"].partition_broadcast(P))
                load(k.wedge[0:TE_ROWS, :], io["L0_gnn_Wt"])
                load(rk[0:1, 0:2, :], io["L0_gnn_rel_k"].rearrange("(a t) d -> a t d", a=1))
                load(rk[0:1, 2, :], row(io["L0_gnn_bt"]))
                load(wd[:, :], io["L0_gnn_Wd1"][1:2, :])
                load(k.wdec1[R_TIME:R_TIME + 1, :], io["L0_gnn_Wd1"][0:1, :])
                load(k.wdec1[R_ONE:R_ONE + 1, :], row(io["L0_gnn_bd1"]))
                load(k.wdec2[0:HID, :], io["L0_gnn_Wd2"])
                load(k.wdec2[HID:HID + 1, :], row(io["L0_gnn_bd2"]))
                load(rq[:, :], io["L0_gnn_rel_q"])
                sp.wait_ge(vdone, 1)
                full, rest = S // P, S % P
                n = 0
                for src, dst in ((both_i[:, 0, :], k.d_sched[0]), (both_i[:, 1, :], k.d_sched[1]),
                                 (bno[:, :], k.d_blkf)):
                    if full:
                        sp.dma_start(dst[0:full * P].rearrange("(c p) -> p c", p=P), src[:, 0:full],
                                     allow_slow_non_contiguous=True).then_inc(sched, 16)
                        n += 16
                    if rest:
                        sp.dma_start(dst[full * P:S].rearrange("(p c) -> p c", c=1), src[0:rest, full:full + 1],
                                     allow_slow_non_contiguous=True).then_inc(sched, 16)
                        n += 16
                sp.wait_ge(vdone, 4)
                sp.dma_start(k.wedge[R_TYPE:R_TYPE + 1, :], rk_out[0:1, 0, :]).then_inc(late, 16)
                sp.dma_start(k.wedge[R_ONE:R_ONE + 1, :], rk_out[0:1, 1, :]).then_inc(late, 16)
                sp.dma_start(k.wedge[R_TIME:R_TIME + 1, :], zrow[:, :]).then_inc(late, 16)
                sp.dma_start(k.wdec1[R_TYPE:R_TYPE + 1, :], wd_out[:, :]).then_inc(late, 16)
                sp.dma_start(k.d_typerows, trow[:, :]).then_inc(late, 16)
                sp.wait_ge(sched, n)
                sp.dma_start(k.tile_block[:, :], k.d_sched[:, :]).then_inc(late, 16)
                sp.dma_start(k.blkf[:, :], k.d_blkf.partition_broadcast(P)).then_inc(late, 16)
                sp.wait_ge(late, 7 * 16)

            @block.gpsimd
            def _(pl):
                nc.gpsimd.memset(k.iden[:, :], 0.0).then_inc(ident, 1)
                nc.gpsimd.iota(io_i[:, :], pattern=[[1, P]], base=0, channel_multiplier=0).then_inc(pool, 1)
                nc.gpsimd.iota(stepno_i[:, :], pattern=[[P, C]], base=0, channel_multiplier=1).then_inc(pool, 1)
                pl.wait_ge(ident, 1)
                nc.gpsimd.affine_select(out=k.iden[:, :], in_=k.iden[:, :], compare_op=ALU.not_equal, fill=1.0,
                                        base=0, pattern=[[-1, P]], channel_multiplier=1).then_inc(pool, 1)
                pl.wait_ge(vdone, 3)
                nc.gpsimd.partition_all_reduce(tall[:, :], tmax[:, :], P, bass.bass_isa.ReduceOp.max).then_inc(pool, 1)

            @block.scalar
            def _(act):
                act.wait_ge(loaded, 16 * n_loads)
                nc.scalar.activation(sig[:, 0, :], la[:, :], ACT.Exp, scale=-1.0).then_inc(act_s, 1)

            @block.vector
            def _(dve):
                v = Chain(dve, vec)
                V = nc.vector
                dve.wait_ge(pool, 3)
                v(V.tensor_copy(k.iota[:, :], io_i[:, :]))
                v(V.tensor_copy(k.iotab[:, :], io_i[:, :]))
                v(V.tensor_copy(k.idenb[:, :], k.iden[:, :]))
                v(V.tensor_copy(stepno[:, :], stepno_i[:, :]))
                v(V.memset(zero[:, :], 0.0))
                v(V.memset(zrow[:, :], 0.0))
                v(V.memset(trow[:, :], 0.0))
                dve.wait_ge(loaded, 16 * n_loads)
                v(V.tensor_copy(ends[:, :, :], ends_i[:, :, :]))
                v(V.tensor_scalar(q_i[:, :, :], ends[:, :, :], 1.0 / BN, None, ALU.mult))
                v(V.tensor_copy(q[:, :, :], q_i[:, :, :]))
                ef = ends[:, :, :].rearrange("p a t -> p (a t)")
                qf = q[:, :, :].rearrange("p a t -> p (a t)")
                rf = rem[:, :, :].rearrange("p a t -> p (a t)")
                ff = flag[:, :, :].rearrange("p a t -> p (a t)")
                v(V.scalar_tensor_tensor(rf, qf, -float(BN), ef, ALU.mult, ALU.add))
                v(V.tensor_scalar(ff, rf, float(BN), None, ALU.is_ge))
                v(V.tensor_tensor(qf, qf, ff, ALU.add))
                v(V.tensor_scalar(ff, rf, 0.0, None, ALU.is_lt))
                v(V.tensor_tensor(qf, qf, ff, ALU.subtract))
                v(V.tensor_tensor(count[:, :], q[:, 1, :], q[:, 0, :], ALU.subtract))
                v(V.tensor_scalar(count[:, :], count[:, :], 1.0, None, ALU.add))
                v(V.tensor_tensor_scan(begin[:, :], count[:, :], zero[:, :], 0.0, ALU.add, ALU.add))
                v(V.tensor_tensor(begin[:, :], begin[:, :], count[:, :], ALU.subtract))
                v(V.tensor_tensor(gap[:, :], q[:, 0, :], begin[:, :], ALU.subtract))
                v(V.tensor_copy(dgap[:, 0:1], gap[:, 0:1]))
                v(V.tensor_tensor(dgap[:, 1:T], gap[:, 1:T], gap[:, 0:T - 1], ALU.subtract))
                for c in range(C):
                    v(V.tensor_scalar(junk[:, :], begin[:, :], stepno[:, c:c + 1], None, ALU.is_le, ALU.add,
                                      accum_out=tno[:, c:c + 1]))
                    v(V.scalar_tensor_tensor(junk[:, :], begin[:, :], stepno[:, c:c + 1], dgap[:, :], ALU.is_le,
                                             ALU.mult, accum_out=gsum[:, c:c + 1]))
                v(V.tensor_tensor(bno[:, :], gsum[:, :], stepno[:, :], ALU.add))
                v(V.tensor_scalar(tno[:, :], tno[:, :], 1.0, 0.0, ALU.subtract, ALU.max))
                v(V.tensor_scalar(both_i[:, 0, :], tno[:, :], float(T - 1), None, ALU.min))
                v(V.tensor_scalar(both_i[:, 1, :], bno[:, :], float(NB - 1), 0.0, ALU.min, ALU.max))
                v(V.tensor_scalar(bno[:, :], bno[:, :], float(BN), None, ALU.mult))
                dve.sem_inc(vdone, 1)
                dve.wait_ge(act_s, 1)
                v(V.tensor_scalar(sig[:, 1, :], sig[:, 0, :], 1.0, None, ALU.add))
                v(V.reciprocal(sig[:, 2, :], sig[:, 1, :]))
                v(V.tensor_scalar(k.heads[:, 2, :], sig[:, 2, :], 1.0 / math.sqrt(D // H0), None, ALU.mult))
                v(V.tensor_scalar(sig[:, 1, :], sig[:, 2, :], 1.0, None, ALU.subtract))
                v(V.tensor_tensor(k.heads[:, 1, :], sig[:, 1, :], beta[:, :], ALU.mult))
                v(V.tensor_tensor(rk_out[0:1, 0, :], rk[0:1, 1, :], rk[0:1, 0, :], ALU.subtract))
                v(V.tensor_tensor(rk_out[0:1, 1, :], rk[0:1, 0, :], rk[0:1, 2, :], ALU.add))
                v(V.tensor_tensor(trow[0:2, 0:D].rearrange("p (h d) -> p h d", h=H0),
                                  rq[:, :].rearrange("p (h d) -> p h d", h=H0),
                                  bc(k.heads[0:2, 2, :], 2, D // H0), ALU.mult))
                v(V.tensor_copy(typesf[:, :], types[:, :]))
                v(V.tensor_reduce(tmax[:, :], typesf[:, :], AX.X, ALU.max))
                dve.sem_inc(vdone, 2)
                dve.wait_ge(pool, 4)
                v(V.tensor_scalar(tall[:, :], tall[:, :], 1.0, 1.0, ALU.add, ALU.max))
                v(V.reciprocal(rden[:, :], tall[:, :]))
                v(V.tensor_scalar(wd_out[:, :], wd[:, :], rden[0:1, :], None, ALU.mult))
                dve.sem_inc(vdone, 1)


def tables0(nc, k):
    io, sz = k.io, k.sz
    NBP = sz.nbp
    with ExitStack() as ctx:
        sb, pb, sem = stage(nc, ctx, "tab", k.retired)
        qm = k.big[:, 0:NBP * 256].rearrange("p (b c) -> p b c", c=256)
        xall = Carve(k.pair)([BN, NBP, D])
        xsq = Carve(k.big)([BN, NBP, D])
        wqkv = sb("wqkv", [P, 3, D])
        xt = [sb(f"xt{u}", [P, BN]) for u in range(2)]
        kmv = [sb(f"kmv{u}", [BN, 3 * D]) for u in range(2)]
        pq = [pb(f"pq{u}", [P, D]) for u in range(2)]
        pkv = [pb(f"pkv{u}", [P, 2 * D]) for u in range(2)]
        n = {m: sb(m, [BN, NBP]) for m in ("n2", "nrm", "z", "th", "rz", "zt", "zc", "sn", "cs", "f", "nm", "ov", "sc", "s", "sneg")}
        cc = {m: sb(m, [P, 1]) for m in ("c", "cn", "ca", "pos", "npos", "ac", "sq", "rsq", "mx")}
        loaded, vec, toact, fract, tdone = (sem(m) for m in ("loaded", "vec", "toact", "fract", "tdone"))
        xt_in = [Mark(sem(f"xtin{u}"), 16) for u in range(2)]
        mm = Mark(sem("mm"), 2, 2)
        ev_q, ev_kv = Mark(sem("evq"), 2, 2), Mark(sem("evkv"), 2, 2)
        st = [Mark(sem(f"st{u}"), 16, 16) for u in range(2)]
        with nc.Block() as block:
            @block.sync
            def _(sp):
                sp.sem_inc(mm.sem, 2)
                sp.sem_inc(ev_q.sem, 2)
                sp.sem_inc(ev_kv.sem, 2)
                for u in range(2):
                    sp.sem_inc(st[u].sem, 16)
                sp.dma_start(xall[:, :, :], io["x"].rearrange("(b p) d -> p b d", p=BN)).then_inc(loaded, 16)
                for i, w in enumerate(("Wq", "Wk", "Wv")):
                    sp.dma_start(wqkv[:, i, :], io["L0_gnn_" + w]).then_inc(loaded, 16)
                sp.dma_start(cc["c"][:, :], io["c_mag"].partition_broadcast(P)).then_inc(loaded, 16)
                sp.dma_start(qm[BN:P, :, :], bc(k.d_typerows, 1, NBP)).then_inc(tdone, 16)
                with sp.Fori(0, NBP // 2) as g:
                    for u in range(2):
                        sp.wait_ge(mm.sem, mm.at(g, 0))
                        sp.dma_start(xt[u][:, :], io["xT"][:, bass.ds(g * (2 * BN) + u * BN, BN)]).then_inc(xt_in[u].sem, 16)
                    for u in range(2):
                        sp.wait_ge(ev_q.sem, ev_q.at(g, u + 1))
                        sp.wait_ge(ev_kv.sem, ev_kv.at(g, u + 1))
                        sp.dma_start(k.d_table0[bass.ds(g * (2 * BN) + u * BN, BN), :], kmv[u][:, :]).then_inc(st[u].sem, 16)
                for u in range(2):
                    sp.wait_ge(st[u].sem, 16 + 16 * (NBP // 2))
                sp.wait_ge(tdone, 16)

            @block.vector
            def _(dve):
                V = nc.vector
                v = Chain(dve, vec)
                dve.wait_ge(loaded, 16 * 5)
                v(V.tensor_tensor(wqkv[:, 0, :].rearrange("p (h d) -> p h d", h=H0),
                                  wqkv[:, 0, :].rearrange("p (h d) -> p h d", h=H0),
                                  bc(k.heads[:, 2, :], 2, D // H0), ALU.mult))
                v(V.tensor_tensor(xsq[:, :, :], xall[:, :, :], xall[:, :, :], ALU.mult))
                v(V.tensor_reduce(n["n2"][:, :], xsq[:, :, :], AX.X, ALU.add))
                v(V.tensor_scalar(cc["cn"][:, :], cc["c"][:, :], -1.0, None, ALU.mult))
                v(V.tensor_tensor(cc["ca"][:, :], cc["c"][:, :], cc["cn"][:, :], ALU.max))
                v(V.tensor_scalar(cc["pos"][:, :], cc["ca"][:, :], 0.0, None, ALU.is_gt))
                v(V.tensor_scalar(cc["npos"][:, :], cc["pos"][:, :], -1.0, 1.0, ALU.mult, ALU.add))
                v(V.tensor_scalar(cc["ac"][:, :], cc["ca"][:, :], 1e-15, None, ALU.max))
                dve.sem_inc(toact, 1)
                dve.wait_ge(fract, 1)
                v(V.tensor_scalar(n["nrm"][:, :], n["nrm"][:, :], 1e-15, None, ALU.max))
                v(V.tensor_scalar(n["z"][:, :], n["nrm"][:, :], cc["sq"][0:BN, :], None, ALU.mult))
                v(V.tensor_scalar(n["zt"][:, :], n["z"][:, :], 1.5, None, ALU.min))
                v(V.tensor_scalar(n["zc"][:, :], n["zt"][:, :], -1.0, math.pi / 2, ALU.mult, ALU.add))
                dve.sem_inc(toact, 1)
                v(V.reciprocal(n["rz"][:, :], n["z"][:, :]))
                v(V.reciprocal(cc["rsq"][:, :], cc["sq"][:, :]))
                v(V.tensor_scalar(cc["mx"][:, :], cc["rsq"][:, :], 1.0 - 1e-5, None, ALU.mult))
                dve.wait_ge(fract, 2)
                v(V.tensor_tensor(n["th"][:, :], n["th"][:, :], n["rz"][:, :], ALU.mult))
                v(V.tensor_tensor(n["cs"][:, :], n["cs"][:, :], n["zt"][:, :], ALU.mult))
                v(V.reciprocal(n["cs"][:, :], n["cs"][:, :]))
                v(V.tensor_tensor(n["sn"][:, :], n["sn"][:, :], n["cs"][:, :], ALU.mult))
                v(V.tensor_scalar(n["sn"][:, :], n["sn"][:, :], cc["npos"][0:BN, :], None, ALU.mult))
                v(V.scalar_tensor_tensor(n["f"][:, :], n["th"][:, :], cc["pos"][0:BN, :], n["sn"][:, :], ALU.mult, ALU.add))
                v(V.tensor_tensor(n["nm"][:, :], n["f"][:, :], n["nrm"][:, :], ALU.mult))
                v(V.tensor_scalar(n["ov"][:, :], n["nm"][:, :], cc["mx"][0:BN, :], None, ALU.is_gt))
                v(V.reciprocal(n["sc"][:, :], n["nm"][:, :]))
                v(V.tensor_scalar(n["sc"][:, :], n["sc"][:, :], cc["mx"][0:BN, :], 1.0, ALU.mult, ALU.subtract))
                v(V.tensor_tensor(n["sc"][:, :], n["sc"][:, :], n["ov"][:, :], ALU.mult))
                v(V.tensor_scalar(n["sc"][:, :], n["sc"][:, :], 1.0, None, ALU.add))
                v(V.tensor_tensor(n["s"][:, :], n["f"][:, :], n["sc"][:, :], ALU.mult))
                v(V.tensor_scalar(n["sneg"][:, :], n["s"][:, :], -1.0, None, ALU.mult))
                with dve.Fori(0, NBP // 2) as g:
                    for u in range(2):
                        b = g * 2 + u
                        V.tensor_scalar(qm[0:BN, bass.ds(b, 1), D:2 * D], xall[:, bass.ds(b, 1), :],
                                        n["sneg"][:, bass.ds(b, 1)], None, ALU.mult)
                        dve.wait_ge(st[u].sem, st[u].at(g, 0))
                        V.tensor_scalar(kmv[u][:, D:2 * D], xall[:, bass.ds(b, 1), :].rearrange("p a d -> p (a d)"),
                                        n["s"][:, bass.ds(b, 1)], None, ALU.mult)
                        dve.wait_ge(mm.sem, mm.at(g, u + 1))
                        apart(dve, k.passed)
                        V.tensor_copy(qm[0:BN, bass.ds(b, 1), 0:D], pq[u][0:BN, 0:D].unsqueeze(1)).then_inc(ev_q.sem, 1)

            @block.scalar
            def _(act):
                A = nc.scalar
                act.wait_ge(toact, 1)
                A.activation(n["nrm"][:, :], n["n2"][:, :], ACT.Sqrt)
                A.activation(cc["sq"][:, :], cc["ac"][:, :], ACT.Sqrt).then_inc(fract, 1)
                act.wait_ge(toact, 2)
                A.activation(n["th"][:, :], n["z"][:, :], ACT.Tanh)
                A.activation(n["sn"][:, :], n["zt"][:, :], ACT.Sin)
                A.activation(n["cs"][:, :], n["zc"][:, :], ACT.Sin).then_inc(fract, 1)
                with act.Fori(0, NBP // 2) as g:
                    for u in range(2):
                        act.wait_ge(mm.sem, mm.at(g, u + 1))
                        act.wait_ge(st[u].sem, st[u].at(g, 0))
                        A.copy(kmv[u][:, 0:D], pkv[u][0:BN, 0:D])
                        A.copy(kmv[u][:, 2 * D:3 * D], pkv[u][0:BN, D:2 * D]).then_inc(ev_kv.sem, 1)

            @block.tensor
            def _(pe):
                pe.wait_ge(vec, 1)
                with pe.Fori(0, NBP // 2) as g:
                    for u in range(2):
                        pe.wait_ge(xt_in[u].sem, xt_in[u].at(g, 16))
                        pe.wait_ge(ev_q.sem, ev_q.at(g, u - 1))
                        pe.wait_ge(ev_kv.sem, ev_kv.at(g, u - 1))
                        nc.tensor.matmul(pq[u][0:BN, :], xt[u][:, :], wqkv[:, 0, :], start=True, stop=True)
                        nc.tensor.matmul(pkv[u][0:BN, :], xt[u][:, :], wqkv[:, 1:3, :].rearrange("p a d -> p (a d)"),
                                         start=True, stop=True).then_inc(mm.sem, 1)


def load_steps(nc, k, eng, which, g, bound):
    _, vals = nc.values_load_multi_w_load_instructions(
        k.tile_block[which:which + 1, bass.ds(g * G, G)], engines=(eng,), min_val=0,
        max_val=bound - 1, skip_runtime_bounds_check_because="clamped where it is worked out")
    return vals


def edges0(nc, k):
    io, sz = k.io, k.sz
    NG, NBP = sz.ng, sz.nbp
    with ExitStack() as ctx:
        sb, pb, sem = stage(nc, ctx, "e0", k.retired)
        qm = k.big[:, 0:NBP * 256].rearrange("p (b c) -> p b c", c=256)
        raw = sb("raw", [P, G, 4], I32)
        feat = sb("feat", [R_ONE + 1, G, P])
        rows = sb("rows", [P, G, 3 * D])
        dl = sb("dl", [P, G])
        tyf = sb("tyf", [P, G])
        oh = sb("oh", [P, G, P], BF16)
        oht = [sb(f"oht{u}", [P, QS, P]) for u in range(2)]
        hid = sb("hid", [HID + 1, QS * P])
        d2 = sb("d2", [P, G])
        p_oht = pb("p_oht", [P, QS, P], BF16)
        p_q = [pb(f"p_q{u}", [P, QS, D]) for u in range(2)]
        p_d = [pb(f"p_d{u}", [P, QS, D]) for u in range(2)]
        p_t = pb("p_t", [P, QS, D])
        p_h = pb("p_h", [P, QS * P])
        p_e = pb("p_e", [P, G, H0])
        raw_in = [Mark(sem(f"raw_in{q}"), 16 * QS) for q in range(NQ)]
        feat_in = [Mark(sem(f"feat_in{q}"), 16 * QS) for q in range(NQ)]
        rows_in = [Mark(sem(f"rows_in{q}"), 16 * QS) for q in range(NQ)]
        value_out = [Mark(sem(f"value_out{q}"), 16, 16) for q in range(NQ)]
        scal = Mark(sem("scal"), 1, 1)
        ohs = Mark(sem("ohs"), NQ)
        oht_t = Mark(sem("oht_t"), NQ, NQ)
        oht_c = Mark(sem("oht_c"), NQ, NQ)
        tps = Mark(sem("tps"), NQ, NQ)
        keys = Mark(sem("keys"), NQ, NQ)
        summed = Mark(sem("summed"), NQ, NQ)
        qd = Mark(sem("qd"), NQ, NQ)
        qused = Mark(sem("qused"), NQ, NQ)
        dused = Mark(sem("dused"), NQ, NQ)
        hps = Mark(sem("hps"), NQ, NQ)
        hsb = Mark(sem("hsb"), NQ, NQ)
        eps = Mark(sem("eps"), NQ, NQ)
        edone = Mark(sem("edone"), 1, 1)
        dcopy = Mark(sem("dcopy"), 1, 1)
        featc = Mark(sem("featc"), NQ, NQ)
        vec = sem("vec")
        ones = sem("ones")
        PER = 7 + NQ * 3 + 1
        with nc.Block() as block:
            @block.sync
            def _(sp):
                for m in (*value_out, summed, scal, oht_t, oht_c, tps, keys, qd, qused, dused, hps, hsb, eps,
                          edone, dcopy, featc):
                    sp.sem_inc(m.sem, m.credit)
                sp.wait_ge(ones, 2)
                with sp.Fori(0, NG) as g:
                    tiles = load_steps(nc, k, ET.SP, 0, g, sz.tiles)
                    for q in range(NQ):
                        sp.wait_ge(keys.sem, keys.at(g, q + 1 - NQ))
                        apart(sp, k.passed)
                        sp.wait_ge(scal.sem, scal.at(g, 0))
                        apart(sp, k.passed)
                        for i in range(q * QS, q * QS + QS):
                            sp.dma_start(raw[:, i, :], io["edge_ids"][bass.ds(tiles[i] * P, P), :]).then_inc(raw_in[q].sem, 16)
                        sp.wait_ge(tps.sem, tps.at(g, 0))
                        sp.wait_ge(hps.sem, hps.at(g, 0))
                        apart(sp, k.passed)
                        for i in range(q * QS, q * QS + QS):
                            sp.dma_start(feat[0:R_ONE, i, :],
                                         io["edge_feat"][bass.ds(tiles[i], 1), :, :].rearrange("a r e -> (a r) e"))\
                                .then_inc(feat_in[q].sem, 16)

            @block.gpsimd
            def _(pl):
                nc.gpsimd.memset(feat[R_TYPE:R_ONE + 1, :, :], 1.0).then_inc(ones, 1)
                nc.gpsimd.memset(hid[HID:HID + 1, :], 1.0).then_inc(ones, 1)
                with pl.Fori(0, NG) as g:
                    for q in range(NQ):
                        pl.wait_ge(raw_in[q].sem, raw_in[q].at(g, 16 * QS))
                        pl.wait_ge(summed.sem, summed.at(g, q + 1 - NQ))
                        pl.wait_ge(qd.sem, qd.at(g, q + 1 - NQ))
                        pl.wait_ge(value_out[q].sem, value_out[q].at(g, 0))
                        apart(pl, k.passed)
                        for i in range(q * QS, q * QS + QS):
                            nc.gpsimd.indirect_dma_start(
                                rows[:, i, :], None, k.d_table0,
                                bass.IndirectOffsetOnAxis(ap=raw[:, i, 0:1], axis=0)).then_inc(rows_in[q].sem, 16)

            @block.vector
            def _(dve):
                V = nc.vector
                with dve.Fori(0, NG) as g:
                    v = Chain(dve, vec, g * PER)
                    s16 = bass.ds(g * G, G)
                    for q in range(NQ):
                        dve.wait_ge(raw_in[q].sem, raw_in[q].at(g, 16 * QS))
                    v.did(V.tensor_tensor(dl[:, :], raw[:, :, 1], k.blkf[:, s16], ALU.subtract))
                    v.did(V.tensor_copy(tyf[:, :], raw[:, :, 2]))
                    v.did(V.tensor_copy(k.dst[:, s16], raw[:, :, 1]))
                    v.did(V.tensor_copy(k.typ8[:, s16], raw[:, :, 3]))
                    v.did(V.tensor_copy(k.src[:, s16], raw[:, :, 0]))
                    v.settle()
                    dve.sem_inc(scal.sem, 1)
                    v.did(V.tensor_copy(k.dstl[:, s16], dl[:, :]))
                    v.did(V.tensor_copy(k.typ2[:, s16], tyf[:, :]))
                    dve.wait_ge(oht_t.sem, oht_t.at(g, 0))
                    for q in range(NQ):
                        i4 = slice(q * QS, q * QS + QS)
                        V.tensor_tensor(oh[:, i4, BN:P], bc(k.iota[:, 0:NT], 1, QS), bc(tyf[:, i4], 2, NT), ALU.is_equal)
                        for i in range(q * QS, q * QS + QS):
                            last = V.tensor_scalar(oh[:, i, 0:BN], k.iotab[:, 0:BN], dl[:, i:i + 1], None, ALU.is_equal)
                        last.then_inc(ohs.sem, 1)
                    for q in range(NQ):
                        i4 = slice(q * QS, q * QS + QS)
                        dve.wait_ge(rows_in[q].sem, rows_in[q].at(g, 16 * QS))
                        dve.wait_ge(tps.sem, tps.at(g, q + 1))
                        prod = rows[:, i4, 0:D]
                        v(V.tensor_tensor(prod, prod, p_t[:, :, :], ALU.add))
                        dve.sem_inc(keys.sem, 1)
                        dve.wait_ge(qd.sem, qd.at(g, q + 1))
                        v(V.tensor_tensor(prod, prod, p_q[q % 2][:, :, :], ALU.mult))
                        dve.sem_inc(qused.sem, 1)
                        v(V.tensor_reduce(
                            k.sco[:, bass.ds(g * (G * H0) + q * (QS * H0), QS * H0)],
                            prod.rearrange("p q (h d) -> p q h d", h=H0), AX.X, ALU.add))
                        dve.sem_inc(summed.sem, 1)
                    dve.wait_ge(dused.sem, dused.at(g, NQ))
                    apart(dve, k.passed)
                    v(V.tensor_copy(k.blkf[:, s16], d2[:, :]))
                    dve.sem_inc(dcopy.sem, 1)
                    assert v.n == PER, v.n

            @block.scalar
            def _(act):
                A = nc.scalar
                with act.Fori(0, NG) as g:
                    def features(q):
                        act.wait_ge(feat_in[q].sem, feat_in[q].at(g, 16 * QS))
                        f = feat[R_TYPE:R_TYPE + 1, q * QS:q * QS + QS, :]
                        A.copy(f, f.bitcast(I32)).then_inc(featc.sem, 1)

                    def onehot(q):
                        act.wait_ge(oht_t.sem, oht_t.at(g, q + 1))
                        act.wait_ge(qd.sem, qd.at(g, q - 1))
                        A.copy(oht[q % 2][:, :, :], p_oht[:, :, :]).then_inc(oht_c.sem, 1)

                    features(0)
                    onehot(0)
                    for q in range(NQ):
                        if q + 1 < NQ:
                            features(q + 1)
                            onehot(q + 1)
                        act.wait_ge(hps.sem, hps.at(g, q + 1))
                        act.wait_ge(eps.sem, eps.at(g, q))
                        A.activation(hid[0:HID, :], p_h[0:HID, :], ACT.Relu).then_inc(hsb.sem, 1)
                        act.wait_ge(qd.sem, qd.at(g, q + 1))
                        act.dma_start(k.d_value[bass.ds(g * NQ + q, 1), :, :, :].rearrange("a p q d -> (a p) q d"),
                                      rows[:, q * QS:q * QS + QS, 2 * D:3 * D]).then_inc(value_out[q].sem, 16)
                        if q == 0:
                            act.wait_ge(dcopy.sem, dcopy.at(g, 0))
                        for i in range(QS):
                            j = q * QS + i
                            last = A.activation(p_d[q % 2][:, i, :], p_d[q % 2][:, i, :], ACT.Square, accum_out=d2[:, j:j + 1])
                        last.then_inc(dused.sem, 1)
                    act.wait_ge(eps.sem, eps.at(g, NQ))
                    A.activation(k.exs[:, bass.ds(g * (G * H0), G * H0)], p_e[:, :, :].rearrange("p g h -> p (g h)"),
                                 ACT.Tanh).then_inc(edone.sem, 1)
                for q in range(NQ):
                    act.wait_ge(value_out[q].sem, 16 + 16 * NG)

            @block.tensor
            def _(pe):
                M = nc.tensor.matmul
                with pe.Fori(0, NG) as g:
                    blocks = load_steps(nc, k, ET.PE, 1, g, sz.nb)

                    def transposes(q):
                        pe.wait_ge(ohs.sem, ohs.at(g, q + 1))
                        pe.wait_ge(oht_c.sem, oht_c.at(g, q))
                        for i in range(QS):
                            last = nc.tensor.transpose(p_oht[:, i, :], oh[:, q * QS + i, :], k.idenb[:, :])
                        last.then_inc(oht_t.sem, 1)

                    transposes(0)
                    for q in range(NQ):
                        pe.wait_ge(featc.sem, featc.at(g, q + 1))
                        pe.wait_ge(keys.sem, keys.at(g, q))
                        for i in range(QS):
                            last = M(p_t[:, i, :], feat[:, q * QS + i, :], k.wedge[:, :], start=True, stop=True)
                        last.then_inc(tps.sem, 1)
                        pe.wait_ge(hsb.sem, hsb.at(g, q))
                        M(p_h[0:HID, :], k.wdec1[R_TYPE:R_ONE + 1, :],
                          feat[R_TYPE:R_ONE + 1, q * QS:q * QS + QS, :].rearrange("p q e -> p (q e)"),
                          start=True, stop=True).then_inc(hps.sem, 1)
                        if q + 1 < NQ:
                            transposes(q + 1)
                        pe.wait_ge(oht_c.sem, oht_c.at(g, q + 1))
                        pe.wait_ge(rows_in[q].sem, rows_in[q].at(g, 16 * QS))
                        pe.wait_ge(qused.sem, qused.at(g, q - 1))
                        pe.wait_ge(dused.sem, dused.at(g, q - 1))
                        for i in range(QS):
                            j = q * QS + i
                            M(p_q[q % 2][:, i, :], oht[q % 2][:, i, :], qm[:, bass.ds(blocks[j], 1), 0:D],
                              start=True, stop=True)
                            M(p_d[q % 2][:, i, :], oht[q % 2][:, i, :], qm[:, bass.ds(blocks[j], 1), D:2 * D],
                              start=True, stop=False)
                            last = M(p_d[q % 2][:, i, :], k.iden[:, :], rows[:, j, D:2 * D], start=False, stop=True)
                        last.then_inc(qd.sem, 1)
                        pe.wait_ge(hsb.sem, hsb.at(g, q + 1))
                        if q == 0:
                            pe.wait_ge(edone.sem, edone.at(g, 0))
                        for i in range(QS):
                            last = M(p_e[:, q * QS + i, :], hid[:, i * P:(i + 1) * P], k.wdec2[:, :], start=True, stop=True)
                        last.then_inc(eps.sem, 1)


def scores0(nc, k):
    S = k.sz.steps
    with ExitStack() as ctx:
        sb, pb, sem = stage(nc, ctx, "s0")
        dist = sb("dist", [P, S])
        d2 = k.blkf
        vec, ready, fract = sem("vec"), sem("ready"), sem("fract")
        sco = k.sco[:, :].rearrange("p (s h) -> p s h", h=H0)
        exs = k.exs[:, :].rearrange("p (s h) -> p s h", h=H0)
        with nc.Block() as block:
            @block.scalar
            def _(act):
                nc.scalar.activation(dist[:, :], d2[:, :], ACT.Sqrt).then_inc(fract, 1)
                act.wait_ge(ready, 1)
                nc.scalar.activation(k.exs[:, :], k.exs[:, :], ACT.Exp).then_inc(fract, 1)

            @block.vector
            def _(dve):
                V = nc.vector
                v = Chain(dve, vec)
                V.tensor_tensor(exs, exs, bc(k.heads[:, 0, :], 1, S), ALU.mult).then_inc(ready, 1)
                dve.wait_ge(fract, 1)
                for h in range(H0):
                    v.did(V.scalar_tensor_tensor(sco[:, :, h], dist[:, :], k.heads[:, 1, h:h + 1], sco[:, :, h],
                                                 ALU.mult, ALU.add))
                v.settle()
                dve.wait_ge(fract, 2)
                v(V.tensor_tensor(k.sco[:, :], k.sco[:, :], k.exs[:, :], ALU.mult))


def segment_max(nc, k, H, tag):
    sz = k.sz
    S, NG = sz.steps, sz.ng
    R = G * H
    with ExitStack() as ctx:
        sb, pb, sem = stage(nc, ctx, f"mx{tag}")
        sco = k.sco[:, :].rearrange("p (g c) -> p g c", c=P)
        exs = k.exs[:, :].rearrange("p (g c) -> p g c", c=P)
        lt = k.exs[0:R, :].rearrange("p (g c) -> p g c", c=P)
        mloc = k.sco[0:R, :].rearrange("p (g c) -> p g c", c=P)
        zn = k.big[0:R, 0:NG * P].rearrange("p (g c) -> p g c", c=P)
        cut = Carve(k.big, NG * P)
        pen = cut([P, S])
        pen2 = cut([P, S])
        li = [sb(f"li{u}", [P, R]) for u in range(2)]
        zi = [sb(f"zi{u}", [P, R]) for u in range(2)]
        diff = [sb(f"diff{u}", [R, P + 1]) for u in range(2)]
        fwd = [sb(f"fwd{u}", [R, P]) for u in range(2)]
        bwd = [sb(f"bwd{u}", [R, P]) for u in range(2)]
        four = sb("four", [R, 4, NG])
        turned = sb("turned", [NG, 4, R])
        line = cut([H, 4, S])
        join = cut([H, S + 1])
        through = cut([H, S])
        gate = cut([H, S + 1])
        run = cut([H, 2, S])
        carry = cut([H, 2, S])
        carry_g = sb("carry_g", [NG, 2, R])
        carry_t = sb("carry_t", [R, 2, NG])
        pl_ = [pb(f"pl{u}", [P, P]) for u in range(2)]
        pz_ = [pb(f"pz{u}", [P, P]) for u in range(2)]
        pf = [pb(f"pf{u}", [P, 4 * P]) for u in range(2)]
        vec = sem("vec")
        tin, tout, tcopy = Mark(sem("tin"), 2, 2), Mark(sem("tout"), 2, 2), Mark(sem("tcopy"), 2, 2)
        PER = 2 * 4
        with nc.Block() as block:
            @block.sync
            def _(sp):
                for m in (tin, tout, tcopy):
                    sp.sem_inc(m.sem, m.credit)

            @block.vector
            def _(dve):
                V = nc.vector
                v = Chain(dve, vec)
                v(V.tensor_scalar(pen[:, :], k.dstl[:, :], 0.0, None, ALU.is_ge))
                v(V.tensor_scalar(pen2[:, :], k.dstl[:, :], float(BN), None, ALU.is_lt))
                v(V.tensor_tensor(pen[:, :], pen[:, :], pen2[:, :], ALU.mult))
                v(V.tensor_scalar(pen[:, :], pen[:, :], 1.0, BIG, ALU.subtract, ALU.mult))
                for u in range(2):
                    v(V.memset(diff[u][:, :], -BIG))
                base = v.n
                with dve.Fori(0, NG // 2) as gg:
                    v = Chain(dve, vec, gg * PER + base)
                    for u in range(2):
                        g = gg * 2 + u
                        s16 = bass.ds(g * G, G)
                        dve.wait_ge(tout.sem, tout.at(gg, u - 1))
                        V.tensor_tensor(li[u][:, :].rearrange("p (t h) -> p t h", h=H),
                                        sco[:, bass.ds(g, 1), 0:R].rearrange("p a (t h) -> p (a t) h", h=H),
                                        bc(pen[:, s16], 2, H), ALU.add)
                        V.tensor_scalar(zi[u][:, :].rearrange("p (t h) -> p t h", h=H),
                                        bc(k.dst[:, s16], 2, H), -BIG, None, ALU.mult).then_inc(tin.sem, 1)
                    for u in range(2):
                        g = gg * 2 + u
                        dve.wait_ge(tcopy.sem, tcopy.at(gg, u + 1))
                        z = zn[:, bass.ds(g, 1), :].rearrange("p a c -> p (a c)")
                        v(V.tensor_tensor(diff[u][:, 1:P], z[:, 1:P], z[:, 0:P - 1], ALU.subtract))
                        v(V.tensor_tensor_scan(fwd[u][:, :], diff[u][:, 0:P],
                                               lt[:, bass.ds(g, 1), :].rearrange("p a c -> p (a c)"),
                                               -3 * BIG, ALU.add, ALU.max))
                        v(V.tensor_tensor_scan(bwd[u][:, ::-1], diff[u][:, 1:P + 1][:, ::-1], fwd[u][:, ::-1],
                                               -3 * BIG, ALU.add, ALU.max))
                        v(V.tensor_scalar(mloc[:, bass.ds(g, 1), :].rearrange("p a c -> p (a c)"), bwd[u][:, :],
                                          0.0, None, ALU.add))
                    assert v.n == PER

            @block.tensor
            def _(pe):
                with pe.Fori(0, NG // 2) as gg:
                    for u in range(2):
                        pe.wait_ge(tin.sem, tin.at(gg, u + 1))
                        pe.wait_ge(tcopy.sem, tcopy.at(gg, u - 1))
                        apart(pe, k.passed)
                        nc.tensor.transpose(pl_[u][0:R, :], li[u][:, :], k.iden[:, :])
                        nc.tensor.transpose(pz_[u][0:R, :], zi[u][:, :], k.iden[:, :]).then_inc(tout.sem, 1)

            @block.scalar
            def _(act):
                with act.Fori(0, NG // 2) as gg:
                    for u in range(2):
                        g = gg * 2 + u
                        act.wait_ge(tout.sem, tout.at(gg, u + 1))
                        nc.scalar.copy(lt[:, bass.ds(g, 1), :].rearrange("p a c -> p (a c)"), pl_[u][0:R, :])
                        nc.scalar.copy(zn[:, bass.ds(g, 1), :].rearrange("p a c -> p (a c)"), pz_[u][0:R, :])\
                            .then_inc(tcopy.sem, 1)

        vec2, pes, lined, carried = sem("vec2"), sem("pes"), sem("lined"), sem("carried")
        HG = G // 2 * NG
        with nc.Block() as block:
            @block.vector
            def _(dve):
                V = nc.vector
                v = Chain(dve, vec2)
                v(V.tensor_copy(four[:, 0, :], mloc[:, :, 0]))
                v(V.tensor_copy(four[:, 1, :], mloc[:, :, P - 1]))
                v(V.tensor_copy(four[:, 2, :], zn[:, :, 0]))
                v(V.tensor_copy(four[:, 3, :], zn[:, :, P - 1]))
                dve.wait_ge(pes, 1)
                v(V.tensor_copy(turned[:, :, :].rearrange("p a r -> p (a r)"), pf[0][0:NG, 0:4 * R]))
                for a in range(4):
                    for half in range(2):
                        dve.wait_ge(pes, 2 + 2 * a + half)
                        t0 = half * (G // 2)
                        v(V.tensor_copy(line[:, a, :].rearrange("h (g t) -> h t g", t=G)[:, t0:t0 + G // 2, :],
                                        pf[half][0:H, 0:HG].rearrange("h (t g) -> h t g", g=NG)))
                v(V.memset(join[:, :], -BIG))
                v(V.tensor_tensor(join[:, 1:S], line[:, 2, 1:S], line[:, 3, 0:S - 1], ALU.not_equal))
                v(V.tensor_scalar(join[:, 1:S], join[:, 1:S], -BIG, None, ALU.mult))
                v(V.tensor_tensor(through[:, :], line[:, 2, :], line[:, 3, :], ALU.not_equal))
                v(V.tensor_scalar(through[:, :], through[:, :], -BIG, None, ALU.mult))
                v(V.tensor_tensor(gate[:, 0:S], join[:, 0:S], through[:, :], ALU.add))
                v(V.tensor_tensor_scan(run[:, 0, :], gate[:, 0:S], line[:, 1, :], -3 * BIG, ALU.add, ALU.max))
                v(V.tensor_tensor(gate[:, 0:S], join[:, 1:S + 1], through[:, :], ALU.add))
                v(V.tensor_tensor_scan(run[:, 1, ::-1], gate[:, 0:S][:, ::-1], line[:, 0, ::-1], -3 * BIG,
                                       ALU.add, ALU.max))
                v(V.memset(carry[:, :, :], -BIG))
                v(V.tensor_tensor(carry[:, 0, 1:S], run[:, 0, 0:S - 1], join[:, 1:S], ALU.add))
                v(V.tensor_tensor(carry[:, 1, 0:S - 1], run[:, 1, 1:S], join[:, 1:S], ALU.add))
                dve.sem_inc(carried, 1)
                dve.wait_ge(pes, 10)
                v(V.tensor_copy(carry_g[:, :, :].rearrange("p a r -> p (a r)"), pf[0][0:NG, 0:2 * R]))
                dve.sem_inc(carried, 1)
                dve.wait_ge(pes, 11)
                v(V.tensor_copy(carry_t[:, :, :].rearrange("p a g -> p (a g)"), pf[1][0:R, 0:2 * NG]))

            @block.tensor
            def _(pe):
                T = nc.tensor.transpose
                pe.wait_ge(vec2, 4)
                for a in range(4):
                    last = T(pf[0][0:NG, a * R:(a + 1) * R], four[:, a, :], k.iden[0:R, 0:R])
                last.then_inc(pes, 1)
                pe.wait_ge(vec2, 5)
                for a in range(4):
                    for half in range(2):
                        n = 2 * a + half
                        if n >= 2:
                            pe.wait_ge(vec2, 5 + n - 1)
                        for t in range(G // 2):
                            tt = half * (G // 2) + t
                            last = T(pf[half][0:H, t * NG:(t + 1) * NG], turned[:, a, tt * H:(tt + 1) * H],
                                     k.iden[0:NG, 0:NG])
                        last.then_inc(pes, 1)
                pe.wait_ge(carried, 1)
                for a in range(2):
                    for t in range(G):
                        last = T(pf[0][0:NG, a * R + t * H:a * R + (t + 1) * H],
                                 carry[:, a, :].rearrange("h (g t) -> h t g", t=G)[:, t, :], k.iden[0:H, 0:H])
                last.then_inc(pes, 1)
                pe.wait_ge(carried, 2)
                for a in range(2):
                    last = T(pf[1][0:R, a * NG:(a + 1) * NG], carry_g[:, a, :], k.iden[0:NG, 0:NG])
                last.then_inc(pes, 1)

        vec3 = sem("vec3")
        xin, ex, xt, xc = (Mark(sem(m), 2, 2) for m in ("xin", "ex", "xt", "xc"))
        PER3 = 2 * 4
        xz = [sb(f"xz{u}", [R, P]) for u in range(2)]
        ez = [sb(f"ez{u}", [R, P]) for u in range(2)]
        with nc.Block() as block:
            @block.sync
            def _(sp):
                for m in (xin, ex, xt, xc):
                    sp.sem_inc(m.sem, m.credit)

            @block.vector
            def _(dve):
                V = nc.vector
                with dve.Fori(0, NG // 2) as gg:
                    v = Chain(dve, vec3, gg * PER3)
                    for u in range(2):
                        g = gg * 2 + u
                        g1 = bass.ds(g, 1)
                        z = zn[:, g1, :].rearrange("p a c -> p (a c)")
                        m = mloc[:, g1, :].rearrange("p a c -> p (a c)")
                        first, lastd = four[:, 2, g1], four[:, 3, g1]
                        v.did(V.tensor_scalar(fwd[u][:, :], z, first, carry_t[:, 0, g1], ALU.subtract, ALU.add))
                        v.did(V.tensor_scalar(diff[u][:, 0:P], z, lastd, -1.0, ALU.subtract, ALU.mult))
                        v.settle()
                        v(V.tensor_tensor(fwd[u][:, :], fwd[u][:, :], m, ALU.max))
                        v(V.scalar_tensor_tensor(fwd[u][:, :], diff[u][:, 0:P], carry_t[:, 1, g1], fwd[u][:, :],
                                                 ALU.add, ALU.max))
                        dve.wait_ge(ex.sem, ex.at(gg, u - 1))
                        V.tensor_tensor(xz[u][:, :],
                                        lt[:, g1, :].rearrange("p a c -> p (a c)"), fwd[u][:, :],
                                        ALU.subtract).then_inc(xin.sem, 1)
                    assert v.n == PER3

            @block.scalar
            def _(act):
                with act.Fori(0, NG // 2) as gg:
                    for u in range(2):
                        g = gg * 2 + u
                        act.wait_ge(xin.sem, xin.at(gg, u + 1))
                        act.wait_ge(xt.sem, xt.at(gg, u - 1))
                        nc.scalar.activation(ez[u][:, :], xz[u][:, :], ACT.Exp).then_inc(ex.sem, 1)
                    for u in range(2):
                        g = gg * 2 + u
                        act.wait_ge(xt.sem, xt.at(gg, u + 1))
                        nc.scalar.copy(exs[:, bass.ds(g, 1), 0:R].rearrange("p a c -> p (a c)"), pl_[u][:, 0:R])\
                            .then_inc(xc.sem, 1)

            @block.tensor
            def _(pe):
                with pe.Fori(0, NG // 2) as gg:
                    for u in range(2):
                        pe.wait_ge(ex.sem, ex.at(gg, u + 1))
                        pe.wait_ge(xc.sem, xc.at(gg, u - 1))
                        apart(pe, k.passed)
                        nc.tensor.transpose(pl_[u][:, 0:R], ez[u][:, :], k.iden[0:R, 0:R]).then_inc(xt.sem, 1)


def weighted_sums(nc, k, H, W, tag):
    sz = k.sz
    NG, NBP, S = sz.ng, sz.nbp, sz.steps
    typed = W > D + H
    with ExitStack() as ctx:
        sb, pb, sem = stage(nc, ctx, f"ws{tag}")
        acc = k.big[0:BN, 0:NBP * W].rearrange("p (b c) -> p b c", c=W)
        exs = k.exs[:, :].rearrange("p (g c) -> p g c", c=P)
        val = sb("val", [P, G, D])
        wv = sb("wv", [P, G, W])
        oh = sb("oh", [P, G, BN])
        dl = sb("dl", [P, G])
        pr = [pb(f"pr{i}", [P, 2, 256]) for i in range(8)]
        val_in = [Mark(sem(f"val_in{q}"), 16) for q in range(NQ)]
        scaled = Mark(sem("scaled"), NQ, NQ)
        extra = Mark(sem("extra"), NQ, NQ)
        ohs = Mark(sem("ohs"), NQ, NQ)
        prod = Mark(sem("prod"), NQ, NQ)
        added = Mark(sem("added"), NQ, NQ)
        vec = sem("vec")
        PER = 1 + G
        with nc.Block() as block:
            @block.sync
            def _(sp):
                for m in (scaled, extra, ohs, prod, added):
                    sp.sem_inc(m.sem, m.credit)
                with sp.Fori(0, NG) as g:
                    for q in range(NQ):
                        sp.wait_ge(scaled.sem, scaled.at(g, q + 1 - NQ))
                        sp.dma_start(val[:, q * QS:q * QS + QS, :],
                                     k.d_value[bass.ds(g * NQ + q, 1), :, :, :].rearrange("a p q d -> (a p) q d"))\
                            .then_inc(val_in[q].sem, 16)

            @block.gpsimd
            def _(pl):
                with pl.Fori(0, NG) as g:
                    for q in range(NQ):
                        i4 = slice(q * QS, q * QS + QS)
                        e = exs[:, bass.ds(g, 1), q * QS * H:(q + 1) * QS * H].rearrange("p a (t h) -> p (a t) h", h=H)
                        pl.wait_ge(val_in[q].sem, val_in[q].at(g, 16))
                        pl.wait_ge(prod.sem, prod.at(g, q + 1 - NQ))
                        nc.gpsimd.tensor_tensor(
                            wv[:, i4, 0:D].rearrange("p t (h d) -> p t h d", h=H),
                            val[:, i4, :].rearrange("p t (h d) -> p t h d", h=H), bc(e, 3, D // H), ALU.mult)\
                            .then_inc(scaled.sem, 1)

            @block.scalar
            def _(act):
                with act.Fori(0, NG) as g:
                    for q in range(NQ):
                        i4 = slice(q * QS, q * QS + QS)
                        e = exs[:, bass.ds(g, 1), q * QS * H:(q + 1) * QS * H].rearrange("p a (t h) -> p (a t) h", h=H)
                        act.wait_ge(prod.sem, prod.at(g, q + 1 - NQ))
                        nc.scalar.copy(wv[:, i4, D:D + H], e).then_inc(extra.sem, 1)

            @block.vector
            def _(dve):
                V = nc.vector
                v = Chain(dve, vec)
                v(V.memset(acc, 0.0))
                with dve.Fori(0, NG) as g:
                    v = Chain(dve, vec, g * PER + 1)
                    blocks = load_steps(nc, k, ET.DVE, 1, g, sz.nb)
                    v(V.tensor_copy(dl[:, :], k.dstl[:, bass.ds(g * G, G)]))

                    def onehot(q):
                        i4 = slice(q * QS, q * QS + QS)
                        dve.wait_ge(prod.sem, prod.at(g, q + 1 - NQ))
                        if typed:
                            e = exs[:, bass.ds(g, 1), q * QS * H:(q + 1) * QS * H].rearrange("p a (t h) -> p (a t) h", h=H)
                            V.tensor_tensor(wv[:, i4, D + H:W], e, bc(k.typ2[:, bass.ds(g * G + q * QS, QS)], 2, H), ALU.mult)
                        for i in range(q * QS, q * QS + QS):
                            last = V.tensor_scalar(oh[:, i, :], k.iota[:, 0:BN], dl[:, i:i + 1], None, ALU.is_equal)
                        last.then_inc(ohs.sem, 1)

                    onehot(0)
                    for q in range(NQ):
                        if q + 1 < NQ:
                            onehot(q + 1)
                        dve.wait_ge(prod.sem, prod.at(g, q + 1))
                        for i in range(q * QS, q * QS + QS):
                            a = acc[:, bass.ds(blocks[i], 1), :]
                            v(V.tensor_tensor(a, a, pr[i // 2][0:BN, i % 2, 0:W].unsqueeze(1), ALU.add))
                        dve.sem_inc(added.sem, 1)
                    assert v.n == PER

            @block.tensor
            def _(pe):
                with pe.Fori(0, NG) as g:
                    for q in range(NQ):
                        pe.wait_ge(scaled.sem, scaled.at(g, q + 1))
                        pe.wait_ge(extra.sem, extra.at(g, q + 1))
                        pe.wait_ge(ohs.sem, ohs.at(g, q + 1))
                        pe.wait_ge(added.sem, added.at(g, q + 1 - NQ))
                        for i in range(q * QS, q * QS + QS):
                            last = nc.tensor.matmul(pr[i // 2][0:BN, i % 2, 0:W], oh[:, i, :], wv[:, i, :],
                                                    start=True, stop=True)
                        last.then_inc(prod.sem, 1)


def moments(V, v, st, mu, var, tmp):
    v(V.tensor_tensor(mu, st[:, :, 1], st[:, :, 4], ALU.add))
    v(V.tensor_tensor(tmp, st[:, :, 1], st[:, :, 4], ALU.subtract))
    v(V.tensor_tensor(tmp, tmp, tmp, ALU.mult))
    v(V.tensor_tensor(var, st[:, :, 2], st[:, :, 5], ALU.add))
    v(V.tensor_scalar(mu, mu, 0.5, None, ALU.mult))
    v(V.tensor_scalar(var, var, 1.0 / D, 1e-5, ALU.mult, ALU.add))
    v(V.scalar_tensor_tensor(var, tmp, 0.25, var, ALU.mult, ALU.add))


def inverse_deviation(nc, k, sb, sem, st, tag):
    NBP = k.sz.nbp
    mu, rs, tmp = sb(f"mu{tag}", [BN, NBP]), sb(f"rs{tag}", [BN, NBP]), sb(f"dev{tag}", [BN, NBP])
    vec, root, var_ready = sem(f"dev_vec{tag}"), sem(f"dev_root{tag}"), sem(f"dev_var{tag}")
    with nc.Block() as block:
        @block.vector
        def _(dve):
            v = Chain(dve, vec)
            moments(nc.vector, v, st, mu[:, :], rs[:, :], tmp[:, :])
            dve.sem_inc(var_ready, 1)
            dve.wait_ge(root, 1)
            v(nc.vector.reciprocal(rs[:, :], tmp[:, :]))

        @block.scalar
        def _(act):
            act.wait_ge(var_ready, 1)
            nc.scalar.activation(tmp[:, :], rs[:, :], ACT.Sqrt).then_inc(root, 1)
    return mu, rs


def one(ap):
    return ap.rearrange("p a d -> p (a d)")


def nodes0(nc, k):
    io, sz = k.io, k.sz
    NBP = sz.nbp
    W = D + 2 * H0
    NI = NBP // 2
    with ExitStack() as ctx:
        sb, pb, sem = stage(nc, ctx, "n0")
        acc = k.big[0:BN, 0:NBP * W].rearrange("p (b c) -> p b c", c=W)
        num = acc[:, :, 0:D]
        y = Carve(k.pair)([BN, NBP, D])
        hh = num
        st = sb("st", [BN, NBP, 6])
        rd = sb("rd", [BN, NBP, H0])
        a0 = sb("a0", [BN, NBP, H0])
        a1 = sb("a1", [BN, NBP, H0])
        rv = sb("rv", [BN, 2, D])
        rows_ = {m: sb(m, [BN, D]) for m in ("bo", "g1", "be1", "bf2", "g2", "be2", "bs", "bd")}
        wo = sb("wo", [P, D])
        wf1 = sb("wf1", [P, FF])
        wf2 = sb("wf2", [P, FF // P, D])
        bf1 = sb("bf1", [P, FF // P])
        wsd = sb("wsd", [P, 2, D])
        xb = [sb(f"xb{u}", [BN, D]) for u in range(2)]
        ag = [sb(f"ag{u}", [BN, D]) for u in range(2)]
        agt = [sb(f"agt{u}", [P, BN]) for u in range(2)]
        tmp = [sb(f"tmp{u}", [BN, D]) for u in range(2)]
        gl = [sb(f"gl{u}", [P, FF // P, BN]) for u in range(2)]
        p_t = [pb(f"p_t{u}", [P, P]) for u in range(2)]
        p_m = [pb(f"p_m{u}", [P, 256]) for u in range(2)]
        p_f = [pb(f"p_f{u}", [P, FF // P, BN]) for u in range(2)]
        t16 = y
        loaded, vec = sem("loaded"), sem("vec")
        loads = [(rows_["bo"], "bo"), (rows_["g1"], "g1"), (rows_["be1"], "be1"), (rows_["bf2"], "bf2"),
                 (rows_["g2"], "g2"), (rows_["be2"], "be2")]

        with nc.Block() as block:
            @block.sync
            def _(sp):
                n = 0
                for dst, name in loads:
                    sp.dma_start(dst[:, :], io["L0_gnn_" + name].partition_broadcast(BN)).then_inc(loaded, 16)
                sp.dma_start(rows_["bs"][:, :], io["L1_gnn_b_src"].partition_broadcast(BN)).then_inc(loaded, 16)
                sp.dma_start(rows_["bd"][:, :], io["L1_gnn_b_dst"].partition_broadcast(BN)).then_inc(loaded, 16)
                sp.dma_start(rv[:, :, :], io["L0_gnn_rel_v"].partition_broadcast(BN)).then_inc(loaded, 16)
                sp.dma_start(wo[:, :], io["L0_gnn_Wo"]).then_inc(loaded, 16)
                sp.dma_start(wf1[:, :], io["L0_gnn_Wf1"]).then_inc(loaded, 16)
                sp.dma_start(wf2[:, :, :], io["L0_gnn_Wf2"].rearrange("(c p) n -> p c n", p=P)).then_inc(loaded, 16)
                sp.dma_start(bf1[:, :], io["L0_gnn_bf1"].rearrange("(c p) -> p c", p=P),
                             allow_slow_non_contiguous=True).then_inc(loaded, 16)
                sp.dma_start(wsd[:, 0, :], io["L1_gnn_W_src"]).then_inc(loaded, 16)
                sp.dma_start(wsd[:, 1, :], io["L1_gnn_W_dst"]).then_inc(loaded, 16)
                sp.wait_ge(loaded, 16 * 15)

            @block.vector
            def _(dve):
                V = nc.vector
                v = Chain(dve, vec)
                den, dent = acc[:, :, D:D + H0], acc[:, :, D + H0:W]
                v(V.tensor_scalar(rd[:, :, :], den, 1e-30, None, ALU.max))
                v(V.reciprocal(rd[:, :, :], rd[:, :, :]))
                v(V.tensor_tensor(a0[:, :, :], den, dent, ALU.subtract))
                v(V.tensor_tensor(a0[:, :, :], a0[:, :, :], rd[:, :, :], ALU.mult))
                v(V.tensor_tensor(a1[:, :, :], dent, rd[:, :, :], ALU.mult))
                dve.wait_ge(loaded, 16 * 15)
                hv = "p b (h d) -> p b h d"
                nv = num.rearrange(hv, h=H0)
                v(V.tensor_tensor(nv, nv, bc(rd[:, :, :], 3, D // H0), ALU.mult))
                for a, r in ((a0, 0), (a1, 1)):
                    rr = bc(rv[:, r, :].rearrange("p (h d) -> p h d", h=H0), 1, NBP)
                    v(V.tensor_tensor(t16[:, :, :].rearrange(hv, h=H0), bc(a[:, :, :], 3, D // H0), rr, ALU.mult))
                    v(V.tensor_tensor(num, num, t16[:, :, :], ALU.add))

        xin = [Mark(sem(f"xin{u}"), 16) for u in range(2)]
        agc, tr, trc, mm, ev, used = (Mark(sem(m), 2, 2) for m in ("agc", "tr", "trc", "mm", "ev", "used"))
        vec1 = sem("vec1")
        with nc.Block() as block:
            @block.sync
            def _(sp):
                for m in (agc, tr, trc, mm, ev):
                    sp.sem_inc(m.sem, m.credit)
                with sp.Fori(0, NI) as g:
                    for u in range(2):
                        sp.wait_ge(ev.sem, ev.at(g, u - 1))
                        sp.dma_start(xb[u][:, :], io["x"][bass.ds(g * (2 * BN) + u * BN, BN), :]).then_inc(xin[u].sem, 16)

            @block.gpsimd
            def _(pl):
                with pl.Fori(0, NI) as g:
                    for u in range(2):
                        pl.wait_ge(tr.sem, tr.at(g, u - 1))
                        nc.gpsimd.tensor_copy(ag[u][:, :].unsqueeze(1), num[:, bass.ds(g * 2 + u, 1), :]).then_inc(agc.sem, 1)

            @block.scalar
            def _(act):
                with act.Fori(0, NI) as g:
                    for u in range(2):
                        act.wait_ge(tr.sem, tr.at(g, u + 1))
                        act.wait_ge(mm.sem, mm.at(g, u - 1))
                        nc.scalar.copy(agt[u][:, :], p_t[u][:, 0:BN]).then_inc(trc.sem, 1)

            @block.tensor
            def _(pe):
                with pe.Fori(0, NI) as g:
                    for u in range(2):
                        pe.wait_ge(agc.sem, agc.at(g, u + 1))
                        pe.wait_ge(trc.sem, trc.at(g, u - 1))
                        nc.tensor.transpose(p_t[u][:, 0:BN], ag[u][:, :], k.iden[0:BN, 0:BN]).then_inc(tr.sem, 1)
                    for u in range(2):
                        pe.wait_ge(trc.sem, trc.at(g, u + 1))
                        pe.wait_ge(ev.sem, ev.at(g, u - 1))
                        nc.tensor.matmul(p_m[u][0:BN, 0:D], agt[u][:, :], wo[:, :], start=True, stop=True).then_inc(mm.sem, 1)

            @block.vector
            def _(dve):
                V = nc.vector
                PER = 6
                with dve.Fori(0, NI) as g:
                    v = Chain(dve, vec1, g * PER)
                    for u in range(2):
                        yb = y[:, bass.ds(g * 2 + u, 1), :]
                        dve.wait_ge(xin[u].sem, xin[u].at(g, 16))
                        v(V.tensor_tensor(tmp[u][:, :], xb[u][:, :], rows_["bo"][:, :], ALU.add))
                        dve.wait_ge(mm.sem, mm.at(g, u + 1))
                        v(V.tensor_tensor(yb, tmp[u][:, :].unsqueeze(1), p_m[u][0:BN, 0:D].unsqueeze(1), ALU.add))
                        dve.sem_inc(ev.sem, 1)
                        v(V.bn_stats(st[:, bass.ds(g * 2 + u, 1), :].rearrange("p a s -> p (a s)"), one(yb)))
                    assert v.n == PER

        mu, rs = inverse_deviation(nc, k, sb, sem, st, "1")

        hb, htr, htc, f1, ge, f2, ev2 = (Mark(sem(m), 2, 2) for m in ("hb", "htr", "htc", "f1", "ge", "f2", "ev2"))
        vec2 = sem("vec2")
        with nc.Block() as block:
            @block.sync
            def _(sp):
                for m in (hb, htr, htc, f1, ge, f2, ev2):
                    sp.sem_inc(m.sem, m.credit)

            @block.vector
            def _(dve):
                V = nc.vector
                PER = 2 * 6
                with dve.Fori(0, NI) as g:
                    v = Chain(dve, vec2, g * PER)
                    for u in range(2):
                        b1 = bass.ds(g * 2 + u, 1)
                        dve.wait_ge(htr.sem, htr.at(g, u - 1))
                        v(V.tensor_scalar(tmp[u][:, :], one(y[:, b1, :]), mu[:, b1], rs[:, b1], ALU.subtract, ALU.mult))
                        v(V.tensor_tensor(tmp[u][:, :], tmp[u][:, :], rows_["g1"][:, :], ALU.mult))
                        v(V.tensor_tensor(ag[u][:, :], tmp[u][:, :], rows_["be1"][:, :], ALU.add))
                        dve.sem_inc(hb.sem, 1)
                        V.tensor_tensor(hh[:, b1, :], ag[u][:, :].unsqueeze(1), rows_["bf2"][:, :].unsqueeze(1), ALU.add)                            .then_inc(vec2, 1)
                        v.n += 1
                    for u in range(2):
                        b1 = bass.ds(g * 2 + u, 1)
                        dve.wait_ge(f2.sem, f2.at(g, u + 1))
                        v.settle()
                        v(V.tensor_tensor(y[:, b1, :], hh[:, b1, :], p_m[u][0:BN, 0:D].unsqueeze(1), ALU.add))
                        dve.sem_inc(ev2.sem, 1)
                        v(V.bn_stats(st[:, b1, :].rearrange("p a s -> p (a s)"), one(y[:, b1, :])))
                    assert v.n == PER, v.n

            @block.scalar
            def _(act):
                with act.Fori(0, NI) as g:
                    for u in range(2):
                        act.wait_ge(htr.sem, htr.at(g, u + 1))
                        act.wait_ge(f1.sem, f1.at(g, u - 1))
                        nc.scalar.copy(agt[u][:, :], p_t[u][:, 0:BN]).then_inc(htc.sem, 1)
                    for u in range(2):
                        act.wait_ge(f1.sem, f1.at(g, u + 1))
                        act.wait_ge(f2.sem, f2.at(g, u - 1))
                        for c in range(FF // P):
                            last = nc.scalar.activation(gl[u][:, c, :], p_f[u][:, c, :], ACT.Gelu, bias=bf1[:, c:c + 1])
                        last.then_inc(ge.sem, 1)

            @block.tensor
            def _(pe):
                M = nc.tensor.matmul
                with pe.Fori(0, NI) as g:
                    for u in range(2):
                        pe.wait_ge(hb.sem, hb.at(g, u + 1))
                        pe.wait_ge(htc.sem, htc.at(g, u - 1))
                        nc.tensor.transpose(p_t[u][:, 0:BN], ag[u][:, :], k.iden[0:BN, 0:BN]).then_inc(htr.sem, 1)
                    for u in range(2):
                        pe.wait_ge(htc.sem, htc.at(g, u + 1))
                        pe.wait_ge(ge.sem, ge.at(g, u - 1))
                        for c in range(FF // P):
                            last = M(p_f[u][:, c, :], wf1[:, c * P:(c + 1) * P], agt[u][:, :], start=True, stop=True)
                        last.then_inc(f1.sem, 1)
                    for u in range(2):
                        pe.wait_ge(ge.sem, ge.at(g, u + 1))
                        pe.wait_ge(ev2.sem, ev2.at(g, u - 1))
                        for c in range(FF // P):
                            last = M(p_m[u][0:BN, 0:D], gl[u][:, c, :], wf2[:, c, :], start=(c == 0), stop=(c == FF // P - 1))
                        last.then_inc(f2.sem, 1)

        mu, rs = inverse_deviation(nc, k, sb, sem, st, "2")

        xin2 = [Mark(sem(f"xin2{u}"), 16) for u in range(2)]
        ev3 = Mark(sem("ev3"), 2, 2)
        vec3 = sem("vec3")
        with nc.Block() as block:
            @block.sync
            def _(sp):
                sp.sem_inc(ev3.sem, 2)
                with sp.Fori(0, NI) as g:
                    for u in range(2):
                        sp.wait_ge(ev3.sem, ev3.at(g, u - 1))
                        sp.dma_start(xb[u][:, :], io["x"][bass.ds(g * (2 * BN) + u * BN, BN), :]).then_inc(xin2[u].sem, 16)

            @block.vector
            def _(dve):
                V = nc.vector
                PER = 2 * 5
                with dve.Fori(0, NI) as g:
                    v = Chain(dve, vec3, g * PER)
                    for u in range(2):
                        b1 = bass.ds(g * 2 + u, 1)
                        v(V.tensor_scalar(tmp[u][:, :], one(y[:, b1, :]), mu[:, b1], rs[:, b1], ALU.subtract, ALU.mult))
                        v(V.tensor_tensor(tmp[u][:, :], tmp[u][:, :], rows_["g2"][:, :], ALU.mult))
                        dve.wait_ge(xin2[u].sem, xin2[u].at(g, 16))
                        v(V.tensor_tensor(xb[u][:, :], xb[u][:, :], rows_["be2"][:, :], ALU.add))
                        v(V.tensor_tensor(y[:, b1, :], xb[u][:, :].unsqueeze(1), tmp[u][:, :].unsqueeze(1), ALU.add))
                        dve.sem_inc(ev3.sem, 1)
                        v(V.bn_stats(st[:, b1, :].rearrange("p a s -> p (a s)"), one(y[:, b1, :])))
                    assert v.n == PER, v.n

        mu, rs = inverse_deviation(nc, k, sb, sem, st, "3")

        xd = k.big[:, 0:NBP * D].rearrange("p (b c) -> p b c", c=D)
        norm, ntr, ntc, nm, evs, evd = (Mark(sem(m), 2, 2) for m in ("norm", "ntr", "ntc", "nm", "evs", "evd"))
        xst = [Mark(sem(f"xst{u}"), 16, 16) for u in range(2)]
        sst = [Mark(sem(f"sst{u}"), 16, 16) for u in range(2)]
        emb = sem("emb")
        with nc.Block() as block:
            @block.sync
            def _(sp):
                for m in (norm, ntr, ntc, nm, evs, evd, *xst, *sst):
                    sp.sem_inc(m.sem, m.credit)
                sp.dma_start(xd[BN:P, :, :], bc(io["L1_gnn_edge_emb"], 1, NBP)).then_inc(emb, 16)
                with sp.Fori(0, NI) as g:
                    for u in range(2):
                        b = bass.ds(g * (2 * BN) + u * BN, BN)
                        sp.wait_ge(norm.sem, norm.at(g, u + 1))
                        sp.dma_start(k.d_x1[b, :], ag[u][:, :]).then_inc(xst[u].sem, 16)
                    for u in range(2):
                        b = bass.ds(g * (2 * BN) + u * BN, BN)
                        sp.wait_ge(evs.sem, evs.at(g, u + 1))
                        sp.dma_start(k.d_table1[b, :], tmp[u][:, :]).then_inc(sst[u].sem, 16)
                for u in range(2):
                    sp.wait_ge(xst[u].sem, 16 + 16 * NI)
                    sp.wait_ge(sst[u].sem, 16 + 16 * NI)
                sp.wait_ge(emb, 16)

            @block.vector
            def _(dve):
                V = nc.vector
                with dve.Fori(0, NI) as g:
                    for u in range(2):
                        b1 = bass.ds(g * 2 + u, 1)
                        dve.wait_ge(ntr.sem, ntr.at(g, u - 1))
                        dve.wait_ge(xst[u].sem, xst[u].at(g, 0))
                        V.tensor_scalar(ag[u][:, :], one(y[:, b1, :]), mu[:, b1], rs[:, b1], ALU.subtract, ALU.mult)                            .then_inc(norm.sem, 1)
                    for u in range(2):
                        b1 = bass.ds(g * 2 + u, 1)
                        dve.wait_ge(nm.sem, nm.at(g, u + 1))
                        dve.wait_ge(sst[u].sem, sst[u].at(g, 0))
                        V.tensor_tensor(tmp[u][:, :], p_m[u][0:BN, 0:D], rows_["bs"][:, :], ALU.add).then_inc(evs.sem, 1)
                        V.tensor_tensor(xd[0:BN, b1, :], p_m[u][0:BN, D:2 * D].unsqueeze(1), rows_["bd"][:, :].unsqueeze(1),
                                        ALU.add).then_inc(evd.sem, 1)

            @block.scalar
            def _(act):
                with act.Fori(0, NI) as g:
                    for u in range(2):
                        act.wait_ge(ntr.sem, ntr.at(g, u + 1))
                        act.wait_ge(nm.sem, nm.at(g, u - 1))
                        nc.scalar.copy(agt[u][:, :], p_t[u][:, 0:BN]).then_inc(ntc.sem, 1)

            @block.tensor
            def _(pe):
                with pe.Fori(0, NI) as g:
                    for u in range(2):
                        pe.wait_ge(norm.sem, norm.at(g, u + 1))
                        pe.wait_ge(ntc.sem, ntc.at(g, u - 1))
                        nc.tensor.transpose(p_t[u][:, 0:BN], ag[u][:, :], k.iden[0:BN, 0:BN]).then_inc(ntr.sem, 1)
                    for u in range(2):
                        pe.wait_ge(ntc.sem, ntc.at(g, u + 1))
                        pe.wait_ge(evd.sem, evd.at(g, u - 1))
                        nc.tensor.matmul(p_m[u][0:BN, :], agt[u][:, :], wsd[:, :, :].rearrange("p a d -> p (a d)"),
                                         start=True, stop=True).then_inc(nm.sem, 1)


def edges1(nc, k):
    sz = k.sz
    NG, NBP = sz.ng, sz.nbp
    with ExitStack() as ctx:
        sb, pb, sem = stage(nc, ctx, "e1")
        xd = k.big[:, 0:NBP * D].rearrange("p (b c) -> p b c", c=D)
        att = sb("att", [P, D])
        idx = [sb(f"idx{q}", [P, QS], I32) for q in range(NQ)]
        rows = sb("rows", [P, G, D])
        dl = sb("dl", [P, G])
        tyf = sb("tyf", [P, G])
        oh = sb("oh", [P, G, P], BF16)
        oht = [sb(f"oht{u}", [P, QS, P]) for u in range(2)]
        prod = sb("prod", [P, QS, D])
        prod2 = sb("prod2", [P, QS, D])
        p_oht = [pb(f"p_oht{u}", [P, QS, P], BF16) for u in range(2)]
        p_q = [pb(f"p_q{u}", [P, QS, D]) for u in range(2)]
        idx_in = Mark(sem("idx_in"), NQ, NQ)
        rows_in = [Mark(sem(f"rows_in{q}"), 16 * QS) for q in range(NQ)]
        value_out = [Mark(sem(f"value_out{q}"), 16, 16) for q in range(NQ)]
        ohs, oht_t, oht_c = Mark(sem("ohs"), NQ), Mark(sem("oht_t"), NQ, NQ), Mark(sem("oht_c"), NQ, NQ)
        qd, qused = Mark(sem("qd"), NQ, NQ), Mark(sem("qused"), NQ, NQ)
        vec, att_in = sem("vec"), sem("att_in")
        PER = 2 + 4 * NQ
        with nc.Block() as block:
            @block.sync
            def _(sp):
                for m in (*value_out, oht_t, oht_c, qd, qused, idx_in):
                    sp.sem_inc(m.sem, m.credit)
                sp.dma_start(att[:, :], k.io["L1_gnn_att"].rearrange("h d -> (h d)").partition_broadcast(P)).then_inc(att_in, 16)
                with sp.Fori(0, NG) as g:
                    for q in range(NQ):
                        sp.wait_ge(rows_in[q].sem, rows_in[q].at(g, 16 * QS))
                        sp.dma_start(k.d_value[bass.ds(g * NQ + q, 1), :, :, :].rearrange("a p q d -> (a p) q d"),
                                     rows[:, q * QS:q * QS + QS, :]).then_inc(value_out[q].sem, 16)
                for q in range(NQ):
                    sp.wait_ge(value_out[q].sem, 16 + 16 * NG)

            @block.gpsimd
            def _(pl):
                with pl.Fori(0, NG) as g:
                    for q in range(NQ):
                        pl.wait_ge(idx_in.sem, idx_in.at(g, q + 1))
                        pl.wait_ge(qused.sem, qused.at(g, q + 1 - NQ))
                        pl.wait_ge(value_out[q].sem, value_out[q].at(g, 0))
                        apart(pl, k.passed)
                        for i in range(QS):
                            nc.gpsimd.indirect_dma_start(
                                rows[:, q * QS + i, :], None, k.d_table1,
                                bass.IndirectOffsetOnAxis(ap=idx[q][:, i:i + 1], axis=0)).then_inc(rows_in[q].sem, 16)

            @block.vector
            def _(dve):
                V = nc.vector
                dve.wait_ge(att_in, 16)
                with dve.Fori(0, NG) as g:
                    v = Chain(dve, vec, g * PER)
                    s16 = bass.ds(g * G, G)
                    v.did(V.tensor_copy(dl[:, :], k.dstl[:, s16]))
                    v.did(V.tensor_copy(tyf[:, :], k.typ8[:, s16]))
                    v.settle()
                    dve.wait_ge(oht_t.sem, oht_t.at(g, 0))
                    for q in range(NQ):
                        i4 = slice(q * QS, q * QS + QS)
                        V.tensor_tensor(oh[:, i4, BN:P], bc(k.iota[:, 0:NT], 1, QS), bc(tyf[:, i4], 2, NT), ALU.is_equal)
                        for i in range(q * QS, q * QS + QS):
                            last = V.tensor_scalar(oh[:, i, 0:BN], k.iotab[:, 0:BN], dl[:, i:i + 1], None, ALU.is_equal)
                        last.then_inc(ohs.sem, 1)
                    for q in range(NQ):
                        i4 = slice(q * QS, q * QS + QS)
                        dve.wait_ge(rows_in[q].sem, rows_in[q].at(g, 16 * QS))
                        dve.wait_ge(qd.sem, qd.at(g, q + 1))
                        v(V.tensor_tensor(prod[:, :, :], rows[:, i4, :], p_q[q % 2][:, :, :], ALU.add))
                        dve.sem_inc(qused.sem, 1)
                        v(V.scalar_tensor_tensor(prod2[:, :, :], prod[:, :, :], 0.2, prod[:, :, :], ALU.mult, ALU.max))
                        v(V.tensor_tensor(prod[:, :, :], prod2[:, :, :], bc(att[:, :], 1, QS), ALU.mult))
                        v(V.tensor_reduce(k.sco[:, bass.ds(g * P + q * (QS * H1), QS * H1)],
                                          prod[:, :, :].rearrange("p q (h d) -> p (q h) d", h=H1), AX.X, ALU.add))
                    assert v.n == PER, v.n

            @block.scalar
            def _(act):
                with act.Fori(0, NG) as g:
                    for q in range(NQ):
                        act.wait_ge(qused.sem, qused.at(g, q + 1 - NQ))
                        nc.scalar.copy(idx[q][:, :], k.src[:, bass.ds(g * G + q * QS, QS)]).then_inc(idx_in.sem, 1)
                    for q in range(NQ):
                        act.wait_ge(oht_t.sem, oht_t.at(g, q + 1))
                        act.wait_ge(qd.sem, qd.at(g, q - 1))
                        nc.scalar.copy(oht[q % 2][:, :, :], p_oht[q % 2][:, :, :]).then_inc(oht_c.sem, 1)

            @block.tensor
            def _(pe):
                with pe.Fori(0, NG) as g:
                    blocks = load_steps(nc, k, ET.PE, 1, g, sz.nb)

                    def transposes(q):
                        pe.wait_ge(ohs.sem, ohs.at(g, q + 1))
                        pe.wait_ge(oht_c.sem, oht_c.at(g, q - 1))
                        for i in range(QS):
                            last = nc.tensor.transpose(p_oht[q % 2][:, i, :], oh[:, q * QS + i, :], k.idenb[:, :])
                        last.then_inc(oht_t.sem, 1)

                    transposes(0)
                    for q in range(NQ):
                        if q + 1 < NQ:
                            transposes(q + 1)
                        pe.wait_ge(oht_c.sem, oht_c.at(g, q + 1))
                        pe.wait_ge(qused.sem, qused.at(g, q - 1))
                        for i in range(QS):
                            last = nc.tensor.matmul(p_q[q % 2][:, i, :], oht[q % 2][:, i, :],
                                                    xd[:, bass.ds(blocks[q * QS + i], 1), :], start=True, stop=True)
                        last.then_inc(qd.sem, 1)


def nodes1(nc, k):
    io, sz = k.io, k.sz
    NBP = sz.nbp
    W = D + H1
    NI = NBP // 2
    with ExitStack() as ctx:
        sb, pb, sem = stage(nc, ctx, "n1")
        acc = k.big[0:BN, 0:NBP * W].rearrange("p (b c) -> p b c", c=W)
        num = acc[:, :, 0:D]
        y = num
        x1 = Carve(k.pair)([BN, NBP, D])
        st = sb("st", [BN, NBP, 6])
        rd = sb("rd", [BN, NBP, H1])
        wout = sb("wout", [P, D])
        wfilm = sb("wfilm", [P, 2 * D])
        task = sb("task", [P, 1])
        taskb = sb("taskb", [P, P])
        bfilm = sb("bfilm", [P, 2 * D])
        film = sb("film", [P, 2 * D])
        gam = sb("gam", [P, D])
        bo = sb("bo", [P, D])
        nw = sb("nw", [BN, D])
        nb_ = sb("nb", [BN, D])
        ag = [sb(f"ag{u}", [BN, D]) for u in range(2)]
        agt = [sb(f"agt{u}", [P, BN]) for u in range(2)]
        tmp = [sb(f"tmp{u}", [BN, D]) for u in range(2)]
        p_t = [pb(f"p_t{u}", [P, P]) for u in range(2)]
        p_m = [pb(f"p_m{u}", [P, 256]) for u in range(2)]
        loaded, vec, film_mm, th = sem("loaded"), sem("vec"), sem("film_mm"), sem("th")
        tb, toact = sem("tb"), sem("toact")
        with nc.Block() as block:
            @block.sync
            def _(sp):
                for dst, src in ((wout[:, :], io["L1_gnn_W_out"]), (wfilm[:, :], io["L1_gnn_W_film"]),
                                 (task[:, :], io["L1_gnn_task_embedding"].rearrange("(p c) -> p c", c=1)),
                                 (bfilm[:, :], io["L1_gnn_b_film"].partition_broadcast(P)),
                                 (bo[:, :], io["L1_gnn_b_out"].partition_broadcast(P)),
                                 (nw[:, :], io["L1_gnn_norm_w"].partition_broadcast(BN)),
                                 (nb_[:, :], io["L1_gnn_norm_b"].partition_broadcast(BN)),
                                 (x1[:, :, :], k.d_x1.rearrange("(b p) d -> p b d", p=BN))):
                    sp.dma_start(dst, src).then_inc(loaded, 16)
                sp.wait_ge(loaded, 16 * 8)

            @block.vector
            def _(dve):
                V = nc.vector
                v = Chain(dve, vec)
                v(V.tensor_scalar(rd[:, :, :], acc[:, :, D:W], 1e-12, None, ALU.max))
                v(V.reciprocal(rd[:, :, :], rd[:, :, :]))
                nv = num.rearrange("p b (h d) -> p b h d", h=H1)
                v(V.tensor_tensor(nv, nv, bc(rd[:, :, :], 3, D // H1), ALU.mult))
                dve.wait_ge(loaded, 16 * 8)
                v(V.tensor_copy(taskb[:, :], task[:, 0:1].broadcast_to([P, P])))
                dve.sem_inc(tb, 1)
                dve.wait_ge(film_mm, 1)
                v(V.tensor_tensor(film[:, :], p_m[0][:, :], bfilm[:, :], ALU.add))
                dve.sem_inc(toact, 1)
                dve.wait_ge(th, 1)
                v(V.tensor_scalar(gam[:, :], gam[:, :], 0.5, 1.0, ALU.mult, ALU.add))
                v(V.tensor_tensor(wout[:, :], wout[:, :], gam[:, :], ALU.mult))
                v(V.tensor_tensor(bo[:, :], bo[:, :], gam[:, :], ALU.mult))
                v(V.tensor_tensor(bo[:, :], bo[:, :], film[:, D:2 * D], ALU.add))

            @block.tensor
            def _(pe):
                pe.wait_ge(tb, 1)
                nc.tensor.matmul(p_m[0][:, :], taskb[:, :], wfilm[:, :], start=True, stop=True).then_inc(film_mm, 1)

            @block.scalar
            def _(act):
                act.wait_ge(toact, 1)
                nc.scalar.activation(gam[:, :], film[:, 0:D], ACT.Tanh).then_inc(th, 1)

        agc, tr, trc, mm, ev = (Mark(sem(m), 2, 2) for m in ("agc", "tr", "trc", "mm", "ev"))
        vec1 = sem("vec1")
        with nc.Block() as block:
            @block.sync
            def _(sp):
                for m in (agc, tr, trc, mm, ev):
                    sp.sem_inc(m.sem, m.credit)

            @block.gpsimd
            def _(pl):
                with pl.Fori(0, NI) as g:
                    for u in range(2):
                        pl.wait_ge(tr.sem, tr.at(g, u - 1))
                        nc.gpsimd.tensor_copy(ag[u][:, :].unsqueeze(1), num[:, bass.ds(g * 2 + u, 1), :]).then_inc(agc.sem, 1)

            @block.scalar
            def _(act):
                with act.Fori(0, NI) as g:
                    for u in range(2):
                        act.wait_ge(tr.sem, tr.at(g, u + 1))
                        act.wait_ge(mm.sem, mm.at(g, u - 1))
                        nc.scalar.copy(agt[u][:, :], p_t[u][:, 0:BN]).then_inc(trc.sem, 1)

            @block.tensor
            def _(pe):
                with pe.Fori(0, NI) as g:
                    for u in range(2):
                        pe.wait_ge(agc.sem, agc.at(g, u + 1))
                        pe.wait_ge(trc.sem, trc.at(g, u - 1))
                        nc.tensor.transpose(p_t[u][:, 0:BN], ag[u][:, :], k.iden[0:BN, 0:BN]).then_inc(tr.sem, 1)
                    for u in range(2):
                        pe.wait_ge(trc.sem, trc.at(g, u + 1))
                        pe.wait_ge(ev.sem, ev.at(g, u - 1))
                        nc.tensor.matmul(p_m[u][0:BN, 0:D], agt[u][:, :], wout[:, :], start=True, stop=True).then_inc(mm.sem, 1)

            @block.vector
            def _(dve):
                V = nc.vector
                PER = 6
                with dve.Fori(0, NI) as g:
                    v = Chain(dve, vec1, g * PER)
                    for u in range(2):
                        b1 = bass.ds(g * 2 + u, 1)
                        v(V.tensor_tensor(tmp[u][:, :].unsqueeze(1), x1[:, b1, :], bo[0:BN, :].unsqueeze(1), ALU.add))
                        dve.wait_ge(mm.sem, mm.at(g, u + 1))
                        v(V.tensor_tensor(y[:, b1, :], tmp[u][:, :].unsqueeze(1), p_m[u][0:BN, 0:D].unsqueeze(1), ALU.add))
                        dve.sem_inc(ev.sem, 1)
                        v(V.bn_stats(st[:, b1, :].rearrange("p a s -> p (a s)"), one(y[:, b1, :])))
                    assert v.n == PER

        mu, rs = inverse_deviation(nc, k, sb, sem, st, "1")
        vec2 = sem("vec2")
        with nc.Block() as block:
            @block.vector
            def _(dve):
                V = nc.vector
                PER = 2 * 5
                with dve.Fori(0, NI) as g:
                    v = Chain(dve, vec2, g * PER)
                    for u in range(2):
                        b1 = bass.ds(g * 2 + u, 1)
                        v(V.tensor_scalar(tmp[u][:, :], one(y[:, b1, :]), mu[:, b1], rs[:, b1], ALU.subtract, ALU.mult))
                        v(V.tensor_tensor(tmp[u][:, :], tmp[u][:, :], nw[:, :], ALU.mult))
                        v(V.tensor_tensor(tmp[u][:, :], tmp[u][:, :], nb_[:, :], ALU.add))
                        v(V.tensor_tensor(y[:, b1, :], x1[:, b1, :], tmp[u][:, :].unsqueeze(1), ALU.add))
                        v(V.bn_stats(st[:, b1, :].rearrange("p a s -> p (a s)"), one(y[:, b1, :])))
                    assert v.n == PER, v.n

        mu, rs = inverse_deviation(nc, k, sb, sem, st, "2")
        ready, out_sem = sem("ready"), sem("out")
        NF = sz.n // BN
        rest = sz.n - NF * BN
        out = io["out"]
        with nc.Block() as block:
            @block.vector
            def _(dve):
                V = nc.vector
                with dve.Fori(0, NBP) as g:
                    V.tensor_scalar(one(x1[:, bass.ds(g, 1), :]), one(y[:, bass.ds(g, 1), :]), mu[:, bass.ds(g, 1)],
                                    rs[:, bass.ds(g, 1)], ALU.subtract, ALU.mult).then_inc(ready, 1)

            @block.sync
            def _(sp):
                step = 6
                n = 0
                for b in range(0, NF, step):
                    e = min(b + step, NF)
                    sp.wait_ge(ready, e)
                    sp.dma_start(out[b * BN:e * BN, :].rearrange("(b p) d -> p b d", p=BN), x1[:, b:e, :]).then_inc(out_sem, 16)
                    n += 16
                if rest:
                    sp.wait_ge(ready, NF + 1)
                    sp.dma_start(out[NF * BN:sz.n, :], x1[0:rest, NF, :]).then_inc(out_sem, 16)
                    n += 16
                sp.wait_ge(out_sem, n)


_WEIGHTS = ["L0_gnn_" + n for n in (
    "Wq Wk Wv rel_q rel_k rel_v Wt bt Wd1 bd1 Wd2 bd2 decay_scale hyp_beta logit_alpha Wo bo g1 be1 g2 be2 "
    "Wf1 bf1 Wf2 bf2").split()] + ["L1_gnn_" + n for n in (
    "task_embedding W_src b_src W_dst b_dst edge_emb att W_out b_out norm_w norm_b W_film b_film").split()]


def kernel(**inputs):
    import numpy as _np
    import concourse.bacc as _bacc
    from concourse.bass_utils import run_bass_kernel_spmd as _run

    x = _np.asarray(inputs["x"])
    src, dst = _np.asarray(inputs["src"]), _np.asarray(inputs["dst"])
    n, edges = x.shape[0], src.shape[0]
    tiles = -(-edges // P)
    pad = tiles * P - edges
    sz = Sizes(n, tiles)

    def padded(a, value=0):
        fill = _np.full((pad,) + a.shape[1:], value, a.dtype)
        return _np.concatenate([a, fill])

    dst = padded(dst, n)
    type2, type8 = padded(_np.asarray(inputs["edge_type_2"])), padded(_np.asarray(inputs["edge_type_8"]))
    attr = padded(_np.asarray(inputs["edge_attr_32"])).reshape(tiles, P, TE_ROWS)
    time = padded(_np.asarray(inputs["edge_weight"])).reshape(tiles, 1, P)
    x_pad = _np.concatenate([x, _np.zeros((sz.nbp * BN - n, D), x.dtype)])
    arrays = {
        "x": x_pad,
        "xT": x_pad.T,
        "first": dst[::P],
        "last": dst[P - 1::P],
        "type2": type2,
        "edge_ids": _np.stack([padded(src), dst, type2, type8], axis=1),
        "edge_feat": _np.concatenate([attr.transpose(0, 2, 1), type2.view(_np.float32).reshape(tiles, 1, P), time], axis=1),
        "c_mag": _np.asarray(inputs["L0_gnn_c_mag"]).reshape(1),
    }
    for name in _WEIGHTS:
        arrays[name] = _np.asarray(inputs[name])
    nc = _bacc.Bacc("TRN2", target_bir_lowering=False, num_devices=1)
    io, feed = {}, {}
    for name, a in arrays.items():
        a = _np.ascontiguousarray(a)
        feed[f"in_{name}"] = a
        io[name] = nc.dram_tensor(f"in_{name}", a.shape, mybir.dt.from_np(a.dtype), kind="ExternalInput").ap()
    io["out"] = nc.dram_tensor("out_0", (n, D), F32, kind="ExternalOutput").ap()
    program(nc, io, sz)
    r = _run(nc, [feed], core_ids=[0])
    return r.results[0]["out_0"]
```

```python
import math
from contextlib import ExitStack

import numpy as np

import concourse.bass as bass
from concourse import mybir

F32 = mybir.dt.float32
BF16 = mybir.dt.bfloat16
I32 = mybir.dt.int32
ALU = mybir.AluOpType
ACT = mybir.ActivationFunctionType
AX = mybir.AxisListType
ET = mybir.EngineType

P = 128
D = 128
BN = 120
NT = P - BN
G = 16
QS = 4
NQ = G // QS
GROUPS = 4
AHEAD = 2
BIG = 1e30
H0, H1 = 8, 4
TE_ROWS = 32
HID = 64
R_TYPE, R_TIME, R_ONE = 32, 33, 34
FF = 512


class Mark:

    def __init__(self, sem, per, credit=0):
        self.sem, self.per, self.credit = sem, per, credit

    def at(self, g, k):
        return g * self.per + (self.credit + k)


class Chain:

    def __init__(self, eng, sem, base=0):
        self.eng, self.sem, self.base, self.n = eng, sem, base, 0

    def did(self, ins):
        self.n += 1
        ins.then_inc(self.sem, 1)

    def settle(self, but=0):
        self.eng.wait_ge(self.sem, self.base + (self.n - but))

    def __call__(self, ins):
        self.did(ins)
        self.settle()


def apart(eng, passed):
    eng.sem_inc(passed, 1)


def bc(ap, axis, n):
    a = ap.unsqueeze(axis)
    shape = list(a.shape)
    shape[axis] = n
    return a.broadcast_to(shape)


class Sizes:
    def __init__(self, n_nodes, n_tiles):
        self.n = n_nodes
        self.tiles = n_tiles
        self.nb = math.ceil(n_nodes / BN)
        self.nbp = math.ceil(self.nb / 6) * 6
        self.steps = math.ceil((n_tiles + self.nb - 1) / (GROUPS * G)) * GROUPS * G
        self.ng = self.steps // G


def program(nc, io, sz):
    with ExitStack() as ctx:
        k = Kept(nc, ctx, io, sz)
        prepare(nc, k)
        tables0(nc, k)
        edges0(nc, k)
        scores0(nc, k)
        segment_max(nc, k, H0, "a")
        weighted_sums(nc, k, H0, D + 2 * H0, "a")
        nodes0(nc, k)
        clear_semaphores(nc, k)
        edges1(nc, k)
        segment_max(nc, k, H1, "b")
        weighted_sums(nc, k, H1, D + H1, "b")
        nodes1(nc, k)


class Kept:

    def __init__(self, nc, ctx, io, sz):
        self.io, self.sz = io, sz
        S, nbp = sz.steps, sz.nbp

        def sb(name, shape, dt=F32):
            return ctx.enter_context(nc.sbuf_tensor(name, shape, dt))

        self.dst = sb("dst_f", [P, S])
        self.dstl = sb("dst_local", [P, S], BF16)
        self.typ = sb("types", [P, S, 2], BF16)
        self.src = sb("src_i", [P, S], I32)
        self.blkf = sb("block_first", [P, S])
        self.tile_block = sb("tile_block", [2, S], I32)
        self.iden = sb("iden", [P, P])
        self.idenb = sb("idenb", [P, P], BF16)
        self.iota = sb("iota_f", [P, P])
        self.iotab = sb("iota_b", [P, P], BF16)
        self.wedge = sb("wedge", [P, D])
        self.wdec1 = sb("wdec1", [P, HID])
        self.wdec2 = sb("wdec2", [HID + 1, H0])
        self.heads = sb("heads", [P, 3, H0])
        self.big = sb("big", [P, max(nbp * 2 * (D + 2 * H0), S * 22)])
        self.pair = sb("scores_exps", [P, max(2 * S * H0, nbp * D)])
        self.sco = self.pair[:, 0:S * H0]
        self.exs = self.pair[:, S * H0:2 * S * H0]
        self.retired = []
        self.passed = ctx.enter_context(nc.semaphore("passed"))
        def dr(name, shape, dt=F32):
            return nc.dram_tensor(name, shape, dt, kind="Internal").ap()

        self.d_sched = dr("d_sched", (2, S), I32)
        self.d_blkf = dr("d_blkf", (S,))
        self.d_typerows = dr("d_typerows", (NT, 256))
        self.d_table0 = dr("d_table0", (nbp * BN, 3 * D))
        self.d_table1 = dr("d_table1", (nbp * BN, D))
        self.d_value = dr("d_value", (S // QS, P, QS, D))
        self.d_x1 = dr("d_x1", (nbp * BN, D))


def clear_semaphores(nc, k):
    numbers = sorted(k.retired)
    assert numbers == list(range(numbers[0], numbers[-1] + 1))
    with nc.Block() as block:
        @block.sync
        def _(sp):
            sp.sem_clear(range(numbers[0], numbers[-1] + 1))


def stage(nc, ctx, prefix, retired=None):
    def sb(name, shape, dt=F32):
        return ctx.enter_context(nc.sbuf_tensor(f"{prefix}_{name}", shape, dt))

    def pb(name, shape, dt=F32):
        return ctx.enter_context(nc.psum_tensor(f"{prefix}_{name}", shape, dt))

    def sem(name):
        s = ctx.enter_context(nc.semaphore(f"{prefix}_{name}"))
        if retired is not None:
            retired.append(s.num)
        return s

    return sb, pb, sem


class Carve:

    def __init__(self, ap, start=0):
        self.ap, self.at = ap, start

    def __call__(self, shape, dt=F32):
        n = math.prod(shape[1:])
        v = self.ap[0:shape[0], self.at:self.at + n]
        self.at += n
        assert self.at <= self.ap.shape[1]
        if dt is not F32:
            v = v.bitcast(dt)
        if len(shape) == 3:
            v = v.rearrange("p (a b) -> p a b", b=shape[2])
        return v


def row(ap):
    return ap.rearrange("(a n) -> a n", a=1)


def prepare(nc, k):
    io, sz = k.io, k.sz
    T, S, NB = sz.tiles, sz.steps, sz.nb
    C = S // P if S % P == 0 else S // P + 1
    with ExitStack() as ctx:
        sb, pb, sem = stage(nc, ctx, "pre", k.retired)
        cut = Carve(k.big)
        ends_i = cut([P, 2, T], I32)
        ends = cut([P, 2, T])
        q_i = cut([P, 2, T], I32)
        q = cut([P, 2, T])
        rem = cut([P, 2, T])
        flag = cut([P, 2, T])
        count = cut([P, T])
        begin = cut([P, T])
        gap = cut([P, T])
        dgap = cut([P, T])
        zero = cut([P, T])
        junk = cut([P, T])
        stepno_i = sb("stepno_i", [P, C], I32)
        stepno = sb("stepno", [P, C])
        tno = sb("tno", [P, C])
        bno = sb("bno", [P, C])
        gsum = sb("gsum", [P, C])
        both_i = sb("both_i", [P, 2, C], I32)
        io_i = sb("io_i", [P, P], I32)
        types = cut([P, T], I32)
        typesf = cut([P, T])
        tmax = sb("tmax", [P, 1])
        tall = sb("tall", [P, 1])
        rden = sb("rden", [P, 1])
        la = sb("la", [P, H0])
        beta = sb("beta", [P, H0])
        sig = sb("sig", [P, 3, H0])
        rk = sb("rk", [1, 3, D])
        rk_out = sb("rk_out", [1, 2, D])
        wd = sb("wd", [1, HID])
        wd_out = sb("wd_out", [1, HID])
        zrow = sb("zrow", [1, D])
        rq = sb("rq", [2, D])
        trow = sb("trow", [NT, 2 * D])
        loaded, ident, vec, vdone, pool, sched, late, act_s = (sem(n) for n in (
            "loaded", "ident", "vec", "vdone", "pool", "sched", "late", "act"))
        n_loads = 15
        with nc.Block() as block:
            @block.sync
            def _(sp):
                def load(dst, src):
                    sp.dma_start(dst, src).then_inc(loaded, 16)

                sp.wait_ge(ident, 3)
                load(ends_i[:, 0, :], io["first"].partition_broadcast(P))
                load(ends_i[:, 1, :], io["last"].partition_broadcast(P))
                load(types[:, :], io["type2"].rearrange("(p c) -> p c", p=P))
                load(la[:, :], io["L0_gnn_logit_alpha"].partition_broadcast(P))
                load(beta[:, :], io["L0_gnn_hyp_beta"].partition_broadcast(P))
                load(k.heads[:, 0, :], io["L0_gnn_decay_scale"].partition_broadcast(P))
                load(k.wedge[0:TE_ROWS, :], io["L0_gnn_Wt"])
                load(rk[0:1, 0:2, :], io["L0_gnn_rel_k"].rearrange("(a t) d -> a t d", a=1))
                load(rk[0:1, 2, :], row(io["L0_gnn_bt"]))
                load(wd[:, :], io["L0_gnn_Wd1"][1:2, :])
                load(k.wdec1[R_TIME:R_TIME + 1, :], io["L0_gnn_Wd1"][0:1, :])
                load(k.wdec1[R_ONE:R_ONE + 1, :], row(io["L0_gnn_bd1"]))
                load(k.wdec2[0:HID, :], io["L0_gnn_Wd2"])
                load(k.wdec2[HID:HID + 1, :], row(io["L0_gnn_bd2"]))
                load(rq[:, :], io["L0_gnn_rel_q"])
                sp.wait_ge(vdone, 1)
                full, rest = S // P, S % P
                n = 0
                for src, dst in ((both_i[:, 0, :], k.d_sched[0]), (both_i[:, 1, :], k.d_sched[1]),
                                 (bno[:, :], k.d_blkf)):
                    if full:
                        sp.dma_start(dst[0:full * P].rearrange("(c p) -> p c", p=P), src[:, 0:full],
                                     allow_slow_non_contiguous=True).then_inc(sched, 16)
                        n += 16
                    if rest:
                        sp.dma_start(dst[full * P:S].rearrange("(p c) -> p c", c=1), src[0:rest, full:full + 1],
                                     allow_slow_non_contiguous=True).then_inc(sched, 16)
                        n += 16
                sp.wait_ge(vdone, 4)
                sp.dma_start(k.wedge[R_TYPE:R_TYPE + 1, :], rk_out[0:1, 0, :]).then_inc(late, 16)
                sp.dma_start(k.wedge[R_ONE:R_ONE + 1, :], rk_out[0:1, 1, :]).then_inc(late, 16)
                sp.dma_start(k.wedge[R_TIME:R_TIME + 1, :], zrow[:, :]).then_inc(late, 16)
                sp.dma_start(k.wdec1[R_TYPE:R_TYPE + 1, :], wd_out[:, :]).then_inc(late, 16)
                sp.dma_start(k.d_typerows, trow[:, :]).then_inc(late, 16)
                sp.wait_ge(sched, n)
                sp.dma_start(k.tile_block[:, :], k.d_sched[:, :]).then_inc(late, 16)
                sp.dma_start(k.blkf[:, :], k.d_blkf.partition_broadcast(P)).then_inc(late, 16)
                sp.wait_ge(late, 7 * 16)

            @block.gpsimd
            def _(pl):
                nc.gpsimd.memset(k.iden[:, :], 0.0).then_inc(ident, 1)
                nc.gpsimd.iota(io_i[:, :], pattern=[[1, P]], base=0, channel_multiplier=0).then_inc(pool, 1)
                nc.gpsimd.iota(stepno_i[:, :], pattern=[[P, C]], base=0, channel_multiplier=1).then_inc(pool, 1)
                nc.gpsimd.memset(k.wedge[:, :], 0.0).then_inc(ident, 1)
                nc.gpsimd.memset(k.wdec1[:, :], 0.0).then_inc(ident, 1)
                pl.wait_ge(ident, 3)
                nc.gpsimd.affine_select(out=k.iden[:, :], in_=k.iden[:, :], compare_op=ALU.not_equal, fill=1.0,
                                        base=0, pattern=[[-1, P]], channel_multiplier=1).then_inc(pool, 1)
                pl.wait_ge(vdone, 3)
                nc.gpsimd.partition_all_reduce(tall[:, :], tmax[:, :], P, bass.bass_isa.ReduceOp.max).then_inc(pool, 1)

            @block.scalar
            def _(act):
                act.wait_ge(loaded, 16 * n_loads)
                nc.scalar.activation(sig[:, 0, :], la[:, :], ACT.Exp, scale=-1.0).then_inc(act_s, 1)

            @block.vector
            def _(dve):
                v = Chain(dve, vec)
                V = nc.vector
                dve.wait_ge(pool, 3)
                v(V.tensor_copy(k.iota[:, :], io_i[:, :]))
                v(V.tensor_copy(k.iotab[:, :], io_i[:, :]))
                v(V.tensor_copy(k.idenb[:, :], k.iden[:, :]))
                v(V.tensor_copy(stepno[:, :], stepno_i[:, :]))
                v(V.memset(zero[:, :], 0.0))
                v(V.memset(zrow[:, :], 0.0))
                v(V.memset(trow[:, :], 0.0))
                dve.wait_ge(loaded, 16 * n_loads)
                v(V.tensor_copy(ends[:, :, :], ends_i[:, :, :]))
                v(V.tensor_scalar(q_i[:, :, :], ends[:, :, :], 1.0 / BN, None, ALU.mult))
                v(V.tensor_copy(q[:, :, :], q_i[:, :, :]))
                ef = ends[:, :, :].rearrange("p a t -> p (a t)")
                qf = q[:, :, :].rearrange("p a t -> p (a t)")
                rf = rem[:, :, :].rearrange("p a t -> p (a t)")
                ff = flag[:, :, :].rearrange("p a t -> p (a t)")
                v(V.scalar_tensor_tensor(rf, qf, -float(BN), ef, ALU.mult, ALU.add))
                v(V.tensor_scalar(ff, rf, float(BN), None, ALU.is_ge))
                v(V.tensor_tensor(qf, qf, ff, ALU.add))
                v(V.tensor_scalar(ff, rf, 0.0, None, ALU.is_lt))
                v(V.tensor_tensor(qf, qf, ff, ALU.subtract))
                v(V.tensor_tensor(count[:, :], q[:, 1, :], q[:, 0, :], ALU.subtract))
                v(V.tensor_scalar(count[:, :], count[:, :], 1.0, None, ALU.add))
                v(V.tensor_tensor_scan(begin[:, :], count[:, :], zero[:, :], 0.0, ALU.add, ALU.add))
                v(V.tensor_tensor(begin[:, :], begin[:, :], count[:, :], ALU.subtract))
                v(V.tensor_tensor(gap[:, :], q[:, 0, :], begin[:, :], ALU.subtract))
                v(V.tensor_copy(dgap[:, 0:1], gap[:, 0:1]))
                v(V.tensor_tensor(dgap[:, 1:T], gap[:, 1:T], gap[:, 0:T - 1], ALU.subtract))
                for c in range(C):
                    v(V.tensor_scalar(junk[:, :], begin[:, :], stepno[:, c:c + 1], None, ALU.is_le, ALU.add,
                                      accum_out=tno[:, c:c + 1]))
                    v(V.scalar_tensor_tensor(junk[:, :], begin[:, :], stepno[:, c:c + 1], dgap[:, :], ALU.is_le,
                                             ALU.mult, accum_out=gsum[:, c:c + 1]))
                v(V.tensor_tensor(bno[:, :], gsum[:, :], stepno[:, :], ALU.add))
                v(V.tensor_scalar(tno[:, :], tno[:, :], 1.0, 0.0, ALU.subtract, ALU.max))
                v(V.tensor_scalar(both_i[:, 0, :], tno[:, :], float(T - 1), None, ALU.min))
                v(V.tensor_scalar(both_i[:, 1, :], bno[:, :], float(NB - 1), 0.0, ALU.min, ALU.max))
                v(V.tensor_scalar(bno[:, :], bno[:, :], float(BN), None, ALU.mult))
                dve.sem_inc(vdone, 1)
                dve.wait_ge(act_s, 1)
                v(V.tensor_scalar(sig[:, 1, :], sig[:, 0, :], 1.0, None, ALU.add))
                v(V.reciprocal(sig[:, 2, :], sig[:, 1, :]))
                v(V.tensor_scalar(k.heads[:, 2, :], sig[:, 2, :], 1.0 / math.sqrt(D // H0), None, ALU.mult))
                v(V.tensor_scalar(sig[:, 1, :], sig[:, 2, :], 1.0, None, ALU.subtract))
                v(V.tensor_tensor(k.heads[:, 1, :], sig[:, 1, :], beta[:, :], ALU.mult))
                v(V.tensor_tensor(rk_out[0:1, 0, :], rk[0:1, 1, :], rk[0:1, 0, :], ALU.subtract))
                v(V.tensor_tensor(rk_out[0:1, 1, :], rk[0:1, 0, :], rk[0:1, 2, :], ALU.add))
                v(V.tensor_tensor(trow[0:2, 0:D].rearrange("p (h d) -> p h d", h=H0),
                                  rq[:, :].rearrange("p (h d) -> p h d", h=H0),
                                  bc(k.heads[0:2, 2, :], 2, D // H0), ALU.mult))
                v(V.tensor_copy(typesf[:, :], types[:, :]))
                v(V.tensor_reduce(tmax[:, :], typesf[:, :], AX.X, ALU.max))
                dve.sem_inc(vdone, 2)
                dve.wait_ge(pool, 4)
                v(V.tensor_scalar(tall[:, :], tall[:, :], 1.0, 1.0, ALU.add, ALU.max))
                v(V.reciprocal(rden[:, :], tall[:, :]))
                v(V.tensor_scalar(wd_out[:, :], wd[:, :], rden[0:1, :], None, ALU.mult))
                dve.sem_inc(vdone, 1)


def tables0(nc, k):
    io, sz = k.io, k.sz
    NBP = sz.nbp
    with ExitStack() as ctx:
        sb, pb, sem = stage(nc, ctx, "tab", k.retired)
        qm = k.big[:, 0:NBP * 256].rearrange("p (b c) -> p b c", c=256)
        xall = Carve(k.pair)([BN, NBP, D])
        xsq = Carve(k.big)([BN, NBP, D])
        wqkv = sb("wqkv", [P, 3, D])
        xt = [sb(f"xt{u}", [P, BN]) for u in range(2)]
        kmv = [sb(f"kmv{u}", [BN, 3 * D]) for u in range(2)]
        pq = [pb(f"pq{u}", [P, D]) for u in range(2)]
        pkv = [pb(f"pkv{u}", [P, 2 * D]) for u in range(2)]
        n = {m: sb(m, [BN, NBP]) for m in ("n2", "nrm", "z", "th", "rz", "zt", "zc", "sn", "cs", "f", "nm", "ov", "sc", "s", "sneg")}
        cc = {m: sb(m, [P, 1]) for m in ("c", "cn", "ca", "pos", "npos", "ac", "sq", "rsq", "mx")}
        loaded, vec, toact, fract, tdone = (sem(m) for m in ("loaded", "vec", "toact", "fract", "tdone"))
        xt_in = [Mark(sem(f"xtin{u}"), 16) for u in range(2)]
        mm = Mark(sem("mm"), 2, 2)
        ev_q, ev_kv = Mark(sem("evq"), 2, 2), Mark(sem("evkv"), 2, 2)
        st = [Mark(sem(f"st{u}"), 16, 16) for u in range(2)]
        with nc.Block() as block:
            @block.sync
            def _(sp):
                sp.sem_inc(mm.sem, 2)
                sp.sem_inc(ev_q.sem, 2)
                sp.sem_inc(ev_kv.sem, 2)
                for u in range(2):
                    sp.sem_inc(st[u].sem, 16)
                sp.dma_start(xall[:, :, :], io["x"].rearrange("(b p) d -> p b d", p=BN)).then_inc(loaded, 16)
                for i, w in enumerate(("Wq", "Wk", "Wv")):
                    sp.dma_start(wqkv[:, i, :], io["L0_gnn_" + w]).then_inc(loaded, 16)
                sp.dma_start(cc["c"][:, :], io["c_mag"].partition_broadcast(P)).then_inc(loaded, 16)
                sp.dma_start(qm[BN:P, :, :], bc(k.d_typerows, 1, NBP)).then_inc(tdone, 16)
                with sp.Fori(0, NBP // 2) as g:
                    for u in range(2):
                        sp.wait_ge(mm.sem, mm.at(g, 0))
                        sp.dma_start(xt[u][:, :], io["xT"][:, bass.ds(g * (2 * BN) + u * BN, BN)]).then_inc(xt_in[u].sem, 16)
                    for u in range(2):
                        sp.wait_ge(ev_q.sem, ev_q.at(g, u + 1))
                        sp.wait_ge(ev_kv.sem, ev_kv.at(g, u + 1))
                        sp.dma_start(k.d_table0[bass.ds(g * (2 * BN) + u * BN, BN), :], kmv[u][:, :]).then_inc(st[u].sem, 16)
                for u in range(2):
                    sp.wait_ge(st[u].sem, 16 + 16 * (NBP // 2))
                sp.wait_ge(tdone, 16)

            @block.vector
            def _(dve):
                V = nc.vector
                v = Chain(dve, vec)
                dve.wait_ge(loaded, 16 * 5)
                v(V.tensor_tensor(wqkv[:, 0, :].rearrange("p (h d) -> p h d", h=H0),
                                  wqkv[:, 0, :].rearrange("p (h d) -> p h d", h=H0),
                                  bc(k.heads[:, 2, :], 2, D // H0), ALU.mult))
                v(V.tensor_tensor(xsq[:, :, :], xall[:, :, :], xall[:, :, :], ALU.mult))
                v(V.tensor_reduce(n["n2"][:, :], xsq[:, :, :], AX.X, ALU.add))
                v(V.tensor_scalar(cc["cn"][:, :], cc["c"][:, :], -1.0, None, ALU.mult))
                v(V.tensor_tensor(cc["ca"][:, :], cc["c"][:, :], cc["cn"][:, :], ALU.max))
                v(V.tensor_scalar(cc["pos"][:, :], cc["ca"][:, :], 0.0, None, ALU.is_gt))
                v(V.tensor_scalar(cc["npos"][:, :], cc["pos"][:, :], -1.0, 1.0, ALU.mult, ALU.add))
                v(V.tensor_scalar(cc["ac"][:, :], cc["ca"][:, :], 1e-15, None, ALU.max))
                dve.sem_inc(toact, 1)
                dve.wait_ge(fract, 1)
                v(V.tensor_scalar(n["nrm"][:, :], n["nrm"][:, :], 1e-15, None, ALU.max))
                v(V.tensor_scalar(n["z"][:, :], n["nrm"][:, :], cc["sq"][0:BN, :], None, ALU.mult))
                v(V.tensor_scalar(n["zt"][:, :], n["z"][:, :], 1.5, None, ALU.min))
                v(V.tensor_scalar(n["zc"][:, :], n["zt"][:, :], -1.0, math.pi / 2, ALU.mult, ALU.add))
                dve.sem_inc(toact, 1)
                v(V.reciprocal(n["rz"][:, :], n["z"][:, :]))
                v(V.reciprocal(cc["rsq"][:, :], cc["sq"][:, :]))
                v(V.tensor_scalar(cc["mx"][:, :], cc["rsq"][:, :], 1.0 - 1e-5, None, ALU.mult))
                dve.wait_ge(fract, 2)
                v(V.tensor_tensor(n["th"][:, :], n["th"][:, :], n["rz"][:, :], ALU.mult))
                v(V.tensor_tensor(n["cs"][:, :], n["cs"][:, :], n["zt"][:, :], ALU.mult))
                v(V.reciprocal(n["cs"][:, :], n["cs"][:, :]))
                v(V.tensor_tensor(n["sn"][:, :], n["sn"][:, :], n["cs"][:, :], ALU.mult))
                v(V.tensor_scalar(n["sn"][:, :], n["sn"][:, :], cc["npos"][0:BN, :], None, ALU.mult))
                v(V.scalar_tensor_tensor(n["f"][:, :], n["th"][:, :], cc["pos"][0:BN, :], n["sn"][:, :], ALU.mult, ALU.add))
                v(V.tensor_tensor(n["nm"][:, :], n["f"][:, :], n["nrm"][:, :], ALU.mult))
                v(V.tensor_scalar(n["ov"][:, :], n["nm"][:, :], cc["mx"][0:BN, :], None, ALU.is_gt))
                v(V.reciprocal(n["sc"][:, :], n["nm"][:, :]))
                v(V.tensor_scalar(n["sc"][:, :], n["sc"][:, :], cc["mx"][0:BN, :], 1.0, ALU.mult, ALU.subtract))
                v(V.tensor_tensor(n["sc"][:, :], n["sc"][:, :], n["ov"][:, :], ALU.mult))
                v(V.tensor_scalar(n["sc"][:, :], n["sc"][:, :], 1.0, None, ALU.add))
                v(V.tensor_tensor(n["s"][:, :], n["f"][:, :], n["sc"][:, :], ALU.mult))
                v(V.tensor_scalar(n["sneg"][:, :], n["s"][:, :], -1.0, None, ALU.mult))
                with dve.Fori(0, NBP // 2) as g:
                    for u in range(2):
                        b = g * 2 + u
                        V.tensor_scalar(qm[0:BN, bass.ds(b, 1), D:2 * D], xall[:, bass.ds(b, 1), :],
                                        n["sneg"][:, bass.ds(b, 1)], None, ALU.mult)
                        dve.wait_ge(st[u].sem, st[u].at(g, 0))
                        V.tensor_scalar(kmv[u][:, D:2 * D], xall[:, bass.ds(b, 1), :].rearrange("p a d -> p (a d)"),
                                        n["s"][:, bass.ds(b, 1)], None, ALU.mult)
                        dve.wait_ge(mm.sem, mm.at(g, u + 1))
                        apart(dve, k.passed)
                        V.tensor_copy(qm[0:BN, bass.ds(b, 1), 0:D], pq[u][0:BN, 0:D].unsqueeze(1)).then_inc(ev_q.sem, 1)

            @block.scalar
            def _(act):
                A = nc.scalar
                act.wait_ge(toact, 1)
                A.activation(n["nrm"][:, :], n["n2"][:, :], ACT.Sqrt)
                A.activation(cc["sq"][:, :], cc["ac"][:, :], ACT.Sqrt).then_inc(fract, 1)
                act.wait_ge(toact, 2)
                A.activation(n["th"][:, :], n["z"][:, :], ACT.Tanh)
                A.activation(n["sn"][:, :], n["zt"][:, :], ACT.Sin)
                A.activation(n["cs"][:, :], n["zc"][:, :], ACT.Sin).then_inc(fract, 1)
                with act.Fori(0, NBP // 2) as g:
                    for u in range(2):
                        act.wait_ge(mm.sem, mm.at(g, u + 1))
                        act.wait_ge(st[u].sem, st[u].at(g, 0))
                        A.copy(kmv[u][:, 0:D], pkv[u][0:BN, 0:D])
                        A.copy(kmv[u][:, 2 * D:3 * D], pkv[u][0:BN, D:2 * D]).then_inc(ev_kv.sem, 1)

            @block.tensor
            def _(pe):
                pe.wait_ge(vec, 1)
                with pe.Fori(0, NBP // 2) as g:
                    for u in range(2):
                        pe.wait_ge(xt_in[u].sem, xt_in[u].at(g, 16))
                        pe.wait_ge(ev_q.sem, ev_q.at(g, u - 1))
                        pe.wait_ge(ev_kv.sem, ev_kv.at(g, u - 1))
                        nc.tensor.matmul(pq[u][0:BN, :], xt[u][:, :], wqkv[:, 0, :], start=True, stop=True)
                        nc.tensor.matmul(pkv[u][0:BN, :], xt[u][:, :], wqkv[:, 1:3, :].rearrange("p a d -> p (a d)"),
                                         start=True, stop=True).then_inc(mm.sem, 1)


def load_steps(nc, k, eng, which, g, bound):
    _, vals = nc.values_load_multi_w_load_instructions(
        k.tile_block[which:which + 1, bass.ds(g * G, G)], engines=(eng,), min_val=0,
        max_val=bound - 1, skip_runtime_bounds_check_because="clamped where it is worked out")
    return vals


def edges0(nc, k):
    io, sz = k.io, k.sz
    NG, NBP = sz.ng, sz.nbp
    with ExitStack() as ctx:
        sb, pb, sem = stage(nc, ctx, "e0", k.retired)
        qm = k.big[:, 0:NBP * 256].rearrange("p (b c) -> p b c", c=256)
        raw = sb("raw", [P, G, 4], I32)
        feat = sb("feat", [P, G, P])
        rows = sb("rows", [P, G, 3 * D])
        dl = sb("dl", [P, G])
        oh = sb("oh", [P, G, P], BF16)
        oht = [sb(f"oht{u}", [P, QS, P]) for u in range(2)]
        hid = sb("hid", [HID + 1, QS * P])
        d2 = sb("d2", [P, G])
        p_oht = pb("p_oht", [P, QS, P], BF16)
        p_q = [pb(f"p_q{u}", [P, QS, D]) for u in range(2)]
        p_d = [pb(f"p_d{u}", [P, QS, D]) for u in range(2)]
        p_t = pb("p_t", [P, QS, D])
        p_h = pb("p_h", [P, QS * P])
        p_e = pb("p_e", [P, G, H0])
        raw_in = [Mark(sem(f"raw_in{q}"), 16 * QS) for q in range(NQ)]
        feat_in = [Mark(sem(f"feat_in{q}"), 16 * QS) for q in range(NQ)]
        rows_in = [Mark(sem(f"rows_in{q}"), 16 * QS) for q in range(NQ)]
        value_out = [Mark(sem(f"value_out{q}"), 16, 16) for q in range(NQ)]
        ohs = Mark(sem("ohs"), NQ)
        oht_t = Mark(sem("oht_t"), NQ, NQ)
        oht_c = Mark(sem("oht_c"), NQ, NQ)
        tps = Mark(sem("tps"), NQ, NQ)
        keys = Mark(sem("keys"), NQ, NQ)
        summed = Mark(sem("summed"), NQ, NQ)
        qd = Mark(sem("qd"), NQ, NQ)
        qused = Mark(sem("qused"), NQ, NQ)
        dused = Mark(sem("dused"), NQ, NQ)
        hps = Mark(sem("hps"), NQ, NQ)
        hsb = Mark(sem("hsb"), NQ, NQ)
        eps = Mark(sem("eps"), NQ, NQ)
        edone = Mark(sem("edone"), 1, 1)
        featc = Mark(sem("featc"), NQ, NQ)
        vec = sem("vec")
        ones, kept = sem("ones"), Mark(sem("kept"), 1)
        build_n, use_n = 5, 4
        PER = NQ * (build_n + use_n)
        with nc.Block() as block:
            @block.sync
            def _(sp):
                for m in (*value_out, summed, oht_t, oht_c, tps, keys, qd, qused, dused, hps, hsb, eps,
                          edone, featc):
                    sp.sem_inc(m.sem, m.credit)
                sp.wait_ge(ones, 3)
                with sp.Fori(0, NG) as g:
                    tiles = load_steps(nc, k, ET.SP, 0, g, sz.tiles)
                    for q in range(NQ):
                        sp.wait_ge(keys.sem, keys.at(g, q + 1 - NQ))
                        apart(sp, k.passed)
                        for i in range(q * QS, q * QS + QS):
                            sp.dma_start(raw[:, i, :], io["edge_ids"][bass.ds(tiles[i] * P, P), :]).then_inc(raw_in[q].sem, 16)
                        sp.wait_ge(tps.sem, tps.at(g, q + 1 - NQ))
                        apart(sp, k.passed)
                        sp.wait_ge(hps.sem, hps.at(g, q + 1 - NQ))
                        apart(sp, k.passed)
                        for i in range(q * QS, q * QS + QS):
                            sp.dma_start(feat[0:R_ONE, i, :],
                                         io["edge_feat"][bass.ds(tiles[i], 1), :, :].rearrange("a r e -> (a r) e"))\
                                .then_inc(feat_in[q].sem, 16)

            @block.gpsimd
            def _(pl):
                nc.gpsimd.memset(feat[:, :, :], 0.0).then_inc(ones, 1)
                pl.wait_ge(ones, 1)
                nc.gpsimd.memset(feat[R_TYPE:R_ONE + 1, :, :], 1.0).then_inc(ones, 1)
                nc.gpsimd.memset(hid[HID:HID + 1, :], 1.0).then_inc(ones, 1)
                with pl.Fori(0, NG) as g:
                    for q in range(NQ):
                        pl.wait_ge(raw_in[q].sem, raw_in[q].at(g, 16 * QS))
                        pl.wait_ge(summed.sem, summed.at(g, q + 1 - NQ))
                        pl.wait_ge(dused.sem, dused.at(g, q + 1 - NQ))
                        pl.wait_ge(value_out[q].sem, value_out[q].at(g, 0))
                        apart(pl, k.passed)
                        for i in range(q * QS, q * QS + QS):
                            nc.gpsimd.indirect_dma_start(
                                rows[:, i, :], None, k.d_table0,
                                bass.IndirectOffsetOnAxis(ap=raw[:, i, 0:1], axis=0)).then_inc(rows_in[q].sem, 16)

            @block.vector
            def _(dve):
                V = nc.vector

                def build(v, g, q):
                    s4 = bass.ds(g * G + q * QS, QS)
                    i4 = slice(q * QS, q * QS + QS)
                    dve.wait_ge(raw_in[q].sem, raw_in[q].at(g, 16 * QS))
                    v.did(V.tensor_tensor(dl[:, i4], raw[:, i4, 1], k.blkf[:, s4], ALU.subtract))
                    v.did(V.tensor_tensor(k.dstl[:, s4], raw[:, i4, 1], k.blkf[:, s4], ALU.subtract))
                    v.did(V.tensor_copy(k.dst[:, s4], raw[:, i4, 1]))
                    v.did(V.tensor_copy(k.typ[:, s4, :], raw[:, i4, 2:4]))
                    v.did(V.tensor_copy(k.src[:, s4], raw[:, i4, 0]))
                    v.settle()
                    dve.wait_ge(oht_t.sem, oht_t.at(g, q + 1 - NQ))
                    V.tensor_tensor(oh[:, i4, BN:P], bc(k.iota[:, 0:NT], 1, QS), bc(k.typ[:, s4, 0], 2, NT), ALU.is_equal)
                    for i in range(q * QS, q * QS + QS):
                        last = V.tensor_scalar(oh[:, i, 0:BN], k.iotab[:, 0:BN], dl[:, i:i + 1], None, ALU.is_equal)
                    last.then_inc(ohs.sem, 1)

                def use(v, g, q):
                    i4 = slice(q * QS, q * QS + QS)
                    prod = rows[:, i4, 0:D]
                    dve.wait_ge(rows_in[q].sem, rows_in[q].at(g, 16 * QS))
                    dve.wait_ge(tps.sem, tps.at(g, q + 1))
                    v(V.tensor_tensor(prod, prod, p_t[:, :, :], ALU.add))
                    dve.sem_inc(keys.sem, 1)
                    dve.wait_ge(qd.sem, qd.at(g, q + 1))
                    v(V.tensor_tensor(prod, prod, p_q[q % 2][:, :, :], ALU.mult))
                    v(V.tensor_tensor(rows[:, i4, D:2 * D], rows[:, i4, D:2 * D], p_d[q % 2][:, :, :], ALU.add))
                    dve.sem_inc(qused.sem, 1)
                    v(V.tensor_reduce(
                        k.sco[:, bass.ds(g * (G * H0) + q * (QS * H0), QS * H0)],
                        prod.rearrange("p q (h d) -> p q h d", h=H0), AX.X, ALU.add))
                    dve.sem_inc(summed.sem, 1)

                first = Chain(dve, vec)
                for q in range(AHEAD):
                    build(first, 0, q)
                with dve.Fori(0, NG - 1) as g:
                    v = Chain(dve, vec, g * PER + first.n)
                    for q in range(NQ):
                        build(v, g + (q + AHEAD) // NQ, (q + AHEAD) % NQ)
                        use(v, g, q)
                    assert v.n == PER, v.n
                v = Chain(dve, vec, (NG - 1) * PER + first.n)
                for q in range(NQ):
                    if q + AHEAD < NQ:
                        build(v, NG - 1, q + AHEAD)
                    use(v, NG - 1, q)

            @block.scalar
            def _(act):
                A = nc.scalar

                def features(g, q):
                    act.wait_ge(feat_in[q].sem, feat_in[q].at(g, 16 * QS))
                    f = feat[R_TYPE:R_TYPE + 1, q * QS:q * QS + QS, :]
                    A.copy(f, f.bitcast(I32)).then_inc(featc.sem, 1)

                def onehot(g, q):
                    act.wait_ge(oht_t.sem, oht_t.at(g, q + 1))
                    act.wait_ge(qd.sem, qd.at(g, q - 1))
                    A.copy(oht[q % 2][:, :, :], p_oht[:, :, :]).then_inc(oht_c.sem, 1)

                def group(g, last_group=False):
                    for q in range(NQ):
                        act.wait_ge(hps.sem, hps.at(g, q + 1))
                        act.wait_ge(eps.sem, eps.at(g, q))
                        A.activation(hid[0:HID, :], p_h[0:HID, :], ACT.Relu).then_inc(hsb.sem, 1)
                        if not (last_group and q + 1 == NQ):
                            features(g + (q + 1) // NQ, (q + 1) % NQ)
                            onehot(g + (q + 1) // NQ, (q + 1) % NQ)
                        act.wait_ge(qused.sem, qused.at(g, q + 1))
                        act.dma_start(k.d_value[bass.ds(g * NQ + q, 1), :, :, :].rearrange("a p q d -> (a p) q d"),
                                      rows[:, q * QS:q * QS + QS, 2 * D:3 * D]).then_inc(value_out[q].sem, 16)
                        for i in range(QS):
                            j = q * QS + i
                            last = A.activation(rows[:, j, D:2 * D], rows[:, j, D:2 * D], ACT.Square, accum_out=d2[:, j:j + 1])
                        last.then_inc(dused.sem, 1)
                    act.wait_ge(eps.sem, eps.at(g, NQ))
                    A.activation(k.exs[:, bass.ds(g * (G * H0), G * H0)], p_e[:, :, :].rearrange("p g h -> p (g h)"),
                                 ACT.Tanh).then_inc(edone.sem, 1)
                    act.wait_ge(dused.sem, dused.at(g, NQ))
                    apart(act, k.passed)
                    A.copy(k.blkf[:, bass.ds(g * G, G)], d2[:, :]).then_inc(kept.sem, 1)
                    act.wait_ge(kept.sem, kept.at(g, 1))

                features(0, 0)
                onehot(0, 0)
                with act.Fori(0, NG - 1) as g:
                    group(g)
                group(NG - 1, True)
                for q in range(NQ):
                    act.wait_ge(value_out[q].sem, 16 + 16 * NG)

            @block.tensor
            def _(pe):
                M = nc.tensor.matmul

                def transposes(g, q):
                    pe.wait_ge(ohs.sem, ohs.at(g, q + 1))
                    pe.wait_ge(oht_c.sem, oht_c.at(g, q))
                    for i in range(QS):
                        last = nc.tensor.transpose(p_oht[:, i, :], oh[:, q * QS + i, :], k.idenb[:, :])
                    last.then_inc(oht_t.sem, 1)

                def group(g, last_group=False):
                    blocks = load_steps(nc, k, ET.PE, 1, g, sz.nb)
                    for q in range(NQ):
                        pe.wait_ge(featc.sem, featc.at(g, q + 1))
                        pe.wait_ge(keys.sem, keys.at(g, q))
                        for i in range(QS):
                            last = M(p_t[:, i, :], feat[:, q * QS + i, :], k.wedge[:, :], start=True, stop=True)
                        last.then_inc(tps.sem, 1)
                        pe.wait_ge(hsb.sem, hsb.at(g, q))
                        M(p_h[0:HID, :], k.wdec1[:, :],
                          feat[:, q * QS:q * QS + QS, :].rearrange("p q e -> p (q e)"),
                          start=True, stop=True).then_inc(hps.sem, 1)
                        if not (last_group and q + 1 == NQ):
                            transposes(g + (q + 1) // NQ, (q + 1) % NQ)
                        pe.wait_ge(oht_c.sem, oht_c.at(g, q + 1))
                        pe.wait_ge(qused.sem, qused.at(g, q - 1))
                        for i in range(QS):
                            j = q * QS + i
                            M(p_q[q % 2][:, i, :], oht[q % 2][:, i, :], qm[:, bass.ds(blocks[j], 1), 0:D],
                              start=True, stop=True)
                            last = M(p_d[q % 2][:, i, :], oht[q % 2][:, i, :], qm[:, bass.ds(blocks[j], 1), D:2 * D],
                                     start=True, stop=True)
                        last.then_inc(qd.sem, 1)
                        pe.wait_ge(hsb.sem, hsb.at(g, q + 1))
                        if q == 0:
                            pe.wait_ge(edone.sem, edone.at(g, 0))
                        for i in range(QS):
                            last = M(p_e[:, q * QS + i, :], hid[:, i * P:(i + 1) * P], k.wdec2[:, :], start=True, stop=True)
                        last.then_inc(eps.sem, 1)

                transposes(0, 0)
                with pe.Fori(0, NG - 1) as g:
                    group(g)
                group(NG - 1, True)


def scores0(nc, k):
    S = k.sz.steps
    with ExitStack() as ctx:
        sb, pb, sem = stage(nc, ctx, "s0")
        dist = sb("dist", [P, S])
        d2 = k.blkf
        vec, ready, fract = sem("vec"), sem("ready"), sem("fract")
        sco = k.sco[:, :].rearrange("p (s h) -> p s h", h=H0)
        exs = k.exs[:, :].rearrange("p (s h) -> p s h", h=H0)
        with nc.Block() as block:
            @block.scalar
            def _(act):
                nc.scalar.activation(dist[:, :], d2[:, :], ACT.Sqrt).then_inc(fract, 1)
                act.wait_ge(ready, 1)
                nc.scalar.activation(k.exs[:, :], k.exs[:, :], ACT.Exp).then_inc(fract, 1)

            @block.vector
            def _(dve):
                V = nc.vector
                v = Chain(dve, vec)
                V.tensor_tensor(exs, exs, bc(k.heads[:, 0, :], 1, S), ALU.mult).then_inc(ready, 1)
                dve.wait_ge(fract, 1)
                for h in range(H0):
                    v.did(V.scalar_tensor_tensor(sco[:, :, h], dist[:, :], k.heads[:, 1, h:h + 1], sco[:, :, h],
                                                 ALU.mult, ALU.add))
                v.settle()
                dve.wait_ge(fract, 2)
                v(V.tensor_tensor(k.sco[:, :], k.sco[:, :], k.exs[:, :], ALU.mult))


def segment_max(nc, k, H, tag):
    sz = k.sz
    S, NG = sz.steps, sz.ng
    R = G * H
    U = GROUPS
    with ExitStack() as ctx:
        sb, pb, sem = stage(nc, ctx, f"mx{tag}")
        sco = k.sco[:, :].rearrange("p (g c) -> p g c", c=P)
        exs = k.exs[:, :].rearrange("p (g c) -> p g c", c=P)
        lt = k.exs[0:R, :].rearrange("p (g c) -> p g c", c=P)
        mloc = k.sco[0:R, :].rearrange("p (g c) -> p g c", c=P)
        zn = k.big[0:R, 0:NG * P].rearrange("p (g c) -> p g c", c=P)
        cut = Carve(k.big, NG * P)
        pen = cut([P, S])
        pen2 = cut([P, S])
        li = [sb(f"li{u}", [P, R]) for u in range(U)]
        zi = [sb(f"zi{u}", [P, R]) for u in range(U)]
        diff = [sb(f"diff{u}", [R, P + 1]) for u in range(U)]
        fwd = [sb(f"fwd{u}", [R, P]) for u in range(U)]
        bwd = [sb(f"bwd{u}", [R, P]) for u in range(U)]
        four = sb("four", [R, 4, NG])
        turned = sb("turned", [NG, 4, R])
        line = cut([H, 4, S])
        join = cut([H, S + 1])
        through = cut([H, S])
        gate = cut([H, S + 1])
        run = cut([H, 2, S])
        carry = cut([H, 2, S])
        carry_g = sb("carry_g", [NG, 2, R])
        carry_t = sb("carry_t", [R, 2, NG])
        pt_ = [pb(f"pt{u}", [P, 2, P]) for u in range(U)]
        pf = [pb(f"pf{u}", [P, 4 * P]) for u in range(2)]
        vec = sem("vec")
        tin, tout, tcopy = (Mark(sem(m), U, U) for m in ("tin", "tout", "tcopy"))
        PER = U * 4
        with nc.Block() as block:
            @block.sync
            def _(sp):
                for m in (tin, tout, tcopy):
                    sp.sem_inc(m.sem, m.credit)

            @block.vector
            def _(dve):
                V = nc.vector
                v = Chain(dve, vec)
                v(V.tensor_scalar(pen[:, :], k.dstl[:, :], 0.0, None, ALU.is_ge))
                v(V.tensor_scalar(pen2[:, :], k.dstl[:, :], float(BN), None, ALU.is_lt))
                v(V.tensor_tensor(pen[:, :], pen[:, :], pen2[:, :], ALU.mult))
                v(V.tensor_scalar(pen[:, :], pen[:, :], 1.0, BIG, ALU.subtract, ALU.mult))
                for u in range(U):
                    v(V.memset(diff[u][:, :], -BIG))
                base = v.n
                with dve.Fori(0, NG // U) as gg:
                    v = Chain(dve, vec, gg * PER + base)
                    for u in range(U):
                        g = gg * U + u
                        s16 = bass.ds(g * G, G)
                        dve.wait_ge(tout.sem, tout.at(gg, u + 1 - U))
                        V.tensor_tensor(li[u][:, :].rearrange("p (t h) -> p t h", h=H),
                                        sco[:, bass.ds(g, 1), 0:R].rearrange("p a (t h) -> p (a t) h", h=H),
                                        bc(pen[:, s16], 2, H), ALU.add)
                        V.tensor_scalar(zi[u][:, :].rearrange("p (t h) -> p t h", h=H),
                                        bc(k.dst[:, s16], 2, H), -BIG, None, ALU.mult).then_inc(tin.sem, 1)
                    for u in range(U):
                        g = gg * U + u
                        dve.wait_ge(tcopy.sem, tcopy.at(gg, u + 1))
                        z = one(zn[:, bass.ds(g, 1), :])
                        v.did(V.tensor_tensor(diff[u][:, 1:P], z[:, 1:P], z[:, 0:P - 1], ALU.subtract))
                    for u in range(U):
                        v.settle(but=U - 1)
                        v.did(V.tensor_tensor_scan(fwd[u][:, :], diff[u][:, 0:P], one(lt[:, bass.ds(gg * U + u, 1), :]),
                                                   -3 * BIG, ALU.add, ALU.max))
                    for u in range(U):
                        v.settle(but=U - 1)
                        v.did(V.tensor_tensor_scan(bwd[u][:, ::-1], diff[u][:, 1:P + 1][:, ::-1], fwd[u][:, ::-1],
                                                   -3 * BIG, ALU.add, ALU.max))
                    for u in range(U):
                        v.settle(but=U - 1)
                        v.did(V.tensor_scalar(one(mloc[:, bass.ds(gg * U + u, 1), :]), bwd[u][:, :], 0.0, None, ALU.add))
                    v.settle()
                    assert v.n == PER

            @block.tensor
            def _(pe):
                with pe.Fori(0, NG // U) as gg:
                    for u in range(U):
                        pe.wait_ge(tin.sem, tin.at(gg, u + 1))
                        pe.wait_ge(tcopy.sem, tcopy.at(gg, u + 1 - U))
                        apart(pe, k.passed)
                        nc.tensor.transpose(pt_[u][0:R, 0, :], li[u][:, :], k.iden[:, :])
                        nc.tensor.transpose(pt_[u][0:R, 1, :], zi[u][:, :], k.iden[:, :]).then_inc(tout.sem, 1)

            @block.scalar
            def _(act):
                with act.Fori(0, NG // U) as gg:
                    for u in range(U):
                        g = gg * U + u
                        act.wait_ge(tout.sem, tout.at(gg, u + 1))
                        nc.scalar.copy(lt[:, bass.ds(g, 1), :].rearrange("p a c -> p (a c)"), pt_[u][0:R, 0, :])
                        nc.scalar.copy(zn[:, bass.ds(g, 1), :].rearrange("p a c -> p (a c)"), pt_[u][0:R, 1, :])\
                            .then_inc(tcopy.sem, 1)

        vec2, pes, lined, carried = sem("vec2"), sem("pes"), sem("lined"), sem("carried")
        HG = G // 2 * NG
        with nc.Block() as block:
            @block.vector
            def _(dve):
                V = nc.vector
                v = Chain(dve, vec2)
                v(V.tensor_copy(four[:, 0, :], mloc[:, :, 0]))
                v(V.tensor_copy(four[:, 1, :], mloc[:, :, P - 1]))
                v(V.tensor_copy(four[:, 2, :], zn[:, :, 0]))
                v(V.tensor_copy(four[:, 3, :], zn[:, :, P - 1]))
                dve.wait_ge(pes, 1)
                v(V.tensor_copy(turned[:, :, :].rearrange("p a r -> p (a r)"), pf[0][0:NG, 0:4 * R]))
                for a in range(4):
                    for half in range(2):
                        dve.wait_ge(pes, 2 + 2 * a + half)
                        t0 = half * (G // 2)
                        v(V.tensor_copy(line[:, a, :].rearrange("h (g t) -> h t g", t=G)[:, t0:t0 + G // 2, :],
                                        pf[half][0:H, 0:HG].rearrange("h (t g) -> h t g", g=NG)))
                v(V.memset(join[:, :], -BIG))
                v(V.tensor_tensor(join[:, 1:S], line[:, 2, 1:S], line[:, 3, 0:S - 1], ALU.not_equal))
                v(V.tensor_scalar(join[:, 1:S], join[:, 1:S], -BIG, None, ALU.mult))
                v(V.tensor_tensor(through[:, :], line[:, 2, :], line[:, 3, :], ALU.not_equal))
                v(V.tensor_scalar(through[:, :], through[:, :], -BIG, None, ALU.mult))
                v(V.tensor_tensor(gate[:, 0:S], join[:, 0:S], through[:, :], ALU.add))
                v(V.tensor_tensor_scan(run[:, 0, :], gate[:, 0:S], line[:, 1, :], -3 * BIG, ALU.add, ALU.max))
                v(V.tensor_tensor(gate[:, 0:S], join[:, 1:S + 1], through[:, :], ALU.add))
                v(V.tensor_tensor_scan(run[:, 1, ::-1], gate[:, 0:S][:, ::-1], line[:, 0, ::-1], -3 * BIG,
                                       ALU.add, ALU.max))
                v(V.memset(carry[:, :, :], -BIG))
                v(V.tensor_tensor(carry[:, 0, 1:S], run[:, 0, 0:S - 1], join[:, 1:S], ALU.add))
                v(V.tensor_tensor(carry[:, 1, 0:S - 1], run[:, 1, 1:S], join[:, 1:S], ALU.add))
                dve.sem_inc(carried, 1)
                dve.wait_ge(pes, 10)
                v(V.tensor_copy(carry_g[:, :, :].rearrange("p a r -> p (a r)"), pf[0][0:NG, 0:2 * R]))
                dve.sem_inc(carried, 1)
                dve.wait_ge(pes, 11)
                v(V.tensor_copy(carry_t[:, :, :].rearrange("p a g -> p (a g)"), pf[1][0:R, 0:2 * NG]))

            @block.tensor
            def _(pe):
                T = nc.tensor.transpose
                pe.wait_ge(vec2, 4)
                for a in range(4):
                    last = T(pf[0][0:NG, a * R:(a + 1) * R], four[:, a, :], k.iden[0:R, 0:R])
                last.then_inc(pes, 1)
                pe.wait_ge(vec2, 5)
                for a in range(4):
                    for half in range(2):
                        n = 2 * a + half
                        if n >= 2:
                            pe.wait_ge(vec2, 5 + n - 1)
                        for t in range(G // 2):
                            tt = half * (G // 2) + t
                            last = T(pf[half][0:H, t * NG:(t + 1) * NG], turned[:, a, tt * H:(tt + 1) * H],
                                     k.iden[0:NG, 0:NG])
                        last.then_inc(pes, 1)
                pe.wait_ge(carried, 1)
                for a in range(2):
                    for t in range(G):
                        last = T(pf[0][0:NG, a * R + t * H:a * R + (t + 1) * H],
                                 carry[:, a, :].rearrange("h (g t) -> h t g", t=G)[:, t, :], k.iden[0:H, 0:H])
                last.then_inc(pes, 1)
                pe.wait_ge(carried, 2)
                for a in range(2):
                    last = T(pf[1][0:R, a * NG:(a + 1) * NG], carry_g[:, a, :], k.iden[0:NG, 0:NG])
                last.then_inc(pes, 1)

        vec3 = sem("vec3")
        xin, ex, xt, xc = (Mark(sem(m), U, U) for m in ("xin", "ex", "xt", "xc"))
        PER3 = U * 4
        xz = [sb(f"xz{u}", [R, P]) for u in range(U)]
        ez = [sb(f"ez{u}", [R, P]) for u in range(U)]
        with nc.Block() as block:
            @block.sync
            def _(sp):
                for m in (xin, ex, xt, xc):
                    sp.sem_inc(m.sem, m.credit)

            @block.vector
            def _(dve):
                V = nc.vector
                with dve.Fori(0, NG // U) as gg:
                    v = Chain(dve, vec3, gg * PER3)
                    g1 = [bass.ds(gg * U + u, 1) for u in range(U)]
                    for u in range(U):
                        z = one(zn[:, g1[u], :])
                        dve.wait_ge(ex.sem, ex.at(gg, u + 1 - U))
                        v.did(V.tensor_scalar(fwd[u][:, :], z, four[:, 2, g1[u]], carry_t[:, 0, g1[u]], ALU.subtract, ALU.add))
                        v.did(V.tensor_scalar(diff[u][:, 0:P], z, four[:, 3, g1[u]], -1.0, ALU.subtract, ALU.mult))
                    for u in range(U):
                        v.settle(but=U - 1)
                        v.did(V.tensor_tensor(fwd[u][:, :], fwd[u][:, :], one(mloc[:, g1[u], :]), ALU.max))
                    for u in range(U):
                        v.settle(but=U - 1)
                        v.did(V.scalar_tensor_tensor(fwd[u][:, :], diff[u][:, 0:P], carry_t[:, 1, g1[u]], fwd[u][:, :],
                                                     ALU.add, ALU.max))
                    for u in range(U):
                        dve.wait_ge(vec3, gg * PER3 + (v.n + u + 1 - U))
                        V.tensor_tensor(xz[u][:, :], one(lt[:, g1[u], :]), fwd[u][:, :], ALU.subtract).then_inc(xin.sem, 1)
                    assert v.n == PER3

            @block.scalar
            def _(act):
                with act.Fori(0, NG // U) as gg:
                    for u in range(U):
                        g = gg * U + u
                        act.wait_ge(xin.sem, xin.at(gg, u + 1))
                        act.wait_ge(xt.sem, xt.at(gg, u + 1 - U))
                        nc.scalar.activation(ez[u][:, :], xz[u][:, :], ACT.Exp).then_inc(ex.sem, 1)
                    for u in range(U):
                        g = gg * U + u
                        act.wait_ge(xt.sem, xt.at(gg, u + 1))
                        nc.scalar.copy(exs[:, bass.ds(g, 1), 0:R].rearrange("p a c -> p (a c)"), pt_[u][:, 0, 0:R])\
                            .then_inc(xc.sem, 1)

            @block.tensor
            def _(pe):
                with pe.Fori(0, NG // U) as gg:
                    for u in range(U):
                        pe.wait_ge(ex.sem, ex.at(gg, u + 1))
                        pe.wait_ge(xc.sem, xc.at(gg, u + 1 - U))
                        apart(pe, k.passed)
                        nc.tensor.transpose(pt_[u][:, 0, 0:R], ez[u][:, :], k.iden[0:R, 0:R]).then_inc(xt.sem, 1)


def weighted_sums(nc, k, H, W, tag):
    sz = k.sz
    NG, NBP, S = sz.ng, sz.nbp, sz.steps
    typed = W > D + H
    with ExitStack() as ctx:
        sb, pb, sem = stage(nc, ctx, f"ws{tag}")
        both = k.big[0:BN, 0:2 * NBP * W]
        acc = [both[:, u * NBP * W:(u + 1) * NBP * W].rearrange("p (b c) -> p b c", c=W) for u in range(2)]
        exs = k.exs[:, :].rearrange("p (g c) -> p g c", c=P)
        val = sb("val", [P, G, D])
        wv = sb("wv", [P, G, W])
        ohb = sb("ohb", [P, G, BN], BF16)
        oh = sb("oh", [P, G, BN])
        dl = sb("dl", [P, G])
        pr = [pb(f"pr{i}", [P, 2, 256]) for i in range(8)]
        val_in = [Mark(sem(f"val_in{q}"), 16) for q in range(NQ)]
        scaled = Mark(sem("scaled"), NQ, NQ)
        extra = Mark(sem("extra"), NQ, NQ)
        ohb_in = Mark(sem("ohb_in"), NQ, NQ)
        prod = Mark(sem("prod"), NQ, NQ)
        added = Mark(sem("added"), NQ, NQ)
        vec = sem("vec")
        PER = NQ * (2 if typed else 1) + G
        with nc.Block() as block:
            @block.sync
            def _(sp):
                for m in (scaled, extra, ohb_in, prod, added):
                    sp.sem_inc(m.sem, m.credit)
                with sp.Fori(0, NG) as g:
                    for q in range(NQ):
                        sp.wait_ge(scaled.sem, scaled.at(g, q + 1 - NQ))
                        sp.dma_start(val[:, q * QS:q * QS + QS, :],
                                     k.d_value[bass.ds(g * NQ + q, 1), :, :, :].rearrange("a p q d -> (a p) q d"))\
                            .then_inc(val_in[q].sem, 16)

            @block.gpsimd
            def _(pl):
                with pl.Fori(0, NG) as g:
                    for q in range(NQ):
                        i4 = slice(q * QS, q * QS + QS)
                        e = exs[:, bass.ds(g, 1), q * QS * H:(q + 1) * QS * H].rearrange("p a (t h) -> p (a t) h", h=H)
                        pl.wait_ge(val_in[q].sem, val_in[q].at(g, 16))
                        pl.wait_ge(prod.sem, prod.at(g, q + 1 - NQ))
                        nc.gpsimd.tensor_tensor(
                            wv[:, i4, 0:D].rearrange("p t (h d) -> p t h d", h=H),
                            val[:, i4, :].rearrange("p t (h d) -> p t h d", h=H), bc(e, 3, D // H), ALU.mult)\
                            .then_inc(scaled.sem, 1)

            @block.scalar
            def _(act):
                with act.Fori(0, NG) as g:
                    for q in range(NQ):
                        i4 = slice(q * QS, q * QS + QS)
                        e = exs[:, bass.ds(g, 1), q * QS * H:(q + 1) * QS * H].rearrange("p a (t h) -> p (a t) h", h=H)
                        act.wait_ge(prod.sem, prod.at(g, q + 1 - NQ))
                        nc.scalar.copy(wv[:, i4, D:D + H], e)
                        act.wait_ge(ohb_in.sem, ohb_in.at(g, q + 1))
                        nc.scalar.copy(oh[:, i4, :], ohb[:, i4, :]).then_inc(extra.sem, 1)

            @block.vector
            def _(dve):
                V = nc.vector

                def build(v, g, q):
                    i4 = slice(q * QS, q * QS + QS)
                    s4 = bass.ds(g * G + q * QS, QS)
                    dve.wait_ge(prod.sem, prod.at(g, q + 1 - NQ))
                    v.did(V.tensor_scalar(dl[:, i4], k.dstl[:, s4], 0.0, None, ALU.add))
                    if typed:
                        e = exs[:, bass.ds(g, 1), q * QS * H:(q + 1) * QS * H].rearrange("p a (t h) -> p (a t) h", h=H)
                        v.did(V.tensor_tensor(wv[:, i4, D + H:W], e, bc(k.typ[:, s4, 0], 2, H), ALU.mult))
                    v.settle()
                    for i in range(q * QS, q * QS + QS):
                        last = V.tensor_scalar(ohb[:, i, :], k.iotab[:, 0:BN], dl[:, i:i + 1], None, ALU.is_equal)
                    last.then_inc(ohb_in.sem, 1)

                def add(v, g, q, blocks):
                    dve.wait_ge(prod.sem, prod.at(g, q + 1))
                    for i in range(q * QS, q * QS + QS):
                        a = acc[i % 2][:, bass.ds(blocks[i], 1), :]
                        v.settle(but=1)
                        v.did(V.tensor_tensor(a, a, pr[i // 2][0:BN, i % 2, 0:W].unsqueeze(1), ALU.add))
                    v.settle()
                    dve.sem_inc(added.sem, 1)

                first = Chain(dve, vec)
                first(V.memset(both, 0.0))
                for q in range(AHEAD):
                    build(first, 0, q)
                with dve.Fori(0, NG - 1) as g:
                    v = Chain(dve, vec, g * PER + first.n)
                    blocks = load_steps(nc, k, ET.DVE, 1, g, sz.nb)
                    for q in range(NQ):
                        build(v, g + (q + AHEAD) // NQ, (q + AHEAD) % NQ)
                        add(v, g, q, blocks)
                    assert v.n == PER, v.n
                v = Chain(dve, vec, (NG - 1) * PER + first.n)
                blocks = load_steps(nc, k, ET.DVE, 1, NG - 1, sz.nb)
                for q in range(NQ):
                    if q + AHEAD < NQ:
                        build(v, NG - 1, q + AHEAD)
                    add(v, NG - 1, q, blocks)
                v(V.tensor_tensor(both[:, 0:NBP * W], both[:, 0:NBP * W], both[:, NBP * W:2 * NBP * W], ALU.add))

            @block.tensor
            def _(pe):
                with pe.Fori(0, NG) as g:
                    for q in range(NQ):
                        pe.wait_ge(scaled.sem, scaled.at(g, q + 1))
                        pe.wait_ge(extra.sem, extra.at(g, q + 1))
                        pe.wait_ge(added.sem, added.at(g, q + 1 - NQ))
                        for i in range(q * QS, q * QS + QS):
                            last = nc.tensor.matmul(pr[i // 2][0:BN, i % 2, 0:W], oh[:, i, :], wv[:, i, :],
                                                    start=True, stop=True)
                        last.then_inc(prod.sem, 1)


def moments(V, v, st, mu, var, tmp):
    v(V.tensor_tensor(mu, st[:, :, 1], st[:, :, 4], ALU.add))
    v(V.tensor_tensor(tmp, st[:, :, 1], st[:, :, 4], ALU.subtract))
    v(V.tensor_tensor(tmp, tmp, tmp, ALU.mult))
    v(V.tensor_tensor(var, st[:, :, 2], st[:, :, 5], ALU.add))
    v(V.tensor_scalar(mu, mu, 0.5, None, ALU.mult))
    v(V.tensor_scalar(var, var, 1.0 / D, 1e-5, ALU.mult, ALU.add))
    v(V.scalar_tensor_tensor(var, tmp, 0.25, var, ALU.mult, ALU.add))


def inverse_deviation(nc, k, sb, sem, st, tag):
    NBP = k.sz.nbp
    mu, rs, tmp = sb(f"mu{tag}", [BN, NBP]), sb(f"rs{tag}", [BN, NBP]), sb(f"dev{tag}", [BN, NBP])
    vec, root, var_ready = sem(f"dev_vec{tag}"), sem(f"dev_root{tag}"), sem(f"dev_var{tag}")
    with nc.Block() as block:
        @block.vector
        def _(dve):
            v = Chain(dve, vec)
            moments(nc.vector, v, st, mu[:, :], rs[:, :], tmp[:, :])
            dve.sem_inc(var_ready, 1)
            dve.wait_ge(root, 1)
            v(nc.vector.reciprocal(rs[:, :], tmp[:, :]))

        @block.scalar
        def _(act):
            act.wait_ge(var_ready, 1)
            nc.scalar.activation(tmp[:, :], rs[:, :], ACT.Sqrt).then_inc(root, 1)
    return mu, rs


def one(ap):
    return ap.rearrange("p a d -> p (a d)")


def nodes0(nc, k):
    io, sz = k.io, k.sz
    NBP = sz.nbp
    W = D + 2 * H0
    NI = NBP // 2
    with ExitStack() as ctx:
        sb, pb, sem = stage(nc, ctx, "n0")
        acc = k.big[0:BN, 0:NBP * W].rearrange("p (b c) -> p b c", c=W)
        num = acc[:, :, 0:D]
        y = Carve(k.pair)([BN, NBP, D])
        hh = num
        st = sb("st", [BN, NBP, 6])
        rd = sb("rd", [BN, NBP, H0])
        a0 = sb("a0", [BN, NBP, H0])
        a1 = sb("a1", [BN, NBP, H0])
        rv = sb("rv", [BN, 2, D])
        rows_ = {m: sb(m, [BN, D]) for m in ("bo", "g1", "be1", "bf2", "g2", "be2", "bs", "bd")}
        wo = sb("wo", [P, D])
        wf1 = sb("wf1", [P, FF])
        wf2 = sb("wf2", [P, FF // P, D])
        bf1 = sb("bf1", [P, FF // P])
        wsd = sb("wsd", [P, 2, D])
        xb = [sb(f"xb{u}", [BN, D]) for u in range(2)]
        ag = [sb(f"ag{u}", [BN, D]) for u in range(2)]
        agt = [sb(f"agt{u}", [P, BN]) for u in range(2)]
        tmp = [sb(f"tmp{u}", [BN, D]) for u in range(2)]
        gl = [sb(f"gl{u}", [P, FF // P, BN]) for u in range(2)]
        p_t = [pb(f"p_t{u}", [P, P]) for u in range(2)]
        p_m = [pb(f"p_m{u}", [P, 256]) for u in range(2)]
        p_f = [pb(f"p_f{u}", [P, FF // P, BN]) for u in range(2)]
        t16 = y
        loaded, vec = sem("loaded"), sem("vec")
        loads = [(rows_["bo"], "bo"), (rows_["g1"], "g1"), (rows_["be1"], "be1"), (rows_["bf2"], "bf2"),
                 (rows_["g2"], "g2"), (rows_["be2"], "be2")]

        with nc.Block() as block:
            @block.sync
            def _(sp):
                n = 0
                for dst, name in loads:
                    sp.dma_start(dst[:, :], io["L0_gnn_" + name].partition_broadcast(BN)).then_inc(loaded, 16)
                sp.dma_start(rows_["bs"][:, :], io["L1_gnn_b_src"].partition_broadcast(BN)).then_inc(loaded, 16)
                sp.dma_start(rows_["bd"][:, :], io["L1_gnn_b_dst"].partition_broadcast(BN)).then_inc(loaded, 16)
                sp.dma_start(rv[:, :, :], io["L0_gnn_rel_v"].partition_broadcast(BN)).then_inc(loaded, 16)
                sp.dma_start(wo[:, :], io["L0_gnn_Wo"]).then_inc(loaded, 16)
                sp.dma_start(wf1[:, :], io["L0_gnn_Wf1"]).then_inc(loaded, 16)
                sp.dma_start(wf2[:, :, :], io["L0_gnn_Wf2"].rearrange("(c p) n -> p c n", p=P)).then_inc(loaded, 16)
                sp.dma_start(bf1[:, :], io["L0_gnn_bf1"].rearrange("(c p) -> p c", p=P),
                             allow_slow_non_contiguous=True).then_inc(loaded, 16)
                sp.dma_start(wsd[:, 0, :], io["L1_gnn_W_src"]).then_inc(loaded, 16)
                sp.dma_start(wsd[:, 1, :], io["L1_gnn_W_dst"]).then_inc(loaded, 16)
                sp.wait_ge(loaded, 16 * 15)

            @block.vector
            def _(dve):
                V = nc.vector
                v = Chain(dve, vec)
                den, dent = acc[:, :, D:D + H0], acc[:, :, D + H0:W]
                v(V.tensor_scalar(rd[:, :, :], den, 1e-30, None, ALU.max))
                v(V.reciprocal(rd[:, :, :], rd[:, :, :]))
                v(V.tensor_tensor(a0[:, :, :], den, dent, ALU.subtract))
                v(V.tensor_tensor(a0[:, :, :], a0[:, :, :], rd[:, :, :], ALU.mult))
                v(V.tensor_tensor(a1[:, :, :], dent, rd[:, :, :], ALU.mult))
                dve.wait_ge(loaded, 16 * 15)
                hv = "p b (h d) -> p b h d"
                nv = num.rearrange(hv, h=H0)
                v(V.tensor_tensor(nv, nv, bc(rd[:, :, :], 3, D // H0), ALU.mult))
                for a, r in ((a0, 0), (a1, 1)):
                    rr = bc(rv[:, r, :].rearrange("p (h d) -> p h d", h=H0), 1, NBP)
                    v(V.tensor_tensor(t16[:, :, :].rearrange(hv, h=H0), bc(a[:, :, :], 3, D // H0), rr, ALU.mult))
                    v(V.tensor_tensor(num, num, t16[:, :, :], ALU.add))

        xin = [Mark(sem(f"xin{u}"), 16) for u in range(2)]
        agc, tr, trc, mm, ev, used = (Mark(sem(m), 2, 2) for m in ("agc", "tr", "trc", "mm", "ev", "used"))
        vec1 = sem("vec1")
        with nc.Block() as block:
            @block.sync
            def _(sp):
                for m in (agc, tr, trc, mm, ev):
                    sp.sem_inc(m.sem, m.credit)
                with sp.Fori(0, NI) as g:
                    for u in range(2):
                        sp.wait_ge(ev.sem, ev.at(g, u - 1))
                        sp.dma_start(xb[u][:, :], io["x"][bass.ds(g * (2 * BN) + u * BN, BN), :]).then_inc(xin[u].sem, 16)

            @block.gpsimd
            def _(pl):
                with pl.Fori(0, NI) as g:
                    for u in range(2):
                        pl.wait_ge(tr.sem, tr.at(g, u - 1))
                        nc.gpsimd.tensor_copy(ag[u][:, :].unsqueeze(1), num[:, bass.ds(g * 2 + u, 1), :]).then_inc(agc.sem, 1)

            @block.scalar
            def _(act):
                with act.Fori(0, NI) as g:
                    for u in range(2):
                        act.wait_ge(tr.sem, tr.at(g, u + 1))
                        act.wait_ge(mm.sem, mm.at(g, u - 1))
                        nc.scalar.copy(agt[u][:, :], p_t[u][:, 0:BN]).then_inc(trc.sem, 1)

            @block.tensor
            def _(pe):
                with pe.Fori(0, NI) as g:
                    for u in range(2):
                        pe.wait_ge(agc.sem, agc.at(g, u + 1))
                        pe.wait_ge(trc.sem, trc.at(g, u - 1))
                        nc.tensor.transpose(p_t[u][:, 0:BN], ag[u][:, :], k.iden[0:BN, 0:BN]).then_inc(tr.sem, 1)
                    for u in range(2):
                        pe.wait_ge(trc.sem, trc.at(g, u + 1))
                        pe.wait_ge(ev.sem, ev.at(g, u - 1))
                        nc.tensor.matmul(p_m[u][0:BN, 0:D], agt[u][:, :], wo[:, :], start=True, stop=True).then_inc(mm.sem, 1)

            @block.vector
            def _(dve):
                V = nc.vector
                PER = 6
                with dve.Fori(0, NI) as g:
                    v = Chain(dve, vec1, g * PER)
                    for u in range(2):
                        yb = y[:, bass.ds(g * 2 + u, 1), :]
                        dve.wait_ge(xin[u].sem, xin[u].at(g, 16))
                        v(V.tensor_tensor(tmp[u][:, :], xb[u][:, :], rows_["bo"][:, :], ALU.add))
                        dve.wait_ge(mm.sem, mm.at(g, u + 1))
                        v(V.tensor_tensor(yb, tmp[u][:, :].unsqueeze(1), p_m[u][0:BN, 0:D].unsqueeze(1), ALU.add))
                        dve.sem_inc(ev.sem, 1)
                        v(V.bn_stats(st[:, bass.ds(g * 2 + u, 1), :].rearrange("p a s -> p (a s)"), one(yb)))
                    assert v.n == PER

        mu, rs = inverse_deviation(nc, k, sb, sem, st, "1")

        hb, htr, htc, f1, ge, f2, ev2 = (Mark(sem(m), 2, 2) for m in ("hb", "htr", "htc", "f1", "ge", "f2", "ev2"))
        vec2 = sem("vec2")
        with nc.Block() as block:
            @block.sync
            def _(sp):
                for m in (hb, htr, htc, f1, ge, f2, ev2):
                    sp.sem_inc(m.sem, m.credit)

            @block.vector
            def _(dve):
                V = nc.vector
                PER = 2 * 6
                with dve.Fori(0, NI) as g:
                    v = Chain(dve, vec2, g * PER)
                    for u in range(2):
                        b1 = bass.ds(g * 2 + u, 1)
                        dve.wait_ge(htr.sem, htr.at(g, u - 1))
                        v(V.tensor_scalar(tmp[u][:, :], one(y[:, b1, :]), mu[:, b1], rs[:, b1], ALU.subtract, ALU.mult))
                        v(V.tensor_tensor(tmp[u][:, :], tmp[u][:, :], rows_["g1"][:, :], ALU.mult))
                        v(V.tensor_tensor(ag[u][:, :], tmp[u][:, :], rows_["be1"][:, :], ALU.add))
                        dve.sem_inc(hb.sem, 1)
                        V.tensor_tensor(hh[:, b1, :], ag[u][:, :].unsqueeze(1), rows_["bf2"][:, :].unsqueeze(1), ALU.add)                            .then_inc(vec2, 1)
                        v.n += 1
                    for u in range(2):
                        b1 = bass.ds(g * 2 + u, 1)
                        dve.wait_ge(f2.sem, f2.at(g, u + 1))
                        v.settle()
                        v(V.tensor_tensor(y[:, b1, :], hh[:, b1, :], p_m[u][0:BN, 0:D].unsqueeze(1), ALU.add))
                        dve.sem_inc(ev2.sem, 1)
                        v(V.bn_stats(st[:, b1, :].rearrange("p a s -> p (a s)"), one(y[:, b1, :])))
                    assert v.n == PER, v.n

            @block.scalar
            def _(act):
                with act.Fori(0, NI) as g:
                    for u in range(2):
                        act.wait_ge(htr.sem, htr.at(g, u + 1))
                        act.wait_ge(f1.sem, f1.at(g, u - 1))
                        nc.scalar.copy(agt[u][:, :], p_t[u][:, 0:BN]).then_inc(htc.sem, 1)
                    for u in range(2):
                        act.wait_ge(f1.sem, f1.at(g, u + 1))
                        act.wait_ge(f2.sem, f2.at(g, u - 1))
                        for c in range(FF // P):
                            last = nc.scalar.activation(gl[u][:, c, :], p_f[u][:, c, :], ACT.Gelu, bias=bf1[:, c:c + 1])
                        last.then_inc(ge.sem, 1)

            @block.tensor
            def _(pe):
                M = nc.tensor.matmul
                with pe.Fori(0, NI) as g:
                    for u in range(2):
                        pe.wait_ge(hb.sem, hb.at(g, u + 1))
                        pe.wait_ge(htc.sem, htc.at(g, u - 1))
                        nc.tensor.transpose(p_t[u][:, 0:BN], ag[u][:, :], k.iden[0:BN, 0:BN]).then_inc(htr.sem, 1)
                    for u in range(2):
                        pe.wait_ge(htc.sem, htc.at(g, u + 1))
                        pe.wait_ge(ge.sem, ge.at(g, u - 1))
                        for c in range(FF // P):
                            last = M(p_f[u][:, c, :], wf1[:, c * P:(c + 1) * P], agt[u][:, :], start=True, stop=True)
                        last.then_inc(f1.sem, 1)
                    for u in range(2):
                        pe.wait_ge(ge.sem, ge.at(g, u + 1))
                        pe.wait_ge(ev2.sem, ev2.at(g, u - 1))
                        for c in range(FF // P):
                            last = M(p_m[u][0:BN, 0:D], gl[u][:, c, :], wf2[:, c, :], start=(c == 0), stop=(c == FF // P - 1))
                        last.then_inc(f2.sem, 1)

        mu, rs = inverse_deviation(nc, k, sb, sem, st, "2")

        xin2 = [Mark(sem(f"xin2{u}"), 16) for u in range(2)]
        ev3 = Mark(sem("ev3"), 2, 2)
        vec3 = sem("vec3")
        with nc.Block() as block:
            @block.sync
            def _(sp):
                sp.sem_inc(ev3.sem, 2)
                with sp.Fori(0, NI) as g:
                    for u in range(2):
                        sp.wait_ge(ev3.sem, ev3.at(g, u - 1))
                        sp.dma_start(xb[u][:, :], io["x"][bass.ds(g * (2 * BN) + u * BN, BN), :]).then_inc(xin2[u].sem, 16)

            @block.vector
            def _(dve):
                V = nc.vector
                PER = 2 * 5
                with dve.Fori(0, NI) as g:
                    v = Chain(dve, vec3, g * PER)
                    for u in range(2):
                        b1 = bass.ds(g * 2 + u, 1)
                        v(V.tensor_scalar(tmp[u][:, :], one(y[:, b1, :]), mu[:, b1], rs[:, b1], ALU.subtract, ALU.mult))
                        v(V.tensor_tensor(tmp[u][:, :], tmp[u][:, :], rows_["g2"][:, :], ALU.mult))
                        dve.wait_ge(xin2[u].sem, xin2[u].at(g, 16))
                        v(V.tensor_tensor(xb[u][:, :], xb[u][:, :], rows_["be2"][:, :], ALU.add))
                        v(V.tensor_tensor(y[:, b1, :], xb[u][:, :].unsqueeze(1), tmp[u][:, :].unsqueeze(1), ALU.add))
                        dve.sem_inc(ev3.sem, 1)
                        v(V.bn_stats(st[:, b1, :].rearrange("p a s -> p (a s)"), one(y[:, b1, :])))
                    assert v.n == PER, v.n

        mu, rs = inverse_deviation(nc, k, sb, sem, st, "3")

        xd = k.big[:, 0:NBP * D].rearrange("p (b c) -> p b c", c=D)
        norm, ntr, ntc, nm, evs, evd = (Mark(sem(m), 2, 2) for m in ("norm", "ntr", "ntc", "nm", "evs", "evd"))
        xst = [Mark(sem(f"xst{u}"), 16, 16) for u in range(2)]
        sst = [Mark(sem(f"sst{u}"), 16, 16) for u in range(2)]
        emb = sem("emb")
        with nc.Block() as block:
            @block.sync
            def _(sp):
                for m in (norm, ntr, ntc, nm, evs, evd, *xst, *sst):
                    sp.sem_inc(m.sem, m.credit)
                sp.dma_start(xd[BN:P, :, :], bc(io["L1_gnn_edge_emb"], 1, NBP)).then_inc(emb, 16)
                with sp.Fori(0, NI) as g:
                    for u in range(2):
                        b = bass.ds(g * (2 * BN) + u * BN, BN)
                        sp.wait_ge(norm.sem, norm.at(g, u + 1))
                        sp.dma_start(k.d_x1[b, :], ag[u][:, :]).then_inc(xst[u].sem, 16)
                    for u in range(2):
                        b = bass.ds(g * (2 * BN) + u * BN, BN)
                        sp.wait_ge(evs.sem, evs.at(g, u + 1))
                        sp.dma_start(k.d_table1[b, :], tmp[u][:, :]).then_inc(sst[u].sem, 16)
                for u in range(2):
                    sp.wait_ge(xst[u].sem, 16 + 16 * NI)
                    sp.wait_ge(sst[u].sem, 16 + 16 * NI)
                sp.wait_ge(emb, 16)

            @block.vector
            def _(dve):
                V = nc.vector
                with dve.Fori(0, NI) as g:
                    for u in range(2):
                        b1 = bass.ds(g * 2 + u, 1)
                        dve.wait_ge(ntr.sem, ntr.at(g, u - 1))
                        dve.wait_ge(xst[u].sem, xst[u].at(g, 0))
                        V.tensor_scalar(ag[u][:, :], one(y[:, b1, :]), mu[:, b1], rs[:, b1], ALU.subtract, ALU.mult)                            .then_inc(norm.sem, 1)
                    for u in range(2):
                        b1 = bass.ds(g * 2 + u, 1)
                        dve.wait_ge(nm.sem, nm.at(g, u + 1))
                        dve.wait_ge(sst[u].sem, sst[u].at(g, 0))
                        V.tensor_tensor(tmp[u][:, :], p_m[u][0:BN, 0:D], rows_["bs"][:, :], ALU.add).then_inc(evs.sem, 1)
                        V.tensor_tensor(xd[0:BN, b1, :], p_m[u][0:BN, D:2 * D].unsqueeze(1), rows_["bd"][:, :].unsqueeze(1),
                                        ALU.add).then_inc(evd.sem, 1)

            @block.scalar
            def _(act):
                with act.Fori(0, NI) as g:
                    for u in range(2):
                        act.wait_ge(ntr.sem, ntr.at(g, u + 1))
                        act.wait_ge(nm.sem, nm.at(g, u - 1))
                        nc.scalar.copy(agt[u][:, :], p_t[u][:, 0:BN]).then_inc(ntc.sem, 1)

            @block.tensor
            def _(pe):
                with pe.Fori(0, NI) as g:
                    for u in range(2):
                        pe.wait_ge(norm.sem, norm.at(g, u + 1))
                        pe.wait_ge(ntc.sem, ntc.at(g, u - 1))
                        nc.tensor.transpose(p_t[u][:, 0:BN], ag[u][:, :], k.iden[0:BN, 0:BN]).then_inc(ntr.sem, 1)
                    for u in range(2):
                        pe.wait_ge(ntc.sem, ntc.at(g, u + 1))
                        pe.wait_ge(evd.sem, evd.at(g, u - 1))
                        nc.tensor.matmul(p_m[u][0:BN, :], agt[u][:, :], wsd[:, :, :].rearrange("p a d -> p (a d)"),
                                         start=True, stop=True).then_inc(nm.sem, 1)


def edges1(nc, k):
    sz = k.sz
    NG, NBP = sz.ng, sz.nbp
    with ExitStack() as ctx:
        sb, pb, sem = stage(nc, ctx, "e1")
        xd = k.big[:, 0:NBP * D].rearrange("p (b c) -> p b c", c=D)
        att = sb("att", [P, D])
        idx = [sb(f"idx{q}", [P, QS], I32) for q in range(NQ)]
        rows = sb("rows", [P, G, D])
        dl = sb("dl", [P, G])
        tyf = sb("tyf", [P, G])
        oh = sb("oh", [P, G, P], BF16)
        oht = [sb(f"oht{u}", [P, QS, P]) for u in range(2)]
        prod = sb("prod", [P, QS, D])
        prod2 = sb("prod2", [P, QS, D])
        p_oht = [pb(f"p_oht{u}", [P, QS, P], BF16) for u in range(2)]
        p_q = [pb(f"p_q{u}", [P, QS, D]) for u in range(2)]
        idx_in = Mark(sem("idx_in"), NQ, NQ)
        rows_in = [Mark(sem(f"rows_in{q}"), 16 * QS) for q in range(NQ)]
        value_out = [Mark(sem(f"value_out{q}"), 16, 16) for q in range(NQ)]
        ohs, oht_t, oht_c = Mark(sem("ohs"), NQ), Mark(sem("oht_t"), NQ, NQ), Mark(sem("oht_c"), NQ, NQ)
        qd, qused = Mark(sem("qd"), NQ, NQ), Mark(sem("qused"), NQ, NQ)
        vec, att_in = sem("vec"), sem("att_in")
        PER = 2 + 4 * NQ
        with nc.Block() as block:
            @block.sync
            def _(sp):
                for m in (*value_out, oht_t, oht_c, qd, qused, idx_in):
                    sp.sem_inc(m.sem, m.credit)
                sp.dma_start(att[:, :], k.io["L1_gnn_att"].rearrange("h d -> (h d)").partition_broadcast(P)).then_inc(att_in, 16)
                with sp.Fori(0, NG) as g:
                    for q in range(NQ):
                        sp.wait_ge(rows_in[q].sem, rows_in[q].at(g, 16 * QS))
                        sp.dma_start(k.d_value[bass.ds(g * NQ + q, 1), :, :, :].rearrange("a p q d -> (a p) q d"),
                                     rows[:, q * QS:q * QS + QS, :]).then_inc(value_out[q].sem, 16)
                for q in range(NQ):
                    sp.wait_ge(value_out[q].sem, 16 + 16 * NG)

            @block.gpsimd
            def _(pl):
                with pl.Fori(0, NG) as g:
                    for q in range(NQ):
                        pl.wait_ge(idx_in.sem, idx_in.at(g, q + 1))
                        pl.wait_ge(qused.sem, qused.at(g, q + 1 - NQ))
                        pl.wait_ge(value_out[q].sem, value_out[q].at(g, 0))
                        apart(pl, k.passed)
                        for i in range(QS):
                            nc.gpsimd.indirect_dma_start(
                                rows[:, q * QS + i, :], None, k.d_table1,
                                bass.IndirectOffsetOnAxis(ap=idx[q][:, i:i + 1], axis=0)).then_inc(rows_in[q].sem, 16)

            @block.vector
            def _(dve):
                V = nc.vector
                dve.wait_ge(att_in, 16)
                with dve.Fori(0, NG) as g:
                    v = Chain(dve, vec, g * PER)
                    s16 = bass.ds(g * G, G)
                    v.did(V.tensor_copy(dl[:, :], k.dstl[:, s16]))
                    v.did(V.tensor_copy(tyf[:, :], k.typ[:, s16, 1]))
                    v.settle()
                    dve.wait_ge(oht_t.sem, oht_t.at(g, 0))
                    for q in range(NQ):
                        i4 = slice(q * QS, q * QS + QS)
                        V.tensor_tensor(oh[:, i4, BN:P], bc(k.iota[:, 0:NT], 1, QS), bc(tyf[:, i4], 2, NT), ALU.is_equal)
                        for i in range(q * QS, q * QS + QS):
                            last = V.tensor_scalar(oh[:, i, 0:BN], k.iotab[:, 0:BN], dl[:, i:i + 1], None, ALU.is_equal)
                        last.then_inc(ohs.sem, 1)
                    for q in range(NQ):
                        i4 = slice(q * QS, q * QS + QS)
                        dve.wait_ge(rows_in[q].sem, rows_in[q].at(g, 16 * QS))
                        dve.wait_ge(qd.sem, qd.at(g, q + 1))
                        v(V.tensor_tensor(prod[:, :, :], rows[:, i4, :], p_q[q % 2][:, :, :], ALU.add))
                        dve.sem_inc(qused.sem, 1)
                        v(V.scalar_tensor_tensor(prod2[:, :, :], prod[:, :, :], 0.2, prod[:, :, :], ALU.mult, ALU.max))
                        v(V.tensor_tensor(prod[:, :, :], prod2[:, :, :], bc(att[:, :], 1, QS), ALU.mult))
                        v(V.tensor_reduce(k.sco[:, bass.ds(g * P + q * (QS * H1), QS * H1)],
                                          prod[:, :, :].rearrange("p q (h d) -> p (q h) d", h=H1), AX.X, ALU.add))
                    assert v.n == PER, v.n

            @block.scalar
            def _(act):
                with act.Fori(0, NG) as g:
                    for q in range(NQ):
                        act.wait_ge(qused.sem, qused.at(g, q + 1 - NQ))
                        nc.scalar.copy(idx[q][:, :], k.src[:, bass.ds(g * G + q * QS, QS)]).then_inc(idx_in.sem, 1)
                    for q in range(NQ):
                        act.wait_ge(oht_t.sem, oht_t.at(g, q + 1))
                        act.wait_ge(qd.sem, qd.at(g, q - 1))
                        nc.scalar.copy(oht[q % 2][:, :, :], p_oht[q % 2][:, :, :]).then_inc(oht_c.sem, 1)

            @block.tensor
            def _(pe):
                with pe.Fori(0, NG) as g:
                    blocks = load_steps(nc, k, ET.PE, 1, g, sz.nb)

                    def transposes(q):
                        pe.wait_ge(ohs.sem, ohs.at(g, q + 1))
                        pe.wait_ge(oht_c.sem, oht_c.at(g, q - 1))
                        for i in range(QS):
                            last = nc.tensor.transpose(p_oht[q % 2][:, i, :], oh[:, q * QS + i, :], k.idenb[:, :])
                        last.then_inc(oht_t.sem, 1)

                    transposes(0)
                    for q in range(NQ):
                        if q + 1 < NQ:
                            transposes(q + 1)
                        pe.wait_ge(oht_c.sem, oht_c.at(g, q + 1))
                        pe.wait_ge(qused.sem, qused.at(g, q - 1))
                        for i in range(QS):
                            last = nc.tensor.matmul(p_q[q % 2][:, i, :], oht[q % 2][:, i, :],
                                                    xd[:, bass.ds(blocks[q * QS + i], 1), :], start=True, stop=True)
                        last.then_inc(qd.sem, 1)


def nodes1(nc, k):
    io, sz = k.io, k.sz
    NBP = sz.nbp
    W = D + H1
    NI = NBP // 2
    with ExitStack() as ctx:
        sb, pb, sem = stage(nc, ctx, "n1")
        acc = k.big[0:BN, 0:NBP * W].rearrange("p (b c) -> p b c", c=W)
        num = acc[:, :, 0:D]
        y = num
        x1 = Carve(k.pair)([BN, NBP, D])
        st = sb("st", [BN, NBP, 6])
        rd = sb("rd", [BN, NBP, H1])
        wout = sb("wout", [P, D])
        wfilm = sb("wfilm", [P, 2 * D])
        task = sb("task", [P, 1])
        taskb = sb("taskb", [P, P])
        bfilm = sb("bfilm", [P, 2 * D])
        film = sb("film", [P, 2 * D])
        gam = sb("gam", [P, D])
        bo = sb("bo", [P, D])
        nw = sb("nw", [BN, D])
        nb_ = sb("nb", [BN, D])
        ag = [sb(f"ag{u}", [BN, D]) for u in range(2)]
        agt = [sb(f"agt{u}", [P, BN]) for u in range(2)]
        tmp = [sb(f"tmp{u}", [BN, D]) for u in range(2)]
        p_t = [pb(f"p_t{u}", [P, P]) for u in range(2)]
        p_m = [pb(f"p_m{u}", [P, 256]) for u in range(2)]
        loaded, vec, film_mm, th = sem("loaded"), sem("vec"), sem("film_mm"), sem("th")
        tb, toact = sem("tb"), sem("toact")
        with nc.Block() as block:
            @block.sync
            def _(sp):
                for dst, src in ((wout[:, :], io["L1_gnn_W_out"]), (wfilm[:, :], io["L1_gnn_W_film"]),
                                 (task[:, :], io["L1_gnn_task_embedding"].rearrange("(p c) -> p c", c=1)),
                                 (bfilm[:, :], io["L1_gnn_b_film"].partition_broadcast(P)),
                                 (bo[:, :], io["L1_gnn_b_out"].partition_broadcast(P)),
                                 (nw[:, :], io["L1_gnn_norm_w"].partition_broadcast(BN)),
                                 (nb_[:, :], io["L1_gnn_norm_b"].partition_broadcast(BN)),
                                 (x1[:, :, :], k.d_x1.rearrange("(b p) d -> p b d", p=BN))):
                    sp.dma_start(dst, src).then_inc(loaded, 16)
                sp.wait_ge(loaded, 16 * 8)

            @block.vector
            def _(dve):
                V = nc.vector
                v = Chain(dve, vec)
                v(V.tensor_scalar(rd[:, :, :], acc[:, :, D:W], 1e-12, None, ALU.max))
                v(V.reciprocal(rd[:, :, :], rd[:, :, :]))
                nv = num.rearrange("p b (h d) -> p b h d", h=H1)
                v(V.tensor_tensor(nv, nv, bc(rd[:, :, :], 3, D // H1), ALU.mult))
                dve.wait_ge(loaded, 16 * 8)
                v(V.tensor_copy(taskb[:, :], task[:, 0:1].broadcast_to([P, P])))
                dve.sem_inc(tb, 1)
                dve.wait_ge(film_mm, 1)
                v(V.tensor_tensor(film[:, :], p_m[0][:, :], bfilm[:, :], ALU.add))
                dve.sem_inc(toact, 1)
                dve.wait_ge(th, 1)
                v(V.tensor_scalar(gam[:, :], gam[:, :], 0.5, 1.0, ALU.mult, ALU.add))
                v(V.tensor_tensor(wout[:, :], wout[:, :], gam[:, :], ALU.mult))
                v(V.tensor_tensor(bo[:, :], bo[:, :], gam[:, :], ALU.mult))
                v(V.tensor_tensor(bo[:, :], bo[:, :], film[:, D:2 * D], ALU.add))

            @block.tensor
            def _(pe):
                pe.wait_ge(tb, 1)
                nc.tensor.matmul(p_m[0][:, :], taskb[:, :], wfilm[:, :], start=True, stop=True).then_inc(film_mm, 1)

            @block.scalar
            def _(act):
                act.wait_ge(toact, 1)
                nc.scalar.activation(gam[:, :], film[:, 0:D], ACT.Tanh).then_inc(th, 1)

        agc, tr, trc, mm, ev = (Mark(sem(m), 2, 2) for m in ("agc", "tr", "trc", "mm", "ev"))
        vec1 = sem("vec1")
        with nc.Block() as block:
            @block.sync
            def _(sp):
                for m in (agc, tr, trc, mm, ev):
                    sp.sem_inc(m.sem, m.credit)

            @block.gpsimd
            def _(pl):
                with pl.Fori(0, NI) as g:
                    for u in range(2):
                        pl.wait_ge(tr.sem, tr.at(g, u - 1))
                        nc.gpsimd.tensor_copy(ag[u][:, :].unsqueeze(1), num[:, bass.ds(g * 2 + u, 1), :]).then_inc(agc.sem, 1)

            @block.scalar
            def _(act):
                with act.Fori(0, NI) as g:
                    for u in range(2):
                        act.wait_ge(tr.sem, tr.at(g, u + 1))
                        act.wait_ge(mm.sem, mm.at(g, u - 1))
                        nc.scalar.copy(agt[u][:, :], p_t[u][:, 0:BN]).then_inc(trc.sem, 1)

            @block.tensor
            def _(pe):
                with pe.Fori(0, NI) as g:
                    for u in range(2):
                        pe.wait_ge(agc.sem, agc.at(g, u + 1))
                        pe.wait_ge(trc.sem, trc.at(g, u - 1))
                        nc.tensor.transpose(p_t[u][:, 0:BN], ag[u][:, :], k.iden[0:BN, 0:BN]).then_inc(tr.sem, 1)
                    for u in range(2):
                        pe.wait_ge(trc.sem, trc.at(g, u + 1))
                        pe.wait_ge(ev.sem, ev.at(g, u - 1))
                        nc.tensor.matmul(p_m[u][0:BN, 0:D], agt[u][:, :], wout[:, :], start=True, stop=True).then_inc(mm.sem, 1)

            @block.vector
            def _(dve):
                V = nc.vector
                PER = 6
                with dve.Fori(0, NI) as g:
                    v = Chain(dve, vec1, g * PER)
                    for u in range(2):
                        b1 = bass.ds(g * 2 + u, 1)
                        v(V.tensor_tensor(tmp[u][:, :].unsqueeze(1), x1[:, b1, :], bo[0:BN, :].unsqueeze(1), ALU.add))
                        dve.wait_ge(mm.sem, mm.at(g, u + 1))
                        v(V.tensor_tensor(y[:, b1, :], tmp[u][:, :].unsqueeze(1), p_m[u][0:BN, 0:D].unsqueeze(1), ALU.add))
                        dve.sem_inc(ev.sem, 1)
                        v(V.bn_stats(st[:, b1, :].rearrange("p a s -> p (a s)"), one(y[:, b1, :])))
                    assert v.n == PER

        mu, rs = inverse_deviation(nc, k, sb, sem, st, "1")
        vec2 = sem("vec2")
        with nc.Block() as block:
            @block.vector
            def _(dve):
                V = nc.vector
                PER = 2 * 5
                with dve.Fori(0, NI) as g:
                    v = Chain(dve, vec2, g * PER)
                    for u in range(2):
                        b1 = bass.ds(g * 2 + u, 1)
                        v(V.tensor_scalar(tmp[u][:, :], one(y[:, b1, :]), mu[:, b1], rs[:, b1], ALU.subtract, ALU.mult))
                        v(V.tensor_tensor(tmp[u][:, :], tmp[u][:, :], nw[:, :], ALU.mult))
                        v(V.tensor_tensor(tmp[u][:, :], tmp[u][:, :], nb_[:, :], ALU.add))
                        v(V.tensor_tensor(y[:, b1, :], x1[:, b1, :], tmp[u][:, :].unsqueeze(1), ALU.add))
                        v(V.bn_stats(st[:, b1, :].rearrange("p a s -> p (a s)"), one(y[:, b1, :])))
                    assert v.n == PER, v.n

        mu, rs = inverse_deviation(nc, k, sb, sem, st, "2")
        ready, out_sem = sem("ready"), sem("out")
        NF = sz.n // BN
        rest = sz.n - NF * BN
        out = io["out"]
        with nc.Block() as block:
            @block.vector
            def _(dve):
                V = nc.vector
                with dve.Fori(0, NBP) as g:
                    V.tensor_scalar(one(x1[:, bass.ds(g, 1), :]), one(y[:, bass.ds(g, 1), :]), mu[:, bass.ds(g, 1)],
                                    rs[:, bass.ds(g, 1)], ALU.subtract, ALU.mult).then_inc(ready, 1)

            @block.sync
            def _(sp):
                step = 6
                n = 0
                for b in range(0, NF, step):
                    e = min(b + step, NF)
                    sp.wait_ge(ready, e)
                    sp.dma_start(out[b * BN:e * BN, :].rearrange("(b p) d -> p b d", p=BN), x1[:, b:e, :]).then_inc(out_sem, 16)
                    n += 16
                if rest:
                    sp.wait_ge(ready, NF + 1)
                    sp.dma_start(out[NF * BN:sz.n, :], x1[0:rest, NF, :]).then_inc(out_sem, 16)
                    n += 16
                sp.wait_ge(out_sem, n)


_WEIGHTS = ["L0_gnn_" + n for n in (
    "Wq Wk Wv rel_q rel_k rel_v Wt bt Wd1 bd1 Wd2 bd2 decay_scale hyp_beta logit_alpha Wo bo g1 be1 g2 be2 "
    "Wf1 bf1 Wf2 bf2").split()] + ["L1_gnn_" + n for n in (
    "task_embedding W_src b_src W_dst b_dst edge_emb att W_out b_out norm_w norm_b W_film b_film").split()]


def kernel(**inputs):
    import numpy as _np
    import concourse.bacc as _bacc
    from concourse.bass_utils import run_bass_kernel_spmd as _run

    x = _np.asarray(inputs["x"])
    src, dst = _np.asarray(inputs["src"]), _np.asarray(inputs["dst"])
    n, edges = x.shape[0], src.shape[0]
    tiles = -(-edges // P)
    pad = tiles * P - edges
    sz = Sizes(n, tiles)

    def padded(a, value=0):
        fill = _np.full((pad,) + a.shape[1:], value, a.dtype)
        return _np.concatenate([a, fill])

    dst = padded(dst, n)
    type2, type8 = padded(_np.asarray(inputs["edge_type_2"])), padded(_np.asarray(inputs["edge_type_8"]))
    attr = padded(_np.asarray(inputs["edge_attr_32"])).reshape(tiles, P, TE_ROWS)
    time = padded(_np.asarray(inputs["edge_weight"])).reshape(tiles, 1, P)
    x_pad = _np.concatenate([x, _np.zeros((sz.nbp * BN - n, D), x.dtype)])
    arrays = {
        "x": x_pad,
        "xT": x_pad.T,
        "first": dst[::P],
        "last": dst[P - 1::P],
        "type2": type2,
        "edge_ids": _np.stack([padded(src), dst, type2, type8], axis=1),
        "edge_feat": _np.concatenate([attr.transpose(0, 2, 1), type2.view(_np.float32).reshape(tiles, 1, P), time], axis=1),
        "c_mag": _np.asarray(inputs["L0_gnn_c_mag"]).reshape(1),
    }
    for name in _WEIGHTS:
        arrays[name] = _np.asarray(inputs[name])
    nc = _bacc.Bacc("TRN2", target_bir_lowering=False, num_devices=1)
    io, feed = {}, {}
    for name, a in arrays.items():
        a = _np.ascontiguousarray(a)
        feed[f"in_{name}"] = a
        io[name] = nc.dram_tensor(f"in_{name}", a.shape, mybir.dt.from_np(a.dtype), kind="ExternalInput").ap()
    io["out"] = nc.dram_tensor("out_0", (n, D), F32, kind="ExternalOutput").ap()
    program(nc, io, sz)
    r = _run(nc, [feed], core_ids=[0])
    return r.results[0]["out_0"]
```
